# Optimizing a Trainium2 kernel written in Bass

```python
import numpy as np
import jax
import jax.numpy as jnp

def _softmax(x, axis=-1):
    return jax.nn.softmax(x, axis=axis)

def _gelu(x):
    return jax.nn.gelu(x, approximate=True)

def _silu(x):
    return jax.nn.silu(x)

def _sigmoid(x):
    return jax.nn.sigmoid(x)

def _layernorm(x, axis=-1, eps=1e-05):
    m = jnp.mean(x, axis=axis, keepdims=True)
    v = jnp.var(x, axis=axis, keepdims=True)
    return (x - m) / jnp.sqrt(v + eps)

def _scatter_add(tgt, idx, src, axis=0):
    return tgt.at[idx].add(src)

def _segment_sum(src, seg, n):
    return jax.ops.segment_sum(src, seg, n)
kernel_name = 'mk_gnn_resnorm_d4_gnn_r32_ac27fa'

def setup_inputs(seed: int=0):
    np.random.seed(seed)
    _w = jnp.asarray

    def _rec_inputs():
        import jax
        import jax.numpy as jnp
        _gk = jax.random.key(seed)
        x = -0.0003713 + 1 * jax.random.normal(jax.random.fold_in(_gk, 1), (3125, 128), jnp.float32)
        _s = jax.random.randint(jax.random.fold_in(_gk, 2), (25000,), 0, 3125, jnp.int32)
        _d = jax.random.randint(jax.random.fold_in(_gk, 3), (25000,), 0, 3125, jnp.int32)
        _loop = jnp.arange(3125, dtype=jnp.int32)
        src = jnp.concatenate([_s, _d, _loop])
        dst = jnp.concatenate([_d, _s, _loop])
        _o = jnp.argsort(dst, stable=True)
        src = src[_o]
        dst = dst[_o]
        edge_attr_128 = -9.77346e-05 + 0.999888 * jax.random.normal(jax.random.fold_in(_gk, 12), (53125, 128), jnp.float32)
        edge_type_3 = jax.random.randint(jax.random.fold_in(_gk, 14), (53125,), 0, 3, jnp.int32)
        edge_weight = jax.random.uniform(jax.random.fold_in(_gk, 15), (53125,), jnp.float32, 0.0, 1)
        return (x, src, dst, edge_attr_128, edge_type_3, edge_weight)
    x, src, dst, edge_attr_128, edge_type_3, edge_weight = _rec_inputs()

    def _L0_gnn_setup():
        import jax, jax.numpy as jnp
        import numpy as np
        N_NODES = 3125
        N_EDGES = 100000
        INP_DIM = 128
        OUT_DIM = 128

        def _gcn_norm(edge_index, edge_attr, n_nodes):
            loop = jnp.arange(n_nodes, dtype=edge_index.dtype)
            row = jnp.concatenate([edge_index[0], loop])
            col = jnp.concatenate([edge_index[1], loop])
            ew = jnp.concatenate([edge_attr, jnp.ones((n_nodes,), edge_attr.dtype)])
            deg = jax.ops.segment_sum(ew, col, num_segments=n_nodes)
            dinv = jnp.where(deg > 0, jax.lax.rsqrt(jnp.maximum(deg, 1e-30)), 0.0)
            norm = dinv[row] * ew * dinv[col]
            return (row, col, norm)

        def _gcn_conv(x, row, col, norm, W, b, n_nodes):
            h = x @ W
            msg = h[row] * norm[:, None]
            out = jax.ops.segment_sum(msg, col, num_segments=n_nodes)
            return out + b
        key = jax.random.key(seed)
        ks = jax.random.split(key, 10)
        x = jax.random.normal(ks[0], (N_NODES, INP_DIM), dtype=jnp.float32)
        edge_index = jax.random.randint(ks[1], (2, N_EDGES), 0, N_NODES, dtype=jnp.int64)
        edge_attr = jax.random.uniform(ks[2], (N_EDGES,), dtype=jnp.float32)

        def glorot(k, fin, fout):
            s = jnp.sqrt(6.0 / (fin + fout)).astype(jnp.float32)
            return jax.random.uniform(k, (fin, fout), jnp.float32, -s, s)
        W1 = glorot(ks[3], INP_DIM, 32)
        b1 = jnp.zeros((32,), jnp.float32)
        W2 = glorot(ks[4], 32, 64)
        b2 = jnp.zeros((64,), jnp.float32)
        W3 = glorot(ks[5], 64, OUT_DIM)
        b3 = jnp.zeros((OUT_DIM,), jnp.float32)
        return {'x': x, 'edge_index': edge_index, 'edge_attr': edge_attr, 'W1': W1, 'b1': b1, 'W2': W2, 'b2': b2, 'W3': W3, 'b3': b3}
    _L0_gnn_all = _L0_gnn_setup()
    _L0_gnn_in = {k: v for k, v in _L0_gnn_all.items() if k in ('W1', 'b1', 'W2', 'b2', 'W3', 'b3')}
    del _L0_gnn_all

    def _L1_gnn_setup():
        import jax, jax.numpy as jnp
        import numpy as np
        N_NODES, N_EDGES, D, H = (50000, 12500, 128, 4)
        SD = D // H
        EPS = 1e-05

        def _lrelu(x):
            return jax.nn.leaky_relu(x, negative_slope=0.01)

        def _layernorm(x, gamma, beta):
            mu = jnp.mean(x, axis=-1, keepdims=True)
            var = jnp.var(x, axis=-1, keepdims=True)
            return (x - mu) * jax.lax.rsqrt(var + EPS) * gamma + beta

        def _edge_softmax(logits, dst, n_nodes):
            mx = jax.ops.segment_max(logits, dst, num_segments=n_nodes)
            e = jnp.exp(logits - mx[dst])
            s = jax.ops.segment_sum(e, dst, num_segments=n_nodes)
            return e / (s[dst] + 1e-20)
        key = jax.random.key(seed)
        ks = jax.random.split(key, 16)
        s = 1.0 / np.sqrt(D)
        inp = {'h': jax.random.normal(ks[0], (N_NODES, D), jnp.float32), 'e_ij': jax.random.normal(ks[1], (N_EDGES, D), jnp.float32), 'src': jax.random.randint(ks[2], (N_EDGES,), 0, N_NODES, jnp.int32), 'dst': jax.random.randint(ks[3], (N_EDGES,), 0, N_NODES, jnp.int32), 'w1': jax.random.normal(ks[4], (D, D), jnp.float32) * s, 'w2': jax.random.normal(ks[5], (D, D), jnp.float32) * s, 'w3': jax.random.normal(ks[6], (D, D), jnp.float32) * s, 'w4': jax.random.normal(ks[7], (D, D), jnp.float32) * s, 'w5': jax.random.normal(ks[8], (D, D), jnp.float32) * s, 'w6': jax.random.normal(ks[9], (D, D), jnp.float32) * s, 'mlp_w1': jax.random.normal(ks[10], (D, 2 * D), jnp.float32) * s, 'mlp_b1': jnp.zeros((2 * D,), jnp.float32), 'mlp_w2': jax.random.normal(ks[11], (2 * D, D), jnp.float32) * (1.0 / np.sqrt(2 * D)), 'mlp_b2': jnp.zeros((D,), jnp.float32), 'gamma': jnp.ones((D,), jnp.float32), 'beta': jnp.zeros((D,), jnp.float32)}
        return inp
    _L1_gnn_all = _L1_gnn_setup()
    _L1_gnn_in = {k: v for k, v in _L1_gnn_all.items() if k in ('w1', 'w2', 'w3', 'w4', 'w5', 'w6', 'mlp_w1', 'mlp_b1', 'mlp_w2', 'mlp_b2', 'gamma', 'beta')}
    del _L1_gnn_all

    def _L2_gnn_setup():
        import jax, jax.numpy as jnp
        import numpy as np
        BN_EPS = 1e-05

        def _prelu(x, a):
            return jnp.where(x >= 0, x, a * x)
        key = jax.random.key(seed)
        ks = jax.random.split(key, 6)
        N, E, D = (3125, 50000, 128)
        feat = jax.random.normal(ks[0], (N, D), dtype=jnp.float32)
        src = jax.random.randint(ks[1], (E,), 0, N, dtype=jnp.int32)
        dst = jax.random.randint(ks[2], (E,), 0, N, dtype=jnp.int32)
        edge_weight = jax.random.uniform(ks[3], (E,), dtype=jnp.float32)
        W = jax.random.normal(ks[4], (D, D), dtype=jnp.float32) * (1.0 / np.sqrt(D))
        b = jnp.zeros((D,), dtype=jnp.float32)
        a1 = jnp.full((1,), 0.25, dtype=jnp.float32)
        a2 = jnp.full((1,), 0.25, dtype=jnp.float32)
        gamma = jnp.ones((D,), dtype=jnp.float32)
        beta = jnp.zeros((D,), dtype=jnp.float32)
        return {'feat': feat, 'src': src, 'dst': dst, 'edge_weight': edge_weight, 'W': W, 'b': b, 'a1': a1, 'gamma': gamma, 'beta': beta, 'a2': a2}
    _L2_gnn_all = _L2_gnn_setup()
    _L2_gnn_in = {k: v for k, v in _L2_gnn_all.items() if k in ('W', 'b', 'a1', 'gamma', 'beta', 'a2')}
    del _L2_gnn_all

    def _L3_gnn_setup():
        import jax, jax.numpy as jnp
        import numpy as np
        N_NODES = 50000
        N_EDGES = 25000
        IN_FEATS = 128
        OUT_FEATS = 128
        N_REL = 3
        key = jax.random.key(seed)
        k1, k2, k3, k4, k5, k6 = jax.random.split(key, 6)
        feature = jax.random.normal(k1, (N_NODES, IN_FEATS), dtype=jnp.float32)
        bound = float(np.sqrt(6.0 / IN_FEATS))
        weight = jax.random.uniform(k2, (N_REL, IN_FEATS, OUT_FEATS), dtype=jnp.float32, minval=-bound, maxval=bound)
        norm = jax.random.uniform(k3, (N_EDGES,), dtype=jnp.float32)
        src = jax.random.randint(k4, (N_EDGES,), 0, N_NODES)
        dst = jax.random.randint(k5, (N_EDGES,), 0, N_NODES)
        rel_type = jax.random.randint(k6, (N_EDGES,), 0, N_REL)
        return {'feature': feature, 'weight': weight, 'norm': norm, 'src': src, 'dst': dst, 'rel_type': rel_type}
    _L3_gnn_all = _L3_gnn_setup()
    _L3_gnn_in = {k: v for k, v in _L3_gnn_all.items() if k in ('weight',)}
    del _L3_gnn_all
    return {'x': x, 'src': src, 'dst': dst, 'edge_attr_128': edge_attr_128, 'edge_type_3': edge_type_3, 'edge_weight': edge_weight, 'L0_gnn_W1': _L0_gnn_in['W1'], 'L0_gnn_b1': _L0_gnn_in['b1'], 'L0_gnn_W2': _L0_gnn_in['W2'], 'L0_gnn_b2': _L0_gnn_in['b2'], 'L0_gnn_W3': _L0_gnn_in['W3'], 'L0_gnn_b3': _L0_gnn_in['b3'], 'L1_gnn_w1': _L1_gnn_in['w1'], 'L1_gnn_w2': _L1_gnn_in['w2'], 'L1_gnn_w3': _L1_gnn_in['w3'], 'L1_gnn_w4': _L1_gnn_in['w4'], 'L1_gnn_w5': _L1_gnn_in['w5'], 'L1_gnn_w6': _L1_gnn_in['w6'], 'L1_gnn_mlp_w1': _L1_gnn_in['mlp_w1'], 'L1_gnn_mlp_b1': _L1_gnn_in['mlp_b1'], 'L1_gnn_mlp_w2': _L1_gnn_in['mlp_w2'], 'L1_gnn_mlp_b2': _L1_gnn_in['mlp_b2'], 'L1_gnn_gamma': _L1_gnn_in['gamma'], 'L1_gnn_beta': _L1_gnn_in['beta'], 'L2_gnn_W': _L2_gnn_in['W'], 'L2_gnn_b': _L2_gnn_in['b'], 'L2_gnn_a1': _L2_gnn_in['a1'], 'L2_gnn_gamma': _L2_gnn_in['gamma'], 'L2_gnn_beta': _L2_gnn_in['beta'], 'L2_gnn_a2': _L2_gnn_in['a2'], 'L3_gnn_weight': _L3_gnn_in['weight']}

def reference(x, src, dst, edge_attr_128, edge_type_3, edge_weight, L0_gnn_W1, L0_gnn_b1, L0_gnn_W2, L0_gnn_b2, L0_gnn_W3, L0_gnn_b3, L1_gnn_w1, L1_gnn_w2, L1_gnn_w3, L1_gnn_w4, L1_gnn_w5, L1_gnn_w6, L1_gnn_mlp_w1, L1_gnn_mlp_b1, L1_gnn_mlp_w2, L1_gnn_mlp_b2, L1_gnn_gamma, L1_gnn_beta, L2_gnn_W, L2_gnn_b, L2_gnn_a1, L2_gnn_gamma, L2_gnn_beta, L2_gnn_a2, L3_gnn_weight):
    import jax
    import jax.numpy as jnp

    def _L0_gnn_ref(x, edge_index, edge_attr, W1, b1, W2, b2, W3, b3):
        import jax, jax.numpy as jnp
        import numpy as np
        N_NODES = 3125
        N_EDGES = 100000
        INP_DIM = 128
        OUT_DIM = 128

        def _gcn_norm(edge_index, edge_attr, n_nodes):
            loop = jnp.arange(n_nodes, dtype=edge_index.dtype)
            row = jnp.concatenate([edge_index[0], loop])
            col = jnp.concatenate([edge_index[1], loop])
            ew = jnp.concatenate([edge_attr, jnp.ones((n_nodes,), edge_attr.dtype)])
            deg = jax.ops.segment_sum(ew, col, num_segments=n_nodes)
            dinv = jnp.where(deg > 0, jax.lax.rsqrt(jnp.maximum(deg, 1e-30)), 0.0)
            norm = dinv[row] * ew * dinv[col]
            return (row, col, norm)

        def _gcn_conv(x, row, col, norm, W, b, n_nodes):
            h = x @ W
            msg = h[row] * norm[:, None]
            out = jax.ops.segment_sum(msg, col, num_segments=n_nodes)
            return out + b
        n = x.shape[0]
        row, col, norm = _gcn_norm(edge_index, edge_attr, n)
        h = jax.nn.elu(_gcn_conv(x, row, col, norm, W1, b1, n))
        h = jax.nn.elu(_gcn_conv(h, row, col, norm, W2, b2, n))
        return _gcn_conv(h, row, col, norm, W3, b3, n)

    def _L1_gnn_ref(h, e_ij, src, dst, w1, w2, w3, w4, w5, w6, mlp_w1, mlp_b1, mlp_w2, mlp_b2, gamma, beta):
        import jax, jax.numpy as jnp
        import numpy as np
        N_NODES, N_EDGES, D, H = (50000, 12500, 128, 4)
        SD = D // H
        EPS = 1e-05

        def _lrelu(x):
            return jax.nn.leaky_relu(x, negative_slope=0.01)

        def _layernorm(x, gamma, beta):
            mu = jnp.mean(x, axis=-1, keepdims=True)
            var = jnp.var(x, axis=-1, keepdims=True)
            return (x - mu) * jax.lax.rsqrt(var + EPS) * gamma + beta

        def _edge_softmax(logits, dst, n_nodes):
            mx = jax.ops.segment_max(logits, dst, num_segments=n_nodes)
            e = jnp.exp(logits - mx[dst])
            s = jax.ops.segment_sum(e, dst, num_segments=n_nodes)
            return e / (s[dst] + 1e-20)
        n = h.shape[0]
        u = _lrelu(h @ w1).reshape(n, H, SD)
        v = _lrelu(h @ w2).reshape(n, H, SD)
        x_ij = (e_ij @ w3).reshape(-1, H, SD)
        m = v[dst] + x_ij
        attn = u[src] * m
        attn = _edge_softmax(attn / np.sqrt(SD).astype(np.float32), dst, n)
        k = _lrelu(h @ w4).reshape(n, H, SD)
        x2 = _lrelu((e_ij @ w5).reshape(-1, H, SD))
        msg = attn * (k[dst] + x2)
        agg = jax.ops.segment_sum(msg, dst, num_segments=n).reshape(n, D)
        out = h @ w6 + agg
        out = _layernorm(out, gamma, beta)
        out = out + (jax.nn.relu(out @ mlp_w1 + mlp_b1) @ mlp_w2 + mlp_b2)
        out = _layernorm(out, gamma, beta)
        return out

    def _L2_gnn_ref(feat, src, dst, edge_weight, W, b, a1, gamma, beta, a2):
        import jax, jax.numpy as jnp
        import numpy as np
        BN_EPS = 1e-05

        def _prelu(x, a):
            return jnp.where(x >= 0, x, a * x)
        N = feat.shape[0]
        msg = feat[src] * edge_weight[:, None]
        agg = jax.ops.segment_sum(msg, dst, num_segments=N)
        h = agg @ W + b
        h = _prelu(h, a1)
        mean = h.mean(axis=0)
        var = h.var(axis=0)
        h = (h - mean) / jnp.sqrt(var + BN_EPS) * gamma + beta
        h = _prelu(h, a2)
        return h

    def _L3_gnn_ref(feature, weight, norm, src, dst, rel_type):
        import jax, jax.numpy as jnp
        import numpy as np
        N_NODES = 50000
        N_EDGES = 25000
        IN_FEATS = 128
        OUT_FEATS = 128
        N_REL = 3
        hr = jnp.einsum('ni,rio->rno', feature, weight)
        msg = hr[rel_type, src] * norm[:, None]
        h = jax.ops.segment_sum(msg, dst, num_segments=feature.shape[0])
        return jax.nn.relu(h)
    edge_index = jnp.stack([src, dst])
    x = _layernorm(x + _L0_gnn_ref(x, edge_index, edge_weight, L0_gnn_W1, L0_gnn_b1, L0_gnn_W2, L0_gnn_b2, L0_gnn_W3, L0_gnn_b3), axis=-1)
    x = _layernorm(x + _L1_gnn_ref(x, edge_attr_128, src, dst, L1_gnn_w1, L1_gnn_w2, L1_gnn_w3, L1_gnn_w4, L1_gnn_w5, L1_gnn_w6, L1_gnn_mlp_w1, L1_gnn_mlp_b1, L1_gnn_mlp_w2, L1_gnn_mlp_b2, L1_gnn_gamma, L1_gnn_beta), axis=-1)
    x = _layernorm(x + _L2_gnn_ref(x, src, dst, edge_weight, L2_gnn_W, L2_gnn_b, L2_gnn_a1, L2_gnn_gamma, L2_gnn_beta, L2_gnn_a2), axis=-1)
    x = _layernorm(x + _L3_gnn_ref(x, L3_gnn_weight, edge_weight, src, dst, edge_type_3), axis=-1)
    return x

_drawn_inputs = setup_inputs


def setup_inputs(seed=0):
    import zlib

    import numpy as np

    out = dict(_drawn_inputs(seed))
    spreads = {'L0_gnn_b1': (0.0, 0.1),
     'L0_gnn_b2': (0.0, 0.1),
     'L0_gnn_b3': (0.0, 0.1),
     'L1_gnn_mlp_b1': (0.0, 0.1),
     'L1_gnn_mlp_b2': (0.0, 0.1),
     'L1_gnn_gamma': (1.0, 0.2),
     'L1_gnn_beta': (0.0, 0.1),
     'L2_gnn_b': (0.0, 0.733),
     'L2_gnn_gamma': (1.0, 0.2),
     'L2_gnn_beta': (0.0, 0.1)}
    factors = {'L1_gnn_w1': 3.493, 'L1_gnn_w2': 7.465, 'L1_gnn_w3': 3.587}
    for name, (base, spread) in spreads.items():
        noise = np.random.default_rng([zlib.crc32(name.encode()), seed]).standard_normal(out[name].shape)
        drawn = base * np.exp(spread * noise) if base else spread * noise
        out[name] = jnp.asarray(drawn.astype(out[name].dtype))
    for name, factor in factors.items():
        out[name] = (out[name] * factor).astype(out[name].dtype)
    return out
```

```python
import concourse.bass as bass
from concourse import mybir
from contextlib import ExitStack

FP32 = mybir.dt.float32
BF16 = mybir.dt.bfloat16
I32 = mybir.dt.int32
ALU = mybir.AluOpType
ACT = mybir.ActivationFunctionType
AX = mybir.AxisListType

P = 125
GRP = 5
CUT = 3
PARTS = ((0, CUT), (CUT, GRP))
BANK = 512
NEG = -1.0e38
EPS = 1e-5
SLOPE = 0.01


def build(nc, t, out, last_layer=4):
    N, D = t["x"].shape
    E = t["src"].shape[0]
    NT = N // P
    ET = E // P
    GR = ET // GRP
    GE = GRP * P
    BL = E // P
    LB = ET // GRP
    assert N == NT * P and E == ET * P and ET == GR * GRP and D == 128
    D1 = t["L0_gnn_W1"].shape[1]
    D2 = t["L0_gnn_W2"].shape[1]
    HD = t["L1_gnn_mlp_w1"].shape[1]
    NREL = t["L3_gnn_weight"].shape[0]
    HEAD = 32
    ctx = ExitStack()
    with ctx:
        def sb(name, shape, dt=FP32):
            return ctx.enter_context(nc.sbuf_tensor(name, shape, dt))

        def dram(name, shape, dt=FP32):
            return nc.dram_tensor(name, shape, dt, kind="Internal").ap()

        sems = {}

        def sem(name):
            if name not in sems:
                sems[name] = ctx.enter_context(nc.semaphore(name))
            return sems[name]

        keep_d = dram("keep_d", (E,), BF16)
        deg_d = dram("deg_d", (E, 1))
        table = [dram("table1", (N, D1)), dram("table2", (N, D1)), dram("table3", (N, D2)), None,
                 dram("table5", (N, D)), dram("table6", (NREL * N, D))]
        u_table = dram("u_table", (N, D))
        v_table = dram("v_table", (N, D))
        WIDTH = [D1, D1, D2, 2 * D, D, D]
        sums_d = [dram(f"sums{k}", (E, w)) for k, w in enumerate(WIDTH)]

        ident = sb("ident", [128, 128])
        ones = sb("ones", [1, 128])
        srcT = sb("srcT", [P, ET + GRP], I32)
        dstT = sb("dstT", [P, ET + GRP], I32)
        relT = sb("relT", [P, ET + GRP], I32)
        weightT = sb("weightT", [P, ET])
        node_id = sb("node_id", [P, NT])
        last_edge = sb("last_edge", [P, NT], I32)
        block_row = sb("block_row", [P, NT], I32)
        occupied = sb("occupied", [P, NT])
        dinv = sb("dinv", [P, NT])
        row_of = {n: sb(n + "_row", [P, t[n].shape[0]]) for n in
                  ("L0_gnn_b1", "L0_gnn_b2", "L0_gnn_b3", "L1_gnn_mlp_b2", "L1_gnn_gamma", "L1_gnn_beta")}
        w1 = sb("w1", [D, D1])
        w2 = sb("w2", [D1, D2])
        w3 = sb("w3", [D2, D])
        att_w = sb("att_w", [D, 4, D])
        w_e3 = sb("w_e3", [D, D])
        w_e5 = sb("w_e5", [D, D])
        mlp1 = sb("mlp1", [D, HD])
        mlp2 = sb("mlp2", [128, HD // 128, D])
        mlp_b1 = sb("mlp_b1", [128, HD // 128])
        w_l2 = sb("w_l2", [D, D])
        l2_cols = sb("l2_cols", [D, 5])
        rel_w = sb("rel_w", [D, NREL, D])

        x = sb("x", [P, NT, D])
        xT = sb("xT", [D, N])
        tmp = sb("tmp", [P, NT, D])
        tmp2 = sb("tmp2", [128, NT * D])
        own = sb("own", [P, NT, D])
        x6 = sb("x6", [P, NT, D])
        arena = sb("arena", [P, max(NT * BL, NT * 3 * D)])
        k_node = arena[:, 2 * NT * D:3 * NT * D].rearrange("p (i d) -> p i d", d=D)
        small = sb("small", [128, 8, NT])
        tmp2n = tmp2[0:P, :].rearrange("p (i d) -> p i d", d=D)

        def ends(d):
            return arena[:, 0:NT * d].rearrange("p (i d) -> p i d", d=d)

        rows = sb("rows", [P, GRP, D])
        v_rows = sb("v_rows", [P, GRP, D])
        e_rows = sb("e_rows", [P, GRP, D])
        idx = sb("idx", [P, GRP], I32)
        v_idx = sb("v_idx", [P, GRP], I32)
        keep = sb("keep", [128, GE], BF16)
        run_s = sb("run_s", [D, GE])
        run_n = sb("run_n", [D, GE])
        run_m = sb("run_m", [D, 1 + GE])
        logit = sb("logit", [D, GE])
        reset = sb("reset", [D, GE])
        fall = sb("fall", [D, GE])
        alpha = sb("alpha", [D, GE])
        beta = sb("beta", [D, GE])
        betax = sb("betax", [D, GE])
        eT = sb("eT", [D, GE])
        uT = sb("uT", [D, GE])
        x2 = sb("x2", [D, GE])
        rows_out = sb("rows_out", [P, GRP * 2 * D])
        PS = ctx.enter_context(nc.psum_tensor("PS", [128, 8 * BANK], FP32))

        def bank(b, p, n, at=0):
            return PS[0:p, b * BANK + at:b * BANK + at + n]

        def tiles(dr, p=P):
            return dr.rearrange("(i p) d -> p i d", p=p)

        ctx.enter_context(nc.allow_non_contiguous_dma(reason="index lists and columns of weights, once"))
        block = ctx.enter_context(nc.Block())

        GCN = {0: (D1, table[0], srcT), 1: (D1, table[1], srcT), 2: (D2, table[2], srcT),
               4: (D, table[4], srcT), 5: (D, table[5], relT)}
        ORDER = {0: 0, 1: 1, 2: 2, 4: 3, 5: 4}

        @block.gpsimd
        def _(eng):
            nc.gpsimd.memset(ident[:, :], 0.0).then_inc(sem("ident_cleared"), 1)
            nc.gpsimd.memset(ones[:, :], 1.0)
            nc.gpsimd.memset(run_s[:, :], 0.0)
            nc.gpsimd.memset(run_n[:, :], 0.0)
            nc.gpsimd.memset(run_m[:, :], NEG)
            nc.gpsimd.iota(block_row[:, :], [[P, NT]], base=0, channel_multiplier=1).then_inc(sem("node_numbers"), 1)
            eng.wait_ge(sem("ident_cleared"), 1)
            nc.gpsimd.affine_select(out=ident[:, :], in_=ident[:, :], compare_op=ALU.not_equal, fill=1.0,
                                    base=0, pattern=[[-1, 128]], channel_multiplier=1).then_inc(sem("const_ready"), 1)

            eng.wait_ge(sem("block_row_ready"), 1)
            dst_blocks = t["dst"].rearrange("(b l) -> b l", l=BL)
            arena_i = arena[:, :].bitcast(I32)
            for i in range(NT):
                eng.indirect_dma_start(out=arena_i[:, i * BL:(i + 1) * BL], out_offset=None, in_=dst_blocks,
                                       in_offset=bass.IndirectOffsetOnAxis(ap=block_row[:, i:i + 1], axis=0)
                                       ).then_inc(sem("block_landed"), 16)
            eng.wait_ge(sem("last_edge_ready"), 1)
            eng.wait_ge(sem("deg_stored"), 16)
            for i in range(NT):
                eng.indirect_dma_start(out=small[0:P, 0, i:i + 1], out_offset=None, in_=deg_d,
                                       in_offset=bass.IndirectOffsetOnAxis(ap=last_edge[:, i:i + 1], axis=0)
                                       ).then_inc(sem("deg_landed"), 16)

            def gather(dst_ap, tab, index):
                return eng.indirect_dma_start(out=dst_ap, out_offset=None, in_=tab,
                                              in_offset=bass.IndirectOffsetOnAxis(ap=index, axis=0))

            def gather_pass(k):
                d, tab, index = GCN[k]
                base = ORDER[k] * GR
                staged = ORDER[k] * (GR + 1) * GRP
                eng.wait_ge(sem(f"table_stored{k}"), 16)

                for b in range(GRP):
                    eng.wait_ge(sem("idx_staged"), staged + b + 1)
                    if base:
                        eng.wait_ge(sem("rows_turned"), (base - 1) * GRP + (b + 1))
                    gather(rows[:, b, 0:d], tab, idx[:, b:b + 1]).then_inc(sem(f"rows_landed{b}"), 16)
                with nc.gpsimd.Fori(1, GR, 1) as g:
                    for b in range(GRP):
                        eng.wait_ge(sem("idx_staged"), g * GRP + (staged + b + 1))
                        nc.gpsimd.nop(nofuse=True)
                        eng.wait_ge(sem("rows_turned"), (g + (base - 1)) * GRP + (b + 1))
                        nc.gpsimd.nop(nofuse=True)
                        gather(rows[:, b, 0:d], tab, idx[:, b:b + 1]).then_inc(sem(f"rows_landed{b}"), 16)

            def fetch_ends(k):
                w = WIDTH[k]
                eng.wait_ge(sem(f"sums_stored{k}"), 1)
                for i in range(NT):
                    gather(arena[:, i * w:(i + 1) * w], sums_d[k], last_edge[:, i:i + 1]).then_inc(sem(f"ends_landed{k}"), 16)

            def attention_pass():
                eng.wait_ge(sem("uv_stored"), 32)

                def part_gathers(g, part):
                    for b in range(*PARTS[part]):
                        gather(rows[:, b, :], u_table, idx[:, b:b + 1]).then_inc(sem(f"att_rows_landed{b}"), 16)
                        gather(v_rows[:, b, :], v_table, v_idx[:, b:b + 1]).then_inc(sem(f"att_rows_landed{b}"), 16)
                for part in range(2):
                    eng.wait_ge(sem("att_idx_staged"), part + 1)
                    part_gathers(0, part)
                with nc.gpsimd.Fori(1, GR, 1) as g:
                    for part in range(2):
                        eng.wait_ge(sem("att_idx_staged"), g * 2 + (part + 1))
                        nc.gpsimd.nop(nofuse=True)
                        part_gathers(g, part)

            for k in range(3):
                gather_pass(k)
                fetch_ends(k)
            if last_layer >= 2:
                attention_pass()
                fetch_ends(3)
            for k in (4, 5)[:max(0, last_layer - 2)]:
                gather_pass(k)
                fetch_ends(k)

        @block.sync
        def _(eng):
            arrive = sem("edge_lists_landed")
            for n, name in enumerate(("src", "dst", "edge_type_3", "edge_weight")):
                view = (tmp2[0:LB, n * GE:(n + 1) * GE])
                if name != "edge_weight":
                    view = view.bitcast(I32)
                eng.dma_start(view.rearrange("r (j p) -> r j p", j=GRP),
                              t[name].rearrange("(j r p) -> r j p", j=GRP, p=P)).then_inc(arrive, 16)
            blk = sem("blocks_landed")
            own_i = own[:, :, :].rearrange("p i d -> p (i d)").bitcast(I32)
            eng.dma_start(own_i[:, 0:BL], t["dst"].rearrange("(p l) -> p l", l=BL)).then_inc(blk, 16)
            eng.dma_start(own_i[1:P, BL:BL + 1], t["dst"].rearrange("(p l) -> p l", l=BL)[0:P - 1, BL - 1:BL]).then_inc(blk, 16)
            eng.dma_start(own_i[0:1, BL:BL + 1], t["dst"].rearrange("(a n) -> a n", a=1)[:, 0:1]).then_inc(blk, 16)
            eng.dma_start(own[:, :, :].rearrange("p i d -> p (i d)")[:, 2 * BL:3 * BL],
                          t["edge_weight"].rearrange("(p l) -> p l", l=BL)).then_inc(blk, 16)
            own_r = own_i[0:1, 3 * BL:3 * BL + 3 * P].rearrange("a (c p) -> a c p", c=3)
            for c, at in ((0, 0), (1, BL - 1)):
                eng.dma_start(own_r[:, c, :], t["dst"].rearrange("(a p l) -> a p l", a=1, l=BL)[:, :, at]).then_inc(blk, 16)
            eng.dma_start(x[:, :, :], tiles(t["x"])).then_inc(sem("x_landed"), 16)
            wl = sem("weights_landed")
            loads = [(w1[:, :], t["L0_gnn_W1"]), (w2[:, :], t["L0_gnn_W2"]), (w3[:, :], t["L0_gnn_W3"])]
            for c, n in enumerate(("w1", "w2", "w4", "w6")):
                loads.append((att_w[:, c, :], t["L1_gnn_" + n]))
            loads += [(w_e3[:, :], t["L1_gnn_w3"]), (w_e5[:, :], t["L1_gnn_w5"]), (mlp1[:, :], t["L1_gnn_mlp_w1"]),
                      (mlp2[:, :, :], t["L1_gnn_mlp_w2"].rearrange("(c p) d -> p c d", p=128)),
                      (mlp_b1[:, :], t["L1_gnn_mlp_b1"].rearrange("(c p) -> p c", p=128)),
                      (w_l2[:, :], t["L2_gnn_W"]),
                      (rel_w[:, :, :], t["L3_gnn_weight"].rearrange("r i o -> i r o"))]
            for c, n in enumerate(("b", "gamma", "beta")):
                loads.append((l2_cols[:, c:c + 1], t["L2_gnn_" + n].rearrange("(p a) -> p a", a=1)))
            for c, n in enumerate(("a1", "a2")):
                loads.append((l2_cols[:, 3 + c:4 + c], t["L2_gnn_" + n].rearrange("(a n) -> a n", a=1).to_broadcast([D, 1])))
            for n, r in row_of.items():
                loads.append((r[:, :], t[n].rearrange("(a n) -> a n", a=1).to_broadcast([P, t[n].shape[0]])))
            assert len(loads) == WEIGHT_LOADS
            for dst_ap, src_ap in loads:
                eng.dma_start(dst_ap, src_ap).then_inc(wl, 16)

            eng.wait_ge(sem("keep_ready"), 1)
            eng.dma_start(keep_d.rearrange("(p l) -> p l", l=BL), keep_blocks(own)).then_inc(sem("keep_stored"), 16)
            eng.wait_ge(sem("block_sums_ready"), 1)
            own_rf = own[0:1, :, :].rearrange("a i d -> a (i d)")
            eng.dma_start(own_rf[:, 3 * BL + 2 * P:3 * BL + 3 * P], run_w(own)[:, BL - 1:BL]).then_inc(sem("block_ends_landed"), 16)
            eng.wait_ge(sem("carry_row_ready"), 1)
            eng.dma_start(small[0:P, 1, 0:1], carry_row(own)).then_inc(sem("carry_landed"), 16)
            eng.wait_ge(sem("degree_ready"), 1)
            eng.dma_start(deg_d.rearrange("(p l) a -> p (l a)", l=BL), run_w(own)).then_inc(sem("deg_stored"), 16)
            eng.wait_ge(sem("keep_stored"), 16)

            def load_keep(k, g, part):
                a, b = PARTS[part]
                src_ap = keep_d.rearrange("(a n) -> a n", a=1)[:, bass.ds(g * GE + a * P, (b - a) * P)]
                eng.dma_start(keep[:, a * P:b * P], src_ap.to_broadcast([128, (b - a) * P])).then_inc(sem(f"keep_landed{part}"), 16)

            def stream(k, extra=None):
                d = WIDTH[k]
                out_v = sums_d[k].rearrange("(i p) d -> p i d", p=P)
                pre = "att_" if k == 3 else ""
                base = 0 if k == 3 else ORDER[k] * GR

                def store(g):
                    eng.wait_ge(sem(pre + "rows_out_filled"), (g + base) * 2 + (2 + FREE[pre]))
                    eng.dma_start(out_v[:, bass.ds(g * GRP, GRP), :],
                                  rows_out[:, 0:GRP * d].rearrange("p (b d) -> p b d", d=d)).then_inc(sem(pre + "sums_written"), 16)
                    eng.wait_ge(sem(pre + "sums_written"), (g + (base + 1)) * 16)
                    eng.sem_inc(sem(pre + "rows_out_free"), 1)

                def edge_rows(g, part):
                    a, b = PARTS[part]
                    eng.dma_start(e_rows[:, a:b, :], tiles(t["edge_attr_128"])[:, bass.ds(g * GRP + a, b - a), :]
                                  ).then_inc(sem(f"e_rows_landed{part}"), 16)

                for part in range(2):
                    load_keep(k, 0, part)
                    if k == 3:
                        edge_rows(0, part)
                with nc.sync.Fori(0, GR - 1, 1) as g:
                    if k == 3:
                        for part in range(2):
                            eng.wait_ge(sem("e_turned"), g * 2 + (part + 1))
                            edge_rows(g + 1, part)
                    for part in range(2):
                        eng.wait_ge(sem("att_reset_made" if k == 3 else "scanned"), (g + base) * 2 + (part + 1))
                        load_keep(k, g + 1, part)
                    store(g)
                store(GR - 1)
                eng.sem_inc(sem(f"sums_stored{k}"), 1)

            def store_table(k, ap_src):
                eng.wait_ge(sem(f"table_ready{k}"), 1)
                eng.dma_start(tiles(table[k]), ap_src).then_inc(sem(f"table_stored{k}"), 16)

            for k, w in ((0, D1), (1, D1), (2, D2)):
                store_table(k, own[:, :, 0:w])
                stream(k)
            if last_layer >= 2:
                eng.wait_ge(sem("u_ready"), 1)
                eng.dma_start(tiles(u_table), tmp[:, :, :]).then_inc(sem("uv_stored"), 16)
                eng.dma_start(tiles(v_table), tmp2n).then_inc(sem("uv_stored"), 16)
                stream(3)
            if last_layer >= 3:
                store_table(4, x[:, :, :])
                stream(4)
            if last_layer >= 4:
                tab = table[5].rearrange("(r i p) d -> p i r d", p=P, r=NREL)
                for i in range(NT):
                    eng.wait_ge(sem("rel_rows_ready"), i + 1)
                    eng.dma_start(tab[:, i, :, :], rel_buf(arena)[:, i % SLOTS, :].rearrange("p (r d) -> p r d", r=NREL)
                                  ).then_inc(sem(f"rel_written{i % SLOTS}"), 16)
                for h in range(SLOTS):
                    eng.wait_ge(sem(f"rel_written{h}"), 16 * len(range(h, NT, SLOTS)))
                eng.sem_inc(sem("table_stored5"), 16)
                stream(5)
            eng.wait_ge(sem("out_ready"), 1)
            eng.dma_start(tiles(out), x[:, :, :]).then_inc(sem("out_stored"), 16)
            eng.wait_ge(sem("out_stored"), 16)

        @block.tensor
        def _(pe):
            count = {"groups": 0, "turned": 0}

            pe.wait_ge(sem("const_ready"), 1)
            for n in range(4):
                pe.wait_ge(sem("lists_float"), n + 1)
                for j in range(GRP):
                    ins = nc.tensor.transpose(bank(n, P, LB, j * LB), list_f(tmp, tmp2, n)[0:LB, j * P:(j + 1) * P], ident[0:LB, 0:LB])
                ins.then_inc(sem("lists_turned"), 1)
            pe.wait_ge(sem("block_rows_float"), 1)
            nc.tensor.matmul(bank(4, P, P), ones[0:1, 0:P], small_row(x6), start=True, stop=True).then_inc(sem("block_first_spread"), 1)

            def to_channels(src, d, ready, value=1):
                pe.wait_ge(sem(ready), value)
                for a in range(0, NT, 4):
                    n = count["turned"]
                    if n >= 2:
                        pe.wait_ge(sem("channels_copied"), n - 1)
                    for i in range(a, min(a + 4, NT)):
                        ins = nc.tensor.transpose(bank(n % 2, d, P, (i - a) * P), src[:, i, 0:d], ident[0:P, 0:P])
                    ins.then_inc(sem("channels_turned"), 1)
                    count["turned"] += 1
                return count["turned"]

            def node_product(w, width, k, per_bank):
                for j, a in enumerate(range(0, NT, per_bank)):
                    n = count["groups"]
                    if n >= 6:
                        pe.wait_ge(sem("products_taken"), n - 5)
                    pe.wait_ge(sem("channels_copied"), channels_needed(count["turned"], min(a + per_bank, NT) - 1))
                    for i in range(a, min(a + per_bank, NT)):
                        ins = nc.tensor.matmul(bank(2 + n % 6, P, width, (i - a) * width), xT[0:k, i * P:(i + 1) * P],
                                               w, start=True, stop=True)
                    ins.then_inc(sem("products_ready"), 1)
                    count["groups"] += 1

            def gcn_pass(k):
                d = WIDTH[k]
                base = ORDER[k] * GR

                def forward(g, part, first):
                    a, b = PARTS[part]
                    if not first:
                        pe.wait_ge(sem("scanned"), (g + (base - 1)) * 2 + (part + 1))
                    for i in range(a, b):
                        pe.wait_ge(sem("rows_weighted"), (g + base) * GRP + (i + 1))
                        if d < 128:
                            nc.tensor.nop(nofuse=True)
                        nc.tensor.transpose(bank(part, d, P, (i - a) * P), rows[:, i, 0:d], ident[0:P, 0:P]
                                            ).then_inc(sem("rows_turned"), 1)

                def back(g, part):
                    a, b = PARTS[part]
                    pe.wait_ge(sem("scanned"), (g + base) * 2 + (part + 1))
                    if d < 128:
                        nc.tensor.nop(nofuse=True)
                    for i in range(a, b):
                        ins = nc.tensor.transpose(bank(2 + part, P, d, (i - a) * d), run_s[0:d, i * P:(i + 1) * P], ident[0:d, 0:d])
                    ins.then_inc(sem("sums_turned"), 1)

                forward(0, 0, base == 0)
                forward(0, 1, base == 0)
                with nc.tensor.Fori(0, GR - 1, 1) as g:
                    for part in range(2):
                        pe.wait_ge(sem("rows_out_filled"), (g + base) * 2 + (part + 1))
                        back(g, part)
                        forward(g + 1, part, False)
                for part in range(2):
                    pe.wait_ge(sem("rows_out_filled"), (GR - 1 + base) * 2 + (part + 1))
                    back(GR - 1, part)

            def attention_pass():
                def forward(g, part, c, first):
                    a, b = PARTS[part]
                    n = (b - a) * P
                    pe.wait_ge(sem(f"e_rows_landed{part}"), (g + 1) * 16)
                    if c is not None:
                        pe.wait_ge(sem("att_e_copied"), c)
                    for i in range(a, b):
                        ins = nc.tensor.transpose(bank(0, D, P, (i - a) * P), e_rows[:, i, :], ident[0:P, 0:P])
                    ins.then_inc(sem("e_turned"), 1)
                    if c is not None:
                        pe.wait_ge(sem("att_u_copied"), c)
                    for i in range(a, b):
                        pe.wait_ge(sem(f"att_rows_landed{i}"), (g + 1) * 32)
                        ins = nc.tensor.transpose(bank(1, D, P, (i - a) * P), rows[:, i, :], ident[0:P, 0:P])
                    ins.then_inc(sem("att_u_turned"), 1)
                    pe.wait_ge(sem("att_e_copied"), g * 2 + (part + 1))
                    if not first:
                        pe.wait_ge(sem("att_logits_made"), (g - 1) * 2 + (part + 1))
                    nc.tensor.matmul(bank(2 + part, D, n), w_e3[:, :], eT[:, a * P:b * P], start=True, stop=False)
                    for i in range(a, b):
                        ins = nc.tensor.matmul(bank(2 + part, D, P, (i - a) * P), v_rows[:, i, :], ident[0:P, 0:P],
                                               start=False, stop=(i == b - 1))
                    ins.then_inc(sem("att_edges_mixed"), 1)
                    if c is not None:
                        pe.wait_ge(sem("att_x2_made"), c)
                    nc.tensor.matmul(bank(4, D, n), w_e5[:, :], eT[:, a * P:b * P], start=True, stop=True
                                     ).then_inc(sem("att_x5_ready"), 1)

                def back(g, part):
                    a, b = PARTS[part]
                    pe.wait_ge(sem("att_scanned"), g * 2 + (part + 1))
                    pe.wait_ge(sem("att_rows_out_filled"), g * 2 + (part + 1))
                    for i in range(a, b):
                        nc.tensor.transpose(bank(5, P, D, (i - a) * 2 * D), run_n[:, i * P:(i + 1) * P], ident[:, :])
                        ins = nc.tensor.transpose(bank(5, P, D, (i - a) * 2 * D + D), run_s[:, i * P:(i + 1) * P], ident[:, :])
                    ins.then_inc(sem("att_sums_turned"), 1)

                forward(0, 0, None, True)
                forward(0, 1, 1, True)
                with nc.tensor.Fori(0, GR - 1, 1) as g:
                    for part in range(2):
                        forward(g + 1, part, g * 2 + (2 + part), False)
                        back(g, part)
                for part in range(2):
                    back(GR - 1, part)

            pe.wait_ge(sem("x_landed"), 16)
            pe.wait_ge(sem("lists_copied"), 4)
            pe.wait_ge(sem("weights_landed"), 16 * WEIGHT_LOADS)
            to_channels(x, D, "x_landed", 16)
            node_product(w1[:, :], D1, D, BANK // D1)
            gcn_pass(0)
            gcn_pass(1)
            pe.wait_ge(sem("conv2_input"), 1)
            to_channels(tmp, D1, "conv2_input")
            node_product(w2[:, :], D2, D1, BANK // D2)
            pe.wait_ge(sem("table_ready2"), 1)
            gcn_pass(2)
            to_channels(tmp, D2, "conv3_input")
            node_product(w3[:, :], D, D2, BANK // D)
            if last_layer >= 2:
                to_channels(x, D, "x_new", 1)
                node_product(att_w[:, :, :].rearrange("p c d -> p (c d)"), 4 * D, D, 1)
                pe.wait_ge(sem("u_ready"), 1)
                attention_pass()
                to_channels(tmp, D, "mlp_input")
                pe.wait_ge(sem("channels_copied"), count["turned"])
                hid = 0
                for a in range(0, NT, 4):
                    m = min(4, NT - a) * P
                    if a > 0:
                        pe.wait_ge(sem("hidden_made"), hid)
                    for h in range(HD // 128):
                        ins = nc.tensor.matmul(bank(h, 128, m), mlp1[:, h * 128:(h + 1) * 128], xT[:, a * P:a * P + m],
                                               start=True, stop=True)
                        ins.then_inc(sem("hidden_ready"), 1)
                        hid += 1
                    pe.wait_ge(sem("hidden_made"), hid)
                    n = count["groups"]
                    pe.wait_ge(sem("products_taken"), n - 5)
                    for i in range(a, min(a + 4, NT)):
                        for h in range(HD // 128):
                            ins = nc.tensor.matmul(bank(2 + n % 6, P, D, (i - a) * D), hidden(eT, uT, h)[:, (i - a) * P:(i - a + 1) * P],
                                                   mlp2[:, h, :], start=(h == 0), stop=(h == HD // 128 - 1))
                    ins.then_inc(sem("products_ready"), 1)
                    count["groups"] += 1
            if last_layer >= 3:
                pe.wait_ge(sem("table_ready4"), 1)
                gcn_pass(4)
                to_channels(tmp, D, "l2_input")
                for a in range(0, NT, 4):
                    m = min(4, NT - a) * P
                    pe.wait_ge(sem("channels_copied"), channels_needed(count["turned"], min(a + 4, NT) - 1))
                    n = count["groups"]
                    pe.wait_ge(sem("products_taken"), n - 5)
                    nc.tensor.matmul(bank(2 + n % 6, D, m), w_l2[:, :], xT[:, a * P:a * P + m],
                                     start=True, stop=True).then_inc(sem("products_ready"), 1)
                    count["groups"] += 1
                pe.wait_ge(sem("l2_normed"), 1)
                for a in range(0, NT, 4):
                    n = count["groups"]
                    pe.wait_ge(sem("products_taken"), n - 5)
                    for i in range(a, min(a + 4, NT)):
                        ins = nc.tensor.transpose(bank(2 + n % 6, P, D, (i - a) * D), tmp2[:, i * P:(i + 1) * P], ident[:, :])
                    ins.then_inc(sem("products_ready"), 1)
                    count["groups"] += 1
            if last_layer >= 4:
                to_channels(x, D, "x_new", 3)
                node_product(rel_w[:, :, :].rearrange("p r d -> p (r d)"), NREL * D, D, 1)
                pe.wait_ge(sem("rel_rows_ready"), NT)
                gcn_pass(5)

        @block.scalar
        def _(act):
            count = {"turned": 0, "groups": 0, "steps": 0}

            def done(ins):
                count["steps"] += 1
                ins.then_inc(sem("scalar_steps"), 1)
                act.wait_ge(sem("scalar_steps"), count["steps"])

            def copy_channels(d):
                for a in range(0, NT, 4):
                    n = count["turned"]
                    m = min(4, NT - a) * P
                    act.wait_ge(sem("channels_turned"), n + 1)
                    nc.scalar.activation(xT[0:d, a * P:a * P + m], bank(n % 2, d, m), ACT.Copy).then_inc(sem("channels_copied"), 1)
                    count["turned"] += 1

            def gcn_pass(k):
                d = WIDTH[k]
                base = ORDER[k] * GR

                def weigh(g, part):
                    a, b = PARTS[part]
                    for i in range(a, b):
                        act.wait_ge(sem(f"rows_landed{i}"), (g + (base + 1)) * 16)
                        nc.scalar.activation(rows[:, i, 0:d], rows[:, i, 0:d], ACT.Copy,
                                             scale=weightT[:, bass.ds(g * GRP + i, 1)]).then_inc(sem("rows_weighted"), 1)

                def empty(g, part):
                    a, b = PARTS[part]
                    act.wait_ge(sem("sums_turned"), (g + base) * 2 + (part + 1))
                    nc.scalar.activation(rows_out[:, a * d:b * d], bank(2 + part, P, (b - a) * d), ACT.Copy
                                         ).then_inc(sem("rows_out_filled"), 1)

                if base == 0:
                    act.sem_inc(sem("rows_out_free"), 1)
                    act.sem_inc(sem("rows_out_filled"), FREE[""])
                weigh(0, 0)
                weigh(0, 1)
                with nc.scalar.Fori(0, GR - 1, 1) as g:
                    act.wait_ge(sem("rows_out_free"), g + (base + 1))
                    for part in range(2):
                        empty(g, part)
                        weigh(g + 1, part)
                act.wait_ge(sem("rows_out_free"), GR + base)
                for part in range(2):
                    empty(GR - 1, part)

            def attention_pass():
                def forward(g, part):
                    a, b = PARTS[part]
                    n = (b - a) * P
                    cols = slice(a * P, b * P)
                    act.wait_ge(sem("e_turned"), g * 2 + (part + 1))
                    nc.scalar.activation(eT[:, cols], bank(0, D, n), ACT.Copy).then_inc(sem("att_e_copied"), 1)
                    act.wait_ge(sem(f"keep_landed{part}"), (g + (3 * GR + 1)) * 16)
                    nc.scalar.activation(reset[:, cols], keep[:, cols], ACT.Copy, bias=NEG, scale=-NEG
                                         ).then_inc(sem("att_reset_made"), 1)
                    act.wait_ge(sem("att_u_turned"), g * 2 + (part + 1))
                    nc.scalar.activation(uT[:, cols], bank(1, D, n), ACT.Copy).then_inc(sem("att_u_copied"), 1)
                    act.wait_ge(sem("att_x5_ready"), g * 2 + (part + 1))
                    nc.scalar.activation(x2[:, cols], bank(4, D, n), ACT.Copy).then_inc(sem("att_x2_made"), 1)

                def exps(g, part):
                    a, b = PARTS[part]
                    cols = slice(a * P, b * P)
                    act.wait_ge(sem("att_falls_made"), g * 2 + (part + 1))
                    nc.scalar.activation(beta[:, cols], logit[:, cols], ACT.Exp)
                    nc.scalar.activation(alpha[:, cols], fall[:, cols], ACT.Exp).then_inc(sem("att_exps_made"), 1)

                def empty(g, part):
                    a, b = PARTS[part]
                    act.wait_ge(sem("att_sums_turned"), g * 2 + (part + 1))
                    nc.scalar.activation(rows_out[:, a * 2 * D:b * 2 * D], bank(5, P, (b - a) * 2 * D), ACT.Copy
                                         ).then_inc(sem("att_rows_out_filled"), 1)

                def forward_later(g, part):
                    act.wait_ge(sem("att_scanned"), (g - 1) * 2 + (part + 1))
                    forward(g, part)

                act.sem_inc(sem("att_rows_out_free"), 1)
                act.sem_inc(sem("att_rows_out_filled"), FREE["att_"])
                forward(0, 0)
                forward(0, 1)
                with nc.scalar.Fori(0, GR - 1, 1) as g:
                    exps(g, 0)
                    exps(g, 1)
                    forward_later(g + 1, 0)
                    act.wait_ge(sem("att_rows_out_free"), g + 1)
                    empty(g, 0)
                    forward_later(g + 1, 1)
                    empty(g, 1)
                exps(GR - 1, 0)
                exps(GR - 1, 1)
                act.wait_ge(sem("att_rows_out_free"), GR)
                empty(GR - 1, 0)
                empty(GR - 1, 1)

            def norm_help(n):
                act.wait_ge(sem("norm_centred"), n + 1)
                nc.scalar.activation(tmp2n, tmp[:, :, :], ACT.Square).then_inc(sem("norm_squares"), 1)
                act.wait_ge(sem("norm_variance"), n + 1)
                nc.scalar.activation(small[0:P, 3, :], small[0:P, 2, :], ACT.Sqrt).then_inc(sem("norm_roots"), 1)

            copy_channels(D)
            act.wait_ge(sem("deg_clamped"), 1)
            nc.scalar.activation(small[0:P, 3, :], small[0:P, 2, :], ACT.Sqrt).then_inc(sem("deg_roots"), 1)
            gcn_pass(0)
            act.wait_ge(sem("elu_input"), 1)
            nc.scalar.activation(tmp2n[:, :, 0:D1], tmp2n[:, :, 0:D1], ACT.Exp).then_inc(sem("elu_exp"), 1)
            gcn_pass(1)
            copy_channels(D1)
            act.wait_ge(sem("elu_input"), 2)
            nc.scalar.activation(tmp2n[:, :, 0:D2], tmp2n[:, :, 0:D2], ACT.Exp).then_inc(sem("elu_exp"), 1)
            gcn_pass(2)
            copy_channels(D2)
            norm_help(0)
            if last_layer >= 2:
                copy_channels(D)
                for i in range(NT):
                    n = GROUPS_BEFORE_UV + i
                    act.wait_ge(sem("products_ready"), n + 1)
                    b = 2 + n % 6
                    nc.scalar.activation(tmp[:, i, :], bank(b, P, D), ACT.Copy)
                    nc.scalar.activation(tmp2n[:, i, :], bank(b, P, D, D), ACT.Copy)
                    nc.scalar.activation(k_node[:, i, :], bank(b, P, D, 2 * D), ACT.Copy)
                    nc.scalar.activation(x6[:, i, :], bank(b, P, D, 3 * D), ACT.Copy).then_inc(sem("products_taken"), 1)
                attention_pass()
                norm_help(1)
                copy_channels(D)
                hid = 0
                for a in range(0, NT, 4):
                    m = min(4, NT - a) * P
                    if a > 0:
                        act.wait_ge(sem("products_ready"), GROUPS_BEFORE_UV + NT + a // 4)
                    for h in range(HD // 128):
                        hid += 1
                        act.wait_ge(sem("hidden_ready"), hid)
                        nc.scalar.activation(hidden(eT, uT, h)[:, 0:m], bank(h, 128, m), ACT.Relu,
                                             bias=mlp_b1[:, h:h + 1]).then_inc(sem("hidden_made"), 1)
                norm_help(2)
                norm_help(3)
            if last_layer >= 3:
                gcn_pass(4)
                copy_channels(D)
                act.wait_ge(sem("l2_variance"), 1)
                nc.scalar.activation(small[:, 5, 0:1], small[:, 4, 0:1], ACT.Sqrt).then_inc(sem("l2_root"), 1)
                norm_help(4)
            if last_layer >= 4:
                copy_channels(D)
                gcn_pass(5)
                norm_help(5)

        @block.vector
        def _(dve):
            V = nc.vector
            count = {"steps": 0, "groups": 0, "norms": 0}

            def done(ins):
                count["steps"] += 1
                ins.then_inc(sem("vector_steps"), 1)
                dve.wait_ge(sem("vector_steps"), count["steps"])
                return ins

            own_f = own[:, :, :].rearrange("p i d -> p (i d)")
            own_i = own_f.bitcast(I32)

            dve.wait_ge(sem("edge_lists_landed"), 64)
            lists_i = tmp2[0:LB, :].bitcast(I32)
            for n in range(2):
                V.tensor_copy(list_f(tmp, tmp2, n)[0:LB, :], lists_i[:, n * GE:(n + 1) * GE]).then_inc(sem("lists_float"), 1)
            dve.wait_ge(sem("lists_float"), 1)
            V.scalar_tensor_tensor(list_f(tmp, tmp2, 2)[0:LB, :], lists_i[:, 2 * GE:3 * GE], float(N), list_f(tmp, tmp2, 0)[0:LB, :],
                                   ALU.mult, ALU.add).then_inc(sem("lists_float"), 1)
            V.tensor_copy(list_f(tmp, tmp2, 3)[0:LB, :], tmp2[0:LB, 3 * GE:4 * GE]).then_inc(sem("lists_float"), 1)
            dve.wait_ge(sem("blocks_landed"), 96)
            dve.wait_ge(sem("node_numbers"), 1)
            done(V.tensor_copy(node_id[:, :], block_row[:, :]))
            keep_f = own_f[:, 4 * BL:5 * BL]
            V.tensor_tensor(keep_f[:, 1:BL], own_i[:, 1:BL], own_i[:, 0:BL - 1], ALU.is_equal)
            V.tensor_tensor(keep_f[:, 0:1], own_i[:, 0:1], own_i[:, BL:BL + 1], ALU.is_equal)
            done(V.memset(small[:, 7, :], 0.0))
            done(V.tensor_copy(keep_f[0:1, 0:1], small[0:1, 7, 0:1]))
            done(V.tensor_copy(keep_blocks(own), keep_f))
            dve.sem_inc(sem("keep_ready"), 1)
            rr = own_i[0:1, 3 * BL:3 * BL + 3 * P].rearrange("a (c p) -> a c p", c=3)
            done(V.tensor_copy(small_row(x6), rr[:, 0, :]))
            dve.sem_inc(sem("block_rows_float"), 1)
            sumw = run_w(own)
            done(V.memset(own_f[:, 5 * BL:5 * BL + 1], 0.0))
            done(V.tensor_tensor_scan(sumw, keep_f, own_f[:, 2 * BL:3 * BL], 0.0, ALU.mult, ALU.add))
            dve.sem_inc(sem("block_sums_ready"), 1)
            for n, target in enumerate((srcT, dstT, relT, weightT)):
                dve.wait_ge(sem("lists_turned"), n + 1)
                if n < 3:
                    V.tensor_copy(target[:, ET:ET + GRP], bank(n, P, GRP))
                V.tensor_copy(target[:, 0:ET], bank(n, P, ET)).then_inc(sem("lists_copied"), 1)
            dve.wait_ge(sem("block_first_spread"), 1)
            cmp = x6[:, :, 0:P]
            xfirst = small_bc(x6)
            bc_first = bank(4, P, P)
            done(V.tensor_tensor(cmp_buf(arena), bc_first[:, None, :].to_broadcast([P, NT, P]),
                                 node_id[:, :, None].to_broadcast([P, NT, P]), ALU.is_le))
            done(V.tensor_reduce(small[0:P, 4, :], cmp_buf(arena), AX.X, ALU.add))
            done(V.tensor_scalar(small[0:P, 4, :], small[0:P, 4, :], -1.0, 0.0, ALU.add, ALU.max))
            done(V.tensor_copy(block_row[:, :], small[0:P, 4, :]))
            dve.sem_inc(sem("block_row_ready"), 1)
            row = x6[0:1, 1:NT, :].rearrange("a i d -> a (i d)")
            firsts, lasts, link, whole, aa, bb, cc = (row[:, c * 128:c * 128 + P] for c in range(7))
            dve.wait_ge(sem("block_ends_landed"), 16)
            done(V.tensor_copy(firsts, rr[:, 0, :]))
            done(V.tensor_copy(lasts, rr[:, 1, :]))
            done(V.memset(row[:, 2 * 128:7 * 128], 0.0))
            done(V.tensor_tensor(link[:, 1:P], firsts[:, 1:P], lasts[:, 0:P - 1], ALU.is_equal))
            done(V.tensor_tensor(whole, firsts, lasts, ALU.is_equal))
            done(V.tensor_tensor(aa[:, 1:P], link[:, 1:P], whole[:, 0:P - 1], ALU.mult))
            done(V.tensor_tensor(bb[:, 1:P], link[:, 1:P], own_f[0:1, 3 * BL + 2 * P:3 * BL + 3 * P - 1], ALU.mult))
            done(V.tensor_tensor_scan(carry_row(own), aa, bb, 0.0, ALU.mult, ALU.add))
            dve.sem_inc(sem("carry_row_ready"), 1)
            dve.wait_ge(sem("carry_landed"), 16)
            done(V.tensor_copy(small[0:P, 5, 0:1], own_i[:, 0:1]))
            prefix = own_f[:, 2 * BL:3 * BL]
            done(V.tensor_scalar(prefix, own_i[:, 0:BL], small[0:P, 5, 0:1], small[0:P, 1, 0:1], ALU.is_equal, ALU.mult))
            done(V.tensor_tensor(sumw, sumw, prefix, ALU.add))
            dve.sem_inc(sem("degree_ready"), 1)
            dve.wait_ge(sem("block_landed"), 16 * NT)
            arena_i = arena[:, :].bitcast(I32)
            junk = tmp2[0:P, 0:BL]
            for i in range(NT):
                done(V.tensor_scalar(junk, arena_i[:, i * BL:(i + 1) * BL], node_id[:, i:i + 1], 0.0, ALU.is_le, ALU.add,
                                     accum_out=small[0:P, 5, i:i + 1]))
                done(V.tensor_scalar(junk, arena_i[:, i * BL:(i + 1) * BL], node_id[:, i:i + 1], 0.0, ALU.is_equal, ALU.add,
                                     accum_out=small[0:P, 6, i:i + 1]))
            done(V.tensor_scalar(occupied[:, :], small[0:P, 6, :], 1.0, None, ALU.min))
            done(V.scalar_tensor_tensor(small[0:P, 5, :], small[0:P, 4, :], float(BL), small[0:P, 5, :], ALU.mult, ALU.add))
            done(V.tensor_scalar(small[0:P, 5, :], small[0:P, 5, :], -1.0, 0.0, ALU.add, ALU.max))
            done(V.tensor_copy(last_edge[:, :], small[0:P, 5, :]))
            dve.sem_inc(sem("last_edge_ready"), 1)
            dve.wait_ge(sem("deg_landed"), 16 * NT)
            done(V.tensor_tensor(small[0:P, 0, :], small[0:P, 0, :], occupied[:, :], ALU.mult))
            done(V.tensor_scalar(small[0:P, 0, :], small[0:P, 0, :], 1.0, None, ALU.add))
            done(V.tensor_scalar(small[0:P, 2, :], small[0:P, 0, :], 1e-30, None, ALU.max))
            dve.sem_inc(sem("deg_clamped"), 1)
            dve.wait_ge(sem("deg_roots"), 1)
            done(V.reciprocal(small[0:P, 3, :], small[0:P, 3, :]))
            done(V.tensor_scalar(small[0:P, 0, :], small[0:P, 0, :], 0.0, None, ALU.is_gt))
            done(V.tensor_tensor(dinv[:, :], small[0:P, 0, :], small[0:P, 3, :], ALU.mult))

            def each(v, w):
                return v[:, :, None].to_broadcast([P, NT, w])

            def chan(r, n, w):
                return r[:, None, :].to_broadcast([P, n, w])

            def products(width, per_bank, take):
                for a in range(0, NT, per_bank):
                    n = count["groups"]
                    m = min(per_bank, NT - a)
                    dve.wait_ge(sem("products_ready"), n + 1)
                    ps = bank(2 + n % 6, P, m * width).rearrange("p (i d) -> p i d", d=width)
                    take(a, m, ps).then_inc(sem("products_taken"), 1)
                    count["groups"] += 1
                dve.wait_ge(sem("products_taken"), count["groups"])

            def gcn_pass(k):
                d = WIDTH[k]
                base = ORDER[k] * GR
                kbase = k * GR

                def stage(g, b):
                    V.tensor_copy(idx[:, b:b + 1], GCN[k][2][:, bass.ds(g * GRP + b, 1)]).then_inc(sem("idx_staged"), 1)

                def scan(g, part):
                    a, b = PARTS[part]
                    for i in range(a, b):
                        dve.wait_ge(sem(f"rows_landed{i}"), (g + (base + 1)) * 16)
                        stage(g + 1, i)
                    dve.wait_ge(sem(f"keep_landed{part}"), (g + (kbase + 1)) * 16)
                    dve.wait_ge(sem("rows_turned"), (g + base) * GRP + b)
                    before = run_s[0:d, a * P - 1:a * P] if part else run_s[0:d, GE - 1:GE]
                    V.tensor_tensor_scan(run_s[0:d, a * P:b * P], keep[0:d, a * P:b * P], bank(part, d, (b - a) * P),
                                         before, ALU.mult, ALU.add).then_inc(sem("scanned"), 1)

                for b in range(GRP):
                    stage(0, b)
                scan(0, 0)
                dve.wait_ge(sem("scanned"), base * 2 + 1)
                scan(0, 1)
                with V.Fori(1, GR, 1) as g:
                    for part in range(2):
                        dve.wait_ge(sem("scanned"), (g + base) * 2 + part)
                        dve.wait_ge(sem("sums_turned"), (g + (base - 1)) * 2 + (part + 1))
                        scan(g, part)

            def take_ends(k, w):
                dve.wait_ge(sem(f"ends_landed{k}"), 16 * NT)
                done(V.tensor_tensor(ends(w), ends(w), each(occupied, w), ALU.mult))

            def elu(dst_ap, src_ap, w, n):
                done(V.tensor_scalar(tmp2n[:, :, 0:w], src_ap, 0.0, None, ALU.min))
                dve.sem_inc(sem("elu_input"), 1)
                dve.wait_ge(sem("elu_exp"), n)
                done(V.tensor_scalar(src_ap, src_ap, 0.0, -1.0, ALU.max, ALU.add))
                done(V.tensor_tensor(dst_ap, src_ap, tmp2n[:, :, 0:w], ALU.add))

            def layer_norm(dst_ap, src_ap):
                n = count["norms"]
                done(V.tensor_reduce(small[0:P, 1, :], src_ap, AX.X, ALU.add))
                done(V.tensor_scalar(small[0:P, 1, :], small[0:P, 1, :], 1.0 / D, None, ALU.mult))
                done(V.tensor_tensor(tmp[:, :, :], src_ap, each(small[0:P, 1, :], D), ALU.subtract))
                dve.sem_inc(sem("norm_centred"), 1)
                dve.wait_ge(sem("norm_squares"), n + 1)
                done(V.tensor_reduce(small[0:P, 2, :], tmp2n, AX.X, ALU.add))
                done(V.tensor_scalar(small[0:P, 2, :], small[0:P, 2, :], 1.0 / D, EPS, ALU.mult, ALU.add))
                dve.sem_inc(sem("norm_variance"), 1)
                dve.wait_ge(sem("norm_roots"), n + 1)
                done(V.reciprocal(small[0:P, 3, :], small[0:P, 3, :]))
                done(V.tensor_tensor(dst_ap, tmp[:, :, :], each(small[0:P, 3, :], D), ALU.mult))
                count["norms"] += 1

            dve.wait_ge(sem("deg_stored"), 16)
            products(D1, BANK // D1, lambda a, m, ps: V.tensor_tensor(
                own[:, a:a + m, 0:D1], ps, dinv[:, a:a + m, None].to_broadcast([P, m, D1]), ALU.mult))
            dve.sem_inc(sem("table_ready0"), 1)
            for k, w in ((0, D1), (1, D1), (2, D2)):
                gcn_pass(k)
                take_ends(k, w)
                done(V.tensor_tensor(tmp[:, :, 0:w], ends(w), own[:, :, 0:w], ALU.add))
                done(V.tensor_tensor(tmp[:, :, 0:w], tmp[:, :, 0:w], each(dinv, w), ALU.mult))
                if k == 0:
                    done(V.tensor_tensor(tmp[:, :, 0:w], tmp[:, :, 0:w], chan(row_of["L0_gnn_b1"], NT, w), ALU.add))
                    elu(tmp[:, :, 0:w], tmp[:, :, 0:w], w, 1)
                    done(V.tensor_tensor(own[:, :, 0:w], tmp[:, :, 0:w], each(dinv, w), ALU.mult))
                    dve.sem_inc(sem("table_ready1"), 1)
                elif k == 1:
                    dve.sem_inc(sem("conv2_input"), 1)
                    b2 = row_of["L0_gnn_b2"]
                    products(D2, BANK // D2, lambda a, m, ps: V.tensor_tensor(
                        own[:, a:a + m, 0:D2], ps, chan(b2, m, D2), ALU.add))
                    elu(own[:, :, 0:D2], own[:, :, 0:D2], D2, 2)
                    done(V.tensor_tensor(own[:, :, 0:D2], own[:, :, 0:D2], each(dinv, D2), ALU.mult))
                    dve.sem_inc(sem("table_ready2"), 1)
                else:
                    dve.sem_inc(sem("conv3_input"), 1)
                    done(V.tensor_tensor(x[:, :, :], x[:, :, :], chan(row_of["L0_gnn_b3"], NT, D), ALU.add))
                    products(D, BANK // D, lambda a, m, ps: V.tensor_tensor(
                        x[:, a:a + m, :], ps, x[:, a:a + m, :], ALU.add))
                    layer_norm(x[:, :, :], x[:, :, :])
                    dve.sem_inc(sem("x_new"), 1)

            def attention_pass():
                def stage(g, part):
                    a, b = PARTS[part]
                    V.tensor_copy(idx[:, a:b], srcT[:, bass.ds(g * GRP + a, b - a)])
                    V.tensor_copy(v_idx[:, a:b], dstT[:, bass.ds(g * GRP + a, b - a)]).then_inc(sem("att_idx_staged"), 1)

                def first_half(g, part, first):
                    a, b = PARTS[part]
                    n = (b - a) * P
                    cols = slice(a * P, b * P)
                    c = g * 2 + part
                    steps = sem("att_steps")
                    dve.wait_ge(sem("att_edges_mixed"), c + 1)
                    stage(g + 1, part)
                    dve.wait_ge(sem("att_u_copied"), c + 1)
                    dve.wait_ge(sem("att_reset_made"), c + 1)
                    V.tensor_tensor(logit[:, cols], bank(2 + part, D, n), uT[:, cols], ALU.mult
                                    ).then_inc(sem("att_logits_made"), 1)
                    if part == 0 and not first:
                        V.tensor_copy(run_m[:, 0:1], run_m[:, GE:GE + 1]).then_inc(steps, 1)
                    else:
                        dve.sem_inc(steps, 1)
                    dve.wait_ge(steps, c * 4 + 1)
                    dve.wait_ge(sem("att_logits_made"), c + 1)
                    V.tensor_tensor_scan(run_m[:, 1 + a * P:1 + b * P], reset[:, cols], logit[:, cols],
                                         run_m[:, a * P:a * P + 1], ALU.add, ALU.max).then_inc(steps, 1)
                    dve.wait_ge(steps, c * 4 + 2)
                    V.tensor_tensor(logit[:, cols], logit[:, cols], run_m[:, 1 + a * P:1 + b * P], ALU.subtract)
                    V.tensor_tensor(fall[:, cols], run_m[:, a * P:b * P], run_m[:, 1 + a * P:1 + b * P], ALU.subtract
                                    ).then_inc(steps, 1)
                    dve.wait_ge(steps, c * 4 + 3)
                    V.tensor_tensor(fall[:, cols], fall[:, cols], reset[:, cols], ALU.add).then_inc(sem("att_falls_made"), 1)
                    dve.sem_inc(steps, 1)

                def second_half(g, part, first):
                    a, b = PARTS[part]
                    cols = slice(a * P, b * P)
                    c = g * 2 + part
                    dve.wait_ge(sem("att_exps_made"), c + 1)
                    dve.wait_ge(sem("att_x2_made"), c + 1)
                    if not first:
                        dve.wait_ge(sem("att_sums_turned"), (g - 1) * 2 + (part + 1))
                    V.tensor_tensor(betax[:, cols], beta[:, cols], x2[:, cols], ALU.mult).then_inc(sem("att_betax_made"), 1)
                    at = a * P - 1 if part else GE - 1
                    V.tensor_tensor_scan(run_s[:, cols], alpha[:, cols], beta[:, cols], run_s[:, at:at + 1],
                                         ALU.mult, ALU.add)
                    dve.wait_ge(sem("att_betax_made"), c * 2 + 1)
                    V.scalar_tensor_tensor(betax[:, cols], betax[:, cols], SLOPE, betax[:, cols], ALU.mult, ALU.max
                                           ).then_inc(sem("att_betax_made"), 1)
                    dve.wait_ge(sem("att_betax_made"), c * 2 + 2)
                    V.tensor_tensor_scan(run_n[:, cols], alpha[:, cols], betax[:, cols], run_n[:, at:at + 1],
                                         ALU.mult, ALU.add).then_inc(sem("att_scanned"), 1)

                stage(0, 0)
                stage(0, 1)
                first_half(0, 0, True)
                first_half(0, 1, True)
                second_half(0, 0, True)
                first_half(1, 0, False)
                second_half(0, 1, True)
                with V.Fori(1, GR - 1, 1) as g:
                    first_half(g, 1, False)
                    second_half(g, 0, False)
                    first_half(g + 1, 0, False)
                    second_half(g, 1, False)
                first_half(GR - 1, 1, False)
                second_half(GR - 1, 0, False)
                second_half(GR - 1, 1, False)

            def affine(v):
                done(V.tensor_tensor(v, v, chan(row_of["L1_gnn_gamma"], NT, D), ALU.mult))
                done(V.tensor_tensor(v, v, chan(row_of["L1_gnn_beta"], NT, D), ALU.add))

            if last_layer >= 2:
                count["groups"] += NT
                dve.wait_ge(sem("products_taken"), count["groups"])
                for v in (tmp[:, :, :], tmp2n, k_node):
                    done(V.scalar_tensor_tensor(v, v, SLOPE, v, ALU.mult, ALU.max))
                done(V.tensor_scalar(tmp[:, :, :], tmp[:, :, :], float(HEAD) ** -0.5, None, ALU.mult))
                dve.sem_inc(sem("u_ready"), 1)
                dve.wait_ge(sem("uv_stored"), 32)
                attention_pass()
                dve.wait_ge(sem("ends_landed3"), 16 * NT)
                both = ends(2 * D)
                num, den = both[:, :, 0:D], both[:, :, D:2 * D]
                done(V.tensor_tensor(tmp[:, :, :], k_node, den, ALU.mult))
                done(V.tensor_tensor(tmp[:, :, :], tmp[:, :, :], num, ALU.add))
                done(V.tensor_scalar(den, den, 1e-20, None, ALU.add))
                done(V.reciprocal(den, den))
                done(V.tensor_tensor(tmp[:, :, :], tmp[:, :, :], den, ALU.mult))
                done(V.tensor_tensor(tmp[:, :, :], tmp[:, :, :], each(occupied, D), ALU.mult))
                done(V.tensor_tensor(x6[:, :, :], x6[:, :, :], tmp[:, :, :], ALU.add))
                layer_norm(tmp[:, :, :], x6[:, :, :])
                affine(tmp[:, :, :])
                dve.sem_inc(sem("mlp_input"), 1)
                done(V.tensor_tensor(x6[:, :, :], tmp[:, :, :], chan(row_of["L1_gnn_mlp_b2"], NT, D), ALU.add))
                products(D, 4, lambda a, m, ps: V.tensor_tensor(x6[:, a:a + m, :], ps, x6[:, a:a + m, :], ALU.add))
                layer_norm(x6[:, :, :], x6[:, :, :])
                affine(x6[:, :, :])
                done(V.tensor_tensor(x[:, :, :], x[:, :, :], x6[:, :, :], ALU.add))
                layer_norm(x[:, :, :], x[:, :, :])
                dve.sem_inc(sem("x_new"), 1)
            if last_layer >= 3:
                dve.sem_inc(sem("table_ready4"), 1)
                gcn_pass(4)
                dve.wait_ge(sem("ends_landed4"), 16 * NT)
                done(V.tensor_tensor(tmp[:, :, :], ends(D), each(occupied, D), ALU.mult))
                dve.sem_inc(sem("l2_input"), 1)
                h = tmp2[:, 0:N]
                col = lambda c: l2_cols[:, c:c + 1]
                for a in range(0, NT, 4):
                    n = count["groups"]
                    m = min(4, NT - a) * P
                    dve.wait_ge(sem("products_ready"), n + 1)
                    V.tensor_scalar(h[:, a * P:a * P + m], bank(2 + n % 6, D, m), col(0), None, ALU.add
                                    ).then_inc(sem("products_taken"), 1)
                    count["groups"] += 1
                dve.wait_ge(sem("products_taken"), count["groups"])

                def prelu(c):
                    done(V.tensor_scalar(arena_h(xT), h, 0.0, col(c), ALU.min, ALU.mult))
                    done(V.scalar_tensor_tensor(h, h, 0.0, arena_h(xT), ALU.max, ALU.add))
                prelu(3)
                s = small[:, 4, :]
                done(V.tensor_reduce(s[:, 1:2], h, AX.X, ALU.add))
                done(V.tensor_scalar(s[:, 1:2], s[:, 1:2], 1.0 / N, None, ALU.mult))
                done(V.tensor_scalar(h, h, s[:, 1:2], None, ALU.subtract))
                done(V.tensor_tensor(arena_h(xT), h, h, ALU.mult))
                done(V.tensor_reduce(s[:, 0:1], arena_h(xT), AX.X, ALU.add))
                done(V.tensor_scalar(s[:, 0:1], s[:, 0:1], 1.0 / N, EPS, ALU.mult, ALU.add))
                dve.sem_inc(sem("l2_variance"), 1)
                dve.wait_ge(sem("l2_root"), 1)
                done(V.reciprocal(s[:, 2:3], small[:, 5, 0:1]))
                done(V.tensor_tensor(s[:, 2:3], s[:, 2:3], col(1), ALU.mult))
                done(V.tensor_scalar(h, h, s[:, 2:3], col(2), ALU.mult, ALU.add))
                prelu(4)
                dve.sem_inc(sem("l2_normed"), 1)
                products(D, 4, lambda a, m, ps: V.tensor_tensor(x[:, a:a + m, :], ps, x[:, a:a + m, :], ALU.add))
                layer_norm(x[:, :, :], x[:, :, :])
                dve.sem_inc(sem("x_new"), 1)
            if last_layer >= 4:
                for i in range(NT):
                    n = count["groups"]
                    dve.wait_ge(sem("products_ready"), n + 1)
                    if i >= SLOTS:
                        dve.wait_ge(sem(f"rel_written{i % SLOTS}"), 16 * (i // SLOTS))
                    V.tensor_copy(rel_buf(arena)[:, i % SLOTS, :], bank(2 + n % 6, P, NREL * D)).then_inc(sem("products_taken"), 1)
                    count["groups"] += 1
                    dve.wait_ge(sem("products_taken"), count["groups"])
                    dve.sem_inc(sem("rel_rows_ready"), 1)
                gcn_pass(5)
                dve.wait_ge(sem("ends_landed5"), 16 * NT)
                done(V.tensor_tensor(ends(D), ends(D), each(occupied, D), ALU.mult))
                done(V.scalar_tensor_tensor(x[:, :, :], ends(D), 0.0, x[:, :, :], ALU.max, ALU.add))
                layer_norm(x[:, :, :], x[:, :, :])
            dve.sem_inc(sem("out_ready"), 1)


WEIGHT_LOADS = 25
SLOTS = 6
FREE = {"": 2, "att_": 1}
GROUPS_BEFORE_UV = 2 + 4 + 7
BLK = 425


def flat(a):
    return a[:, :, :].rearrange("p i d -> p (i d)")


def keep_blocks(own):
    return flat(own)[:, 5 * BLK + 8:6 * BLK + 8].bitcast(BF16)[:, 0:BLK]


def run_w(own):
    return flat(own)[:, 6 * BLK + 16:7 * BLK + 16]


def carry_row(own):
    return flat(own)[0:1, 7 * BLK + 16:7 * BLK + 16 + P]


def small_row(x6):
    return flat(x6)[0:1, 0:P]


def small_bc(x6):
    return flat(x6)[:, 0:P]


def cmp_buf(arena):
    return arena[:, 0:25 * P].rearrange("p (i b) -> p i b", b=P)


def list_f(tmp, tmp2, n):
    return flat(tmp)[:, n * 625:(n + 1) * 625]


def hidden(a, b, h):
    return a if h == 0 else b


def arena_h(xT):
    return xT[:, :]


def rel_buf(arena):
    return arena[:, 0:SLOTS * 384].rearrange("p (s d) -> p s d", d=384)


def channels_needed(total, tile):
    return total - 7 + tile // 4 + 1


_INS = ['x', 'src', 'dst', 'edge_attr_128', 'edge_type_3', 'edge_weight', 'L0_gnn_W1', 'L0_gnn_b1', 'L0_gnn_W2',
        'L0_gnn_b2', 'L0_gnn_W3', 'L0_gnn_b3', 'L1_gnn_w1', 'L1_gnn_w2', 'L1_gnn_w3', 'L1_gnn_w4', 'L1_gnn_w5',
        'L1_gnn_w6', 'L1_gnn_mlp_w1', 'L1_gnn_mlp_b1', 'L1_gnn_mlp_w2', 'L1_gnn_mlp_b2', 'L1_gnn_gamma',
        'L1_gnn_beta', 'L2_gnn_W', 'L2_gnn_b', 'L2_gnn_a1', 'L2_gnn_gamma', 'L2_gnn_beta', 'L2_gnn_a2',
        'L3_gnn_weight']


def kernel(**inputs):
    import numpy as _np
    import concourse.bacc as _bacc
    from concourse import mybir as _mybir
    from concourse.bass_utils import run_bass_kernel_spmd as _run

    nc = _bacc.Bacc("TRN2", target_bir_lowering=False, num_devices=1)
    arrays, t = {}, {}
    for name in _INS:
        a = _np.ascontiguousarray(inputs[name])
        arrays["in_" + name] = a
        t[name] = nc.dram_tensor("in_" + name, a.shape, _mybir.dt.from_np(a.dtype), kind="ExternalInput").ap()
    out = nc.dram_tensor("out_0", t["x"].shape, _mybir.dt.float32, kind="ExternalOutput").ap()
    build(nc, t, out)
    r = _run(nc, [arrays], core_ids=[0])
    return r.results[0]["out_0"]
```

```python
import concourse.bass as bass
from concourse import mybir
from contextlib import ExitStack

FP32 = mybir.dt.float32
BF16 = mybir.dt.bfloat16
I32 = mybir.dt.int32
ALU = mybir.AluOpType
ACT = mybir.ActivationFunctionType
AX = mybir.AxisListType

P = 125
GRP = 5
CUT = 3
PARTS = ((0, CUT), (CUT, GRP))
BANK = 512
NEG = -1.0e38
EPS = 1e-5
SLOPE = 0.01


def build(nc, t, out, last_layer=4):
    N, D = t["x"].shape
    E = t["src"].shape[0]
    NT = N // P
    ET = E // P
    GR = ET // GRP
    GE = GRP * P
    BL = E // P
    LB = ET // GRP
    assert N == NT * P and E == ET * P and ET == GR * GRP and D == 128
    D1 = t["L0_gnn_W1"].shape[1]
    D2 = t["L0_gnn_W2"].shape[1]
    HD = t["L1_gnn_mlp_w1"].shape[1]
    NREL = t["L3_gnn_weight"].shape[0]
    HEAD = 32
    ctx = ExitStack()
    with ctx:
        def sb(name, shape, dt=FP32):
            return ctx.enter_context(nc.sbuf_tensor(name, shape, dt))

        def dram(name, shape, dt=FP32):
            return nc.dram_tensor(name, shape, dt, kind="Internal").ap()

        sems = {}

        def sem(name):
            if name not in sems:
                sems[name] = ctx.enter_context(nc.semaphore(name))
            return sems[name]

        keep_d = dram("keep_d", (E,), BF16)
        reset_d = dram("reset_d", (E + 1,), BF16)
        deg_d = dram("deg_d", (E, 1))
        table = [dram("table1", (N, D1)), dram("table2", (N, D1)), dram("table3", (N, D2)), None,
                 dram("table5", (N, D)), dram("table6", (NREL * N, D))]
        u_table = dram("u_table", (N, D))
        v_table = dram("v_table", (N, D))
        spread_v = dram("spread_v", (E + N, D))
        before_d = dram("before_d", (N + 1,))
        WIDTH = [D1, D1, D2, 2 * D, D, D]
        sums_d = [dram(f"sums{k}", (E, w)) for k, w in enumerate(WIDTH)]

        ident = sb("ident", [128, 128])
        ones = sb("ones", [1, 128])
        srcT = sb("srcT", [P, ET + GRP], I32)
        dstT = sb("dstT", [P, ET])
        relT = sb("relT", [P, ET + GRP], I32)
        weightT = sb("weightT", [P, ET])
        node_id = sb("node_id", [P, NT])
        last_edge = sb("last_edge", [P, NT], I32)
        block_row = sb("block_row", [P, NT], I32)
        occupied = sb("occupied", [P, NT])
        dinv = sb("dinv", [P, NT])
        row_of = {n: sb(n + "_row", [P, t[n].shape[0]]) for n in
                  ("L0_gnn_b1", "L0_gnn_b2", "L0_gnn_b3", "L1_gnn_mlp_b2", "L1_gnn_gamma", "L1_gnn_beta")}
        w1 = sb("w1", [D, D1])
        w2 = sb("w2", [D1, D2])
        w3 = sb("w3", [D2, D])
        att_w = sb("att_w", [D, 4, D])
        w_e3 = sb("w_e3", [D, D])
        w_e5 = sb("w_e5", [D, D])
        mlp1 = sb("mlp1", [D, HD])
        mlp2 = sb("mlp2", [128, HD // 128, D])
        mlp_b1 = sb("mlp_b1", [128, HD // 128])
        w_l2 = sb("w_l2", [D, D])
        l2_cols = sb("l2_cols", [D, 5])
        rel_w = sb("rel_w", [D, NREL, D])

        x = sb("x", [P, NT, D])
        xT = sb("xT", [D, N])
        tmp = sb("tmp", [P, NT, D])
        tmp2 = sb("tmp2", [128, NT * D])
        own = sb("own", [P, NT, D])
        x6 = sb("x6", [P, NT, D])
        arena = sb("arena", [P, max(NT * BL, NT * 3 * D)])
        k_node = arena[:, 2 * NT * D:3 * NT * D].rearrange("p (i d) -> p i d", d=D)
        small = sb("small", [128, 8, NT])
        tmp2n = tmp2[0:P, :].rearrange("p (i d) -> p i d", d=D)

        def ends(d):
            return arena[:, 0:NT * d].rearrange("p (i d) -> p i d", d=d)

        rows = sb("rows", [P, GRP, D])
        v_rows = sb("v_rows", [P, GRP, D])
        e_rows = sb("e_rows", [P, GRP, D])
        idx = sb("idx", [P, GRP], I32)
        dst_row = sb("dst_row", [P, GE], I32)
        same = sb("same", [P, GE])
        zeros = sb("zeros", [P, D])
        start_dst = sb("start_dst", [LB, GRP], I32)
        start_v = sb("start_v", [LB, GRP, D])
        first_edge = sb("first_edge", [P, NT], I32)
        keep = sb("keep", [128, GE], BF16)
        run_s = sb("run_s", [D, GE])
        run_n = sb("run_n", [D, GE])
        run_m = sb("run_m", [D, 1 + GE])
        logit = sb("logit", [D, GE])
        fall = sb("fall", [D, GE])
        alpha = sb("alpha", [D, GE])
        beta = sb("beta", [D, GE])
        betax = sb("betax", [D, GE])
        eT = sb("eT", [D, GE])
        uT = sb("uT", [D, GE])
        rows_out = sb("rows_out", [P, GRP * 2 * D])
        PS = ctx.enter_context(nc.psum_tensor("PS", [128, 8 * BANK], FP32))

        def bank(b, p, n, at=0):
            return PS[0:p, b * BANK + at:b * BANK + at + n]

        def tiles(dr, p=P):
            return dr.rearrange("(i p) d -> p i d", p=p)

        ctx.enter_context(nc.allow_non_contiguous_dma(reason="index lists and columns of weights, once"))
        block = ctx.enter_context(nc.Block())

        GCN = {0: (D1, table[0], srcT), 1: (D1, table[1], srcT), 2: (D2, table[2], srcT),
               4: (D, table[4], srcT), 5: (D, table[5], relT)}
        ORDER = {0: 0, 1: 1, 2: 2, 4: 3, 5: 4}

        @block.gpsimd
        def _(eng):
            nc.gpsimd.memset(ident[:, :], 0.0).then_inc(sem("ident_cleared"), 1)
            nc.gpsimd.memset(ones[:, :], 1.0)
            nc.gpsimd.memset(zeros[:, :], 0.0)
            nc.gpsimd.memset(run_s[:, :], 0.0)
            nc.gpsimd.memset(run_n[:, :], 0.0)
            nc.gpsimd.memset(run_m[:, :], NEG)
            nc.gpsimd.iota(block_row[:, :], [[P, NT]], base=0, channel_multiplier=1).then_inc(sem("node_numbers"), 1)
            eng.wait_ge(sem("ident_cleared"), 1)
            nc.gpsimd.affine_select(out=ident[:, :], in_=ident[:, :], compare_op=ALU.not_equal, fill=1.0,
                                    base=0, pattern=[[-1, 128]], channel_multiplier=1).then_inc(sem("const_ready"), 1)

            eng.wait_ge(sem("block_row_ready"), 1)
            dst_blocks = t["dst"].rearrange("(b l) -> b l", l=BL)
            arena_i = arena[:, :].bitcast(I32)
            for i in range(NT):
                eng.indirect_dma_start(out=arena_i[:, i * BL:(i + 1) * BL], out_offset=None, in_=dst_blocks,
                                       in_offset=bass.IndirectOffsetOnAxis(ap=block_row[:, i:i + 1], axis=0)
                                       ).then_inc(sem("block_landed"), 16)
            eng.wait_ge(sem("last_edge_ready"), 1)
            eng.wait_ge(sem("deg_stored"), 16)
            for i in range(NT):
                eng.indirect_dma_start(out=small[0:P, 0, i:i + 1], out_offset=None, in_=deg_d,
                                       in_offset=bass.IndirectOffsetOnAxis(ap=last_edge[:, i:i + 1], axis=0)
                                       ).then_inc(sem("deg_landed"), 16)

            def gather(dst_ap, tab, index):
                return eng.indirect_dma_start(out=dst_ap, out_offset=None, in_=tab,
                                              in_offset=bass.IndirectOffsetOnAxis(ap=index, axis=0))

            def gather_pass(k):
                d, tab, index = GCN[k]
                base = ORDER[k] * GR
                staged = ORDER[k] * (GR + 1) * GRP
                eng.wait_ge(sem(f"table_stored{k}"), 16)

                for b in range(GRP):
                    eng.wait_ge(sem("idx_staged"), staged + b + 1)
                    if base:
                        eng.wait_ge(sem("rows_turned"), (base - 1) * GRP + (b + 1))
                    gather(rows[:, b, 0:d], tab, idx[:, b:b + 1]).then_inc(sem(f"rows_landed{b}"), 16)
                with nc.gpsimd.Fori(1, GR, 1) as g:
                    for b in range(GRP):
                        eng.wait_ge(sem("idx_staged"), g * GRP + (staged + b + 1))
                        nc.gpsimd.nop(nofuse=True)
                        eng.wait_ge(sem("rows_turned"), (g + (base - 1)) * GRP + (b + 1))
                        nc.gpsimd.nop(nofuse=True)
                        gather(rows[:, b, 0:d], tab, idx[:, b:b + 1]).then_inc(sem(f"rows_landed{b}"), 16)

            def fetch_ends(k):
                w = WIDTH[k]
                eng.wait_ge(sem(f"sums_stored{k}"), 1)
                for i in range(NT):
                    gather(arena[:, i * w:(i + 1) * w], sums_d[k], last_edge[:, i:i + 1]).then_inc(sem(f"ends_landed{k}"), 16)

            def attention_pass():
                eng.wait_ge(sem("first_edge_ready"), 1)
                eng.wait_ge(sem("uv_ready"), 1)
                eng.wait_ge(sem("spread_zeroed"), 16 * GR)
                for i in range(NT):
                    eng.indirect_dma_start(out=spread_v, out_offset=bass.IndirectOffsetOnAxis(ap=first_edge[:, i:i + 1], axis=0),
                                           in_=tmp2n[:, i, :], in_offset=None).then_inc(sem("v_spread"), 16)
                eng.wait_ge(sem("start_dst_landed"), 16)
                eng.wait_ge(sem("uv_stored"), 32)
                for j in range(GRP):
                    gather(start_v[:, j, :], v_table, start_dst[:, j:j + 1]).then_inc(sem("start_v_landed"), 16)

                def part_gathers(g, part, first):
                    a, b = PARTS[part]
                    if not first:
                        eng.wait_ge(sem("att_u_turned"), (g - 1) * 2 + (part + 1))
                    nc.gpsimd.tensor_copy(idx[:, a:b], srcT[:, bass.ds(g * GRP + a, b - a)]).then_inc(sem("att_idx_staged"), 1)
                    eng.wait_ge(sem("att_idx_staged"), g * 2 + (part + 1))
                    nc.gpsimd.nop(nofuse=True)
                    for i in range(a, b):
                        gather(rows[:, i, :], u_table, idx[:, i:i + 1]).then_inc(sem(f"att_rows_landed{i}"), 16)
                for part in range(2):
                    part_gathers(0, part, True)
                with nc.gpsimd.Fori(1, GR, 1) as g:
                    for part in range(2):
                        part_gathers(g, part, False)

            for k in range(3):
                gather_pass(k)
                fetch_ends(k)
            if last_layer >= 2:
                attention_pass()
                fetch_ends(3)
            for k in (4, 5)[:max(0, last_layer - 2)]:
                gather_pass(k)
                fetch_ends(k)

        @block.sync
        def _(eng):
            arrive = sem("edge_lists_landed")
            for n, name in enumerate(("src", "dst", "edge_type_3", "edge_weight")):
                view = (tmp2[0:LB, n * GE:(n + 1) * GE])
                if name != "edge_weight":
                    view = view.bitcast(I32)
                eng.dma_start(view.rearrange("r (j p) -> r j p", j=GRP),
                              t[name].rearrange("(j r p) -> r j p", j=GRP, p=P)).then_inc(arrive, 16)
            blk = sem("blocks_landed")
            own_i = own[:, :, :].rearrange("p i d -> p (i d)").bitcast(I32)
            eng.dma_start(own_i[:, 0:BL], t["dst"].rearrange("(p l) -> p l", l=BL)).then_inc(blk, 16)
            eng.dma_start(own_i[1:P, BL:BL + 1], t["dst"].rearrange("(p l) -> p l", l=BL)[0:P - 1, BL - 1:BL]).then_inc(blk, 16)
            eng.dma_start(own_i[0:1, BL:BL + 1], t["dst"].rearrange("(a n) -> a n", a=1)[:, 0:1]).then_inc(blk, 16)
            eng.dma_start(own[:, :, :].rearrange("p i d -> p (i d)")[:, 2 * BL:3 * BL],
                          t["edge_weight"].rearrange("(p l) -> p l", l=BL)).then_inc(blk, 16)
            own_r = own_i[0:1, 3 * BL:3 * BL + 3 * P].rearrange("a (c p) -> a c p", c=3)
            for c, at in ((0, 0), (1, BL - 1)):
                eng.dma_start(own_r[:, c, :], t["dst"].rearrange("(a p l) -> a p l", a=1, l=BL)[:, :, at]).then_inc(blk, 16)
            eng.dma_start(x[:, :, :], tiles(t["x"])).then_inc(sem("x_landed"), 16)
            eng.dma_start(start_dst[:, :], t["dst"].rearrange("(j r p) -> r j p", j=GRP, p=P)[:, :, 0]).then_inc(sem("start_dst_landed"), 16)
            wl = sem("weights_landed")
            loads = [(w1[:, :], t["L0_gnn_W1"]), (w2[:, :], t["L0_gnn_W2"]), (w3[:, :], t["L0_gnn_W3"])]
            for c, n in enumerate(("w1", "w2", "w4", "w6")):
                loads.append((att_w[:, c, :], t["L1_gnn_" + n]))
            loads += [(w_e3[:, :], t["L1_gnn_w3"]), (w_e5[:, :], t["L1_gnn_w5"]), (mlp1[:, :], t["L1_gnn_mlp_w1"]),
                      (mlp2[:, :, :], t["L1_gnn_mlp_w2"].rearrange("(c p) d -> p c d", p=128)),
                      (mlp_b1[:, :], t["L1_gnn_mlp_b1"].rearrange("(c p) -> p c", p=128)),
                      (w_l2[:, :], t["L2_gnn_W"]),
                      (rel_w[:, :, :], t["L3_gnn_weight"].rearrange("r i o -> i r o"))]
            for c, n in enumerate(("b", "gamma", "beta")):
                loads.append((l2_cols[:, c:c + 1], t["L2_gnn_" + n].rearrange("(p a) -> p a", a=1)))
            for c, n in enumerate(("a1", "a2")):
                loads.append((l2_cols[:, 3 + c:4 + c], t["L2_gnn_" + n].rearrange("(a n) -> a n", a=1).to_broadcast([D, 1])))
            for n, r in row_of.items():
                loads.append((r[:, :], t[n].rearrange("(a n) -> a n", a=1).to_broadcast([P, t[n].shape[0]])))
            assert len(loads) == WEIGHT_LOADS
            for dst_ap, src_ap in loads:
                eng.dma_start(dst_ap, src_ap).then_inc(wl, 16)

            eng.wait_ge(sem("keep_ready"), 1)
            eng.dma_start(keep_d.rearrange("(p l) -> p l", l=BL), keep_blocks(own)).then_inc(sem("keep_stored"), 16)
            reset_v = reset_d.rearrange("(a n) -> a n", a=1)
            eng.dma_start(reset_v[:, 0:E].rearrange("a (p l) -> (a p) l", l=BL), reset_blocks(own)).then_inc(sem("keep_stored"), 16)
            eng.dma_start(reset_v[:, E:E + 1], reset_blocks(own)[0:1, 0:1]).then_inc(sem("keep_stored"), 16)
            eng.wait_ge(sem("block_sums_ready"), 1)
            own_rf = own[0:1, :, :].rearrange("a i d -> a (i d)")
            eng.dma_start(own_rf[:, 3 * BL + 2 * P:3 * BL + 3 * P], run_w(own)[:, BL - 1:BL]).then_inc(sem("block_ends_landed"), 16)
            eng.wait_ge(sem("carry_row_ready"), 1)
            eng.dma_start(small[0:P, 1, 0:1], carry_row(own)).then_inc(sem("carry_landed"), 16)
            eng.wait_ge(sem("degree_ready"), 1)
            eng.dma_start(deg_d.rearrange("(p l) a -> p (l a)", l=BL), run_w(own)).then_inc(sem("deg_stored"), 16)
            eng.wait_ge(sem("keep_stored"), 48)

            def load_keep(k, g, part):
                a, b = PARTS[part]
                if k == 3:
                    src_ap = reset_v[:, bass.ds(g * GE + (a * P + 1), (b - a) * P)]
                else:
                    src_ap = keep_d.rearrange("(a n) -> a n", a=1)[:, bass.ds(g * GE + a * P, (b - a) * P)]
                eng.dma_start(keep[:, a * P:b * P], src_ap.to_broadcast([128, (b - a) * P])).then_inc(sem(f"keep_landed{part}"), 16)

            def stream(k):
                d = WIDTH[k]
                out_v = sums_d[k].rearrange("(i p) d -> p i d", p=P)
                base = ORDER[k] * GR

                def store(g):
                    eng.wait_ge(sem("rows_out_filled"), (g + base) * 2 + (2 + FREE))
                    eng.dma_start(out_v[:, bass.ds(g * GRP, GRP), :],
                                  rows_out[:, 0:GRP * d].rearrange("p (b d) -> p b d", d=d)).then_inc(sem("sums_written"), 16)
                    eng.wait_ge(sem("sums_written"), (g + (base + 1)) * 16)
                    eng.sem_inc(sem("rows_out_free"), 1)

                for part in range(2):
                    load_keep(k, 0, part)
                def clear(g):
                    eng.dma_start(tiles(spread_v[0:E, :])[:, bass.ds(g * GRP, GRP), :],
                                  zeros[:, None, :].to_broadcast([P, GRP, D])).then_inc(sem("spread_zeroed"), 16)

                with nc.sync.Fori(0, GR - 1, 1) as g:
                    if k == 0:
                        clear(g)
                    for part in range(2):
                        eng.wait_ge(sem("scanned"), (g + base) * 2 + (part + 1))
                        load_keep(k, g + 1, part)
                    store(g)
                if k == 0:
                    clear(GR - 1)
                store(GR - 1)
                eng.sem_inc(sem(f"sums_stored{k}"), 1)

            def attention_loads():
                def edge_rows(g, part):
                    a, b = PARTS[part]
                    eng.dma_start(e_rows[:, a:b, :], tiles(t["edge_attr_128"])[:, bass.ds(g * GRP + a, b - a), :]
                                  ).then_inc(sem(f"e_rows_landed{part}"), 16)

                def dst_rows(g, part):
                    a, b = PARTS[part]
                    src_ap = t["dst"].rearrange("(a n) -> a n", a=1)[:, bass.ds(g * GE + a * P, (b - a) * P)]
                    eng.dma_start(dst_row[:, a * P:b * P], src_ap.to_broadcast([P, (b - a) * P])
                                  ).then_inc(sem(f"dst_row_landed{part}"), 16)

                def spread_rows(g, part):
                    a, b = PARTS[part]
                    eng.dma_start(v_rows[:, a:b, :], tiles(spread_v[0:E, :])[:, bass.ds(g * GRP + a, b - a), :]
                                  ).then_inc(sem(f"v_rows_landed{part}"), 16)

                for part in range(2):
                    edge_rows(0, part)
                    dst_rows(0, part)
                    load_keep(3, 0, part)
                eng.wait_ge(sem("v_spread"), 16 * NT)
                eng.wait_ge(sem("start_v_landed"), 16 * GRP)
                eng.dma_start(spread_v[0:E, :].rearrange("(j r p) d -> r j p d", j=GRP, p=P)[:, :, 0, :], start_v[:, :, :]
                              ).then_inc(sem("start_v_stored"), 16)
                eng.wait_ge(sem("start_v_stored"), 16)
                for part in range(2):
                    spread_rows(0, part)
                with nc.sync.Fori(0, GR - 1, 1) as g:
                    for part in range(2):
                        c = g * 2 + (part + 1)
                        eng.wait_ge(sem("e_turned"), c)
                        edge_rows(g + 1, part)
                        eng.wait_ge(sem("att_same_made"), c)
                        dst_rows(g + 1, part)
                        eng.wait_ge(sem("att_edges_mixed"), c)
                        spread_rows(g + 1, part)
                        eng.wait_ge(sem("att_max_scanned"), c)
                        load_keep(3, g + 1, part)

            def shift_counts():
                eng.wait_ge(sem("last_edge_ready"), 1)
                before_v = before_d.rearrange("(a n) -> a n", a=1)
                eng.dma_start(before_v[:, 0:1], zeros[0:1, 0:1]).then_inc(sem("before_stored"), 16)
                eng.dma_start(before_v[:, 1:N + 1].rearrange("a (i p) -> (a p) i", p=P), small[0:P, 7, :]).then_inc(sem("before_stored"), 16)
                eng.wait_ge(sem("before_stored"), 32)
                eng.dma_start(small[0:P, 6, :], before_v[:, 0:N].rearrange("a (i p) -> (a p) i", p=P)).then_inc(sem("before_landed"), 16)

            def store_table(k, ap_src):
                eng.wait_ge(sem(f"table_ready{k}"), 1)
                eng.dma_start(tiles(table[k]), ap_src).then_inc(sem(f"table_stored{k}"), 16)

            for k, w in ((0, D1), (1, D1), (2, D2)):
                store_table(k, own[:, :, 0:w])
                stream(k)
                if k == 0:
                    shift_counts()
            if last_layer >= 2:
                eng.wait_ge(sem("uv_ready"), 1)
                eng.dma_start(tiles(u_table), tmp[:, :, :]).then_inc(sem("uv_stored"), 16)
                eng.dma_start(tiles(v_table), tmp2n).then_inc(sem("uv_stored"), 16)
                attention_loads()
            if last_layer >= 3:
                store_table(4, x[:, :, :])
                stream(4)
            if last_layer >= 4:
                tab = table[5].rearrange("(r i p) d -> p i r d", p=P, r=NREL)
                for i in range(NT):
                    eng.wait_ge(sem("rel_rows_ready"), i + 1)
                    eng.dma_start(tab[:, i, :, :], rel_buf(arena)[:, i % SLOTS, :].rearrange("p (r d) -> p r d", r=NREL)
                                  ).then_inc(sem(f"rel_written{i % SLOTS}"), 16)
                for h in range(SLOTS):
                    eng.wait_ge(sem(f"rel_written{h}"), 16 * len(range(h, NT, SLOTS)))
                eng.sem_inc(sem("table_stored5"), 16)
                stream(5)
            eng.wait_ge(sem("out_ready"), 1)
            eng.dma_start(tiles(out), x[:, :, :]).then_inc(sem("out_stored"), 16)
            eng.wait_ge(sem("out_stored"), 16)

        @block.tensor
        def _(pe):
            count = {"groups": 0, "turned": 0}

            pe.wait_ge(sem("const_ready"), 1)
            for n in range(4):
                pe.wait_ge(sem("lists_float"), n + 1)
                for j in range(GRP):
                    ins = nc.tensor.transpose(bank(n, P, LB, j * LB), list_f(tmp, tmp2, n)[0:LB, j * P:(j + 1) * P], ident[0:LB, 0:LB])
                ins.then_inc(sem("lists_turned"), 1)
            pe.wait_ge(sem("block_rows_float"), 1)
            nc.tensor.matmul(bank(4, P, P), ones[0:1, 0:P], small_row(x6), start=True, stop=True).then_inc(sem("block_first_spread"), 1)

            def to_channels(src, d, ready, value=1):
                pe.wait_ge(sem(ready), value)
                for a in range(0, NT, 4):
                    n = count["turned"]
                    if n >= 2:
                        pe.wait_ge(sem("channels_copied"), n - 1)
                    for i in range(a, min(a + 4, NT)):
                        ins = nc.tensor.transpose(bank(n % 2, d, P, (i - a) * P), src[:, i, 0:d], ident[0:P, 0:P])
                    ins.then_inc(sem("channels_turned"), 1)
                    count["turned"] += 1
                return count["turned"]

            def node_product(w, width, k, per_bank):
                for j, a in enumerate(range(0, NT, per_bank)):
                    n = count["groups"]
                    if n >= 6:
                        pe.wait_ge(sem("products_taken"), n - 5)
                    pe.wait_ge(sem("channels_copied"), channels_needed(count["turned"], min(a + per_bank, NT) - 1))
                    for i in range(a, min(a + per_bank, NT)):
                        ins = nc.tensor.matmul(bank(2 + n % 6, P, width, (i - a) * width), xT[0:k, i * P:(i + 1) * P],
                                               w, start=True, stop=True)
                    ins.then_inc(sem("products_ready"), 1)
                    count["groups"] += 1

            def gcn_pass(k):
                d = WIDTH[k]
                base = ORDER[k] * GR

                def forward(g, part, first):
                    a, b = PARTS[part]
                    if not first:
                        pe.wait_ge(sem("scanned"), (g + (base - 1)) * 2 + (part + 1))
                    for i in range(a, b):
                        pe.wait_ge(sem("rows_weighted"), (g + base) * GRP + (i + 1))
                        if d < 128:
                            nc.tensor.nop(nofuse=True)
                        nc.tensor.transpose(bank(part, d, P, (i - a) * P), rows[:, i, 0:d], ident[0:P, 0:P]
                                            ).then_inc(sem("rows_turned"), 1)

                def back(g, part):
                    a, b = PARTS[part]
                    pe.wait_ge(sem("scanned"), (g + base) * 2 + (part + 1))
                    if d < 128:
                        nc.tensor.nop(nofuse=True)
                    for i in range(a, b):
                        ins = nc.tensor.transpose(bank(2 + part, P, d, (i - a) * d), run_s[0:d, i * P:(i + 1) * P], ident[0:d, 0:d])
                    ins.then_inc(sem("sums_turned"), 1)

                forward(0, 0, base == 0)
                forward(0, 1, base == 0)
                with nc.tensor.Fori(0, GR - 1, 1) as g:
                    for part in range(2):
                        pe.wait_ge(sem("rows_out_filled"), (g + base) * 2 + (part + 1))
                        back(g, part)
                        forward(g + 1, part, False)
                for part in range(2):
                    pe.wait_ge(sem("rows_out_filled"), (GR - 1 + base) * 2 + (part + 1))
                    back(GR - 1, part)

            def attention_pass():
                def forward(g, part, c):
                    a, b = PARTS[part]
                    n = (b - a) * P
                    later = c is not None and not isinstance(c, int)
                    pe.wait_ge(sem(f"e_rows_landed{part}"), (g + 1) * 16)
                    if c is not None:
                        pe.wait_ge(sem("att_e_copied"), c)
                    for i in range(a, b):
                        ins = nc.tensor.transpose(bank(0, D, P, (i - a) * P), e_rows[:, i, :], ident[0:P, 0:P])
                    ins.then_inc(sem("e_turned"), 1)
                    if c is not None:
                        pe.wait_ge(sem("att_u_copied"), c)
                    for i in range(a, b):
                        pe.wait_ge(sem(f"att_rows_landed{i}"), (g + 1) * 16)
                        ins = nc.tensor.transpose(bank(1, D, P, (i - a) * P), rows[:, i, :], ident[0:P, 0:P])
                    ins.then_inc(sem("att_u_turned"), 1)
                    if later:
                        pe.wait_ge(sem("att_logits_made"), (g - 1) * 2 + (part + 1))
                    pe.wait_ge(sem(f"v_rows_landed{part}"), (g + 1) * 16)
                    pe.wait_ge(sem("att_same_made"), g * 2 + (part + 1))
                    for i in range(a, b):
                        nc.tensor.matmul(bank(2 + part, D, P, (i - a) * P), v_rows[:, i, :], same[:, i * P:(i + 1) * P],
                                         start=(i == a), stop=False)
                    pe.wait_ge(sem("att_e_copied"), g * 2 + (part + 1))
                    nc.tensor.matmul(bank(2 + part, D, n), w_e3[:, :], eT[:, a * P:b * P], start=False, stop=True
                                     ).then_inc(sem("att_edges_mixed"), 1)

                def branch(g, part):
                    a, b = PARTS[part]
                    nc.tensor.matmul(bank(4 + part, D, (b - a) * P), w_e5[:, :], eT[:, a * P:b * P], start=True, stop=True
                                     ).then_inc(sem("att_x5_ready"), 1)

                def back(g, part):
                    a, b = PARTS[part]
                    pe.wait_ge(sem("att_scanned"), g * 2 + (part + 1))
                    pe.wait_ge(sem("att_rows_out_filled"), g * 2 + (part + 1))
                    for i in range(a, b):
                        nc.tensor.transpose(bank(6, P, D, (i - a) * 2 * D), run_n[:, i * P:(i + 1) * P], ident[:, :])
                        ins = nc.tensor.transpose(bank(6, P, D, (i - a) * 2 * D + D), run_s[:, i * P:(i + 1) * P], ident[:, :])
                    ins.then_inc(sem("att_sums_turned"), 1)

                for part in range(2):
                    forward(0, part, 1 if part else None)
                    branch(0, part)
                with nc.tensor.Fori(0, GR - 1, 1) as g:
                    for part in range(2):
                        forward(g + 1, part, g * 2 + (2 + part))
                        back(g, part)
                        branch(g + 1, part)
                for part in range(2):
                    back(GR - 1, part)

            pe.wait_ge(sem("x_landed"), 16)
            pe.wait_ge(sem("lists_copied"), 4)
            pe.wait_ge(sem("weights_landed"), 16 * WEIGHT_LOADS)
            to_channels(x, D, "x_landed", 16)
            node_product(w1[:, :], D1, D, BANK // D1)
            gcn_pass(0)
            gcn_pass(1)
            pe.wait_ge(sem("conv2_input"), 1)
            to_channels(tmp, D1, "conv2_input")
            node_product(w2[:, :], D2, D1, BANK // D2)
            pe.wait_ge(sem("table_ready2"), 1)
            gcn_pass(2)
            to_channels(tmp, D2, "conv3_input")
            node_product(w3[:, :], D, D2, BANK // D)
            if last_layer >= 2:
                to_channels(x, D, "x_new", 1)
                node_product(att_w[:, :, :].rearrange("p c d -> p (c d)"), 4 * D, D, 1)
                pe.wait_ge(sem("uv_ready"), 1)
                attention_pass()
                to_channels(tmp, D, "mlp_input")
                pe.wait_ge(sem("channels_copied"), count["turned"])
                hid = 0
                for a in range(0, NT, 4):
                    m = min(4, NT - a) * P
                    if a > 0:
                        pe.wait_ge(sem("hidden_made"), hid)
                    for h in range(HD // 128):
                        ins = nc.tensor.matmul(bank(h, 128, m), mlp1[:, h * 128:(h + 1) * 128], xT[:, a * P:a * P + m],
                                               start=True, stop=True)
                        ins.then_inc(sem("hidden_ready"), 1)
                        hid += 1
                    pe.wait_ge(sem("hidden_made"), hid)
                    n = count["groups"]
                    pe.wait_ge(sem("products_taken"), n - 5)
                    for i in range(a, min(a + 4, NT)):
                        for h in range(HD // 128):
                            ins = nc.tensor.matmul(bank(2 + n % 6, P, D, (i - a) * D), hidden(eT, uT, h)[:, (i - a) * P:(i - a + 1) * P],
                                                   mlp2[:, h, :], start=(h == 0), stop=(h == HD // 128 - 1))
                    ins.then_inc(sem("products_ready"), 1)
                    count["groups"] += 1
            if last_layer >= 3:
                pe.wait_ge(sem("table_ready4"), 1)
                gcn_pass(4)
                to_channels(tmp, D, "l2_input")
                for a in range(0, NT, 4):
                    m = min(4, NT - a) * P
                    pe.wait_ge(sem("channels_copied"), channels_needed(count["turned"], min(a + 4, NT) - 1))
                    n = count["groups"]
                    pe.wait_ge(sem("products_taken"), n - 5)
                    nc.tensor.matmul(bank(2 + n % 6, D, m), w_l2[:, :], xT[:, a * P:a * P + m],
                                     start=True, stop=True).then_inc(sem("products_ready"), 1)
                    count["groups"] += 1
                pe.wait_ge(sem("l2_normed"), 1)
                for a in range(0, NT, 4):
                    n = count["groups"]
                    pe.wait_ge(sem("products_taken"), n - 5)
                    for i in range(a, min(a + 4, NT)):
                        ins = nc.tensor.transpose(bank(2 + n % 6, P, D, (i - a) * D), tmp2[:, i * P:(i + 1) * P], ident[:, :])
                    ins.then_inc(sem("products_ready"), 1)
                    count["groups"] += 1
            if last_layer >= 4:
                to_channels(x, D, "x_new", 3)
                node_product(rel_w[:, :, :].rearrange("p r d -> p (r d)"), NREL * D, D, 1)
                pe.wait_ge(sem("rel_rows_ready"), NT)
                gcn_pass(5)

        @block.scalar
        def _(act):
            count = {"turned": 0, "groups": 0, "steps": 0}

            def done(ins):
                count["steps"] += 1
                ins.then_inc(sem("scalar_steps"), 1)
                act.wait_ge(sem("scalar_steps"), count["steps"])

            def copy_channels(d):
                for a in range(0, NT, 4):
                    n = count["turned"]
                    m = min(4, NT - a) * P
                    act.wait_ge(sem("channels_turned"), n + 1)
                    nc.scalar.activation(xT[0:d, a * P:a * P + m], bank(n % 2, d, m), ACT.Copy).then_inc(sem("channels_copied"), 1)
                    count["turned"] += 1

            def gcn_pass(k):
                d = WIDTH[k]
                base = ORDER[k] * GR

                def weigh(g, part):
                    a, b = PARTS[part]
                    for i in range(a, b):
                        act.wait_ge(sem(f"rows_landed{i}"), (g + (base + 1)) * 16)
                        nc.scalar.activation(rows[:, i, 0:d], rows[:, i, 0:d], ACT.Copy,
                                             scale=weightT[:, bass.ds(g * GRP + i, 1)]).then_inc(sem("rows_weighted"), 1)

                def empty(g, part):
                    a, b = PARTS[part]
                    act.wait_ge(sem("sums_turned"), (g + base) * 2 + (part + 1))
                    nc.scalar.activation(rows_out[:, a * d:b * d], bank(2 + part, P, (b - a) * d), ACT.Copy
                                         ).then_inc(sem("rows_out_filled"), 1)

                if base == 0:
                    act.sem_inc(sem("rows_out_free"), 1)
                    act.sem_inc(sem("rows_out_filled"), FREE)
                weigh(0, 0)
                weigh(0, 1)
                with nc.scalar.Fori(0, GR - 1, 1) as g:
                    act.wait_ge(sem("rows_out_free"), g + (base + 1))
                    for part in range(2):
                        empty(g, part)
                        weigh(g + 1, part)
                act.wait_ge(sem("rows_out_free"), GR + base)
                for part in range(2):
                    empty(GR - 1, part)

            def attention_pass():
                def forward(g, part):
                    a, b = PARTS[part]
                    n = (b - a) * P
                    cols = slice(a * P, b * P)
                    act.wait_ge(sem("e_turned"), g * 2 + (part + 1))
                    nc.scalar.activation(eT[:, cols], bank(0, D, n), ACT.Copy).then_inc(sem("att_e_copied"), 1)
                    act.wait_ge(sem("att_u_turned"), g * 2 + (part + 1))
                    nc.scalar.activation(uT[:, cols], bank(1, D, n), ACT.Copy).then_inc(sem("att_u_copied"), 1)

                def exps(g, part):
                    a, b = PARTS[part]
                    cols = slice(a * P, b * P)
                    c = g * 2 + part
                    act.wait_ge(sem("att_falls_made"), c + 1)
                    nc.scalar.activation(beta[:, cols], fall[:, cols], ACT.Relu)
                    nc.scalar.activation(alpha[:, cols], fall[:, cols], ACT.Relu, scale=-1.0).then_inc(sem("att_clipped"), 1)
                    act.wait_ge(sem("att_clipped"), c + 1)
                    nc.scalar.activation(beta[:, cols], beta[:, cols], ACT.Exp, scale=-1.0)
                    nc.scalar.activation(alpha[:, cols], alpha[:, cols], ACT.Exp, scale=-1.0).then_inc(sem("att_exps_made"), 1)

                sums_v = tiles(sums_d[3])

                def empty(g, part, first=False):
                    a, b = PARTS[part]
                    if not first:
                        act.wait_ge(sem(f"att_sums_written{part}"), g * 16)
                    act.wait_ge(sem("att_sums_turned"), g * 2 + (part + 1))
                    nc.scalar.activation(rows_out[:, a * 2 * D:b * 2 * D], bank(6, P, (b - a) * 2 * D), ACT.Copy
                                         ).then_inc(sem("att_rows_out_filled"), 1)
                    act.wait_ge(sem("att_rows_out_filled"), g * 2 + (part + 2))
                    act.dma_start(sums_v[:, bass.ds(g * GRP + a, b - a), :],
                                  rows_out[:, a * 2 * D:b * 2 * D].rearrange("p (b d) -> p b d", d=2 * D)
                                  ).then_inc(sem(f"att_sums_written{part}"), 16)

                def forward_later(g, part):
                    act.wait_ge(sem("att_logits_made"), (g - 1) * 2 + (part + 1))
                    act.wait_ge(sem("att_x5_ready"), (g - 1) * 2 + (part + 1))
                    forward(g, part)

                act.sem_inc(sem("att_rows_out_filled"), 1)
                forward(0, 0)
                forward(0, 1)
                exps(0, 0)

                def step(g, first):
                    forward_later(g + 1, 0)
                    exps(g, 1)
                    empty(g, 0, first)
                    forward_later(g + 1, 1)
                    exps(g + 1, 0)
                    empty(g, 1, first)
                step(0, True)
                with nc.scalar.Fori(1, GR - 1, 1) as g:
                    step(g, False)
                exps(GR - 1, 1)
                empty(GR - 1, 0)
                empty(GR - 1, 1)
                for part in range(2):
                    act.wait_ge(sem(f"att_sums_written{part}"), GR * 16)
                act.sem_inc(sem("sums_stored3"), 1)

            def norm_help(n):
                act.wait_ge(sem("norm_centred"), n + 1)
                nc.scalar.activation(tmp2n, tmp[:, :, :], ACT.Square).then_inc(sem("norm_squares"), 1)
                act.wait_ge(sem("norm_variance"), n + 1)
                nc.scalar.activation(small[0:P, 3, :], small[0:P, 2, :], ACT.Sqrt).then_inc(sem("norm_roots"), 1)

            copy_channels(D)
            act.wait_ge(sem("deg_clamped"), 1)
            nc.scalar.activation(small[0:P, 3, :], small[0:P, 2, :], ACT.Sqrt).then_inc(sem("deg_roots"), 1)
            gcn_pass(0)
            act.wait_ge(sem("elu_input"), 1)
            nc.scalar.activation(tmp2n[:, :, 0:D1], tmp2n[:, :, 0:D1], ACT.Exp).then_inc(sem("elu_exp"), 1)
            gcn_pass(1)
            copy_channels(D1)
            act.wait_ge(sem("elu_input"), 2)
            nc.scalar.activation(tmp2n[:, :, 0:D2], tmp2n[:, :, 0:D2], ACT.Exp).then_inc(sem("elu_exp"), 1)
            gcn_pass(2)
            copy_channels(D2)
            norm_help(0)
            if last_layer >= 2:
                copy_channels(D)
                for i in range(NT):
                    n = GROUPS_BEFORE_UV + i
                    act.wait_ge(sem("products_ready"), n + 1)
                    b = 2 + n % 6
                    nc.scalar.activation(tmp[:, i, :], bank(b, P, D), ACT.Copy)
                    nc.scalar.activation(tmp2n[:, i, :], bank(b, P, D, D), ACT.Copy)
                    nc.scalar.activation(k_node[:, i, :], bank(b, P, D, 2 * D), ACT.Copy)
                    nc.scalar.activation(x6[:, i, :], bank(b, P, D, 3 * D), ACT.Copy).then_inc(sem("products_taken"), 1)
                attention_pass()
                norm_help(1)
                copy_channels(D)
                hid = 0
                for a in range(0, NT, 4):
                    m = min(4, NT - a) * P
                    if a > 0:
                        act.wait_ge(sem("products_ready"), GROUPS_BEFORE_UV + NT + a // 4)
                    for h in range(HD // 128):
                        hid += 1
                        act.wait_ge(sem("hidden_ready"), hid)
                        nc.scalar.activation(hidden(eT, uT, h)[:, 0:m], bank(h, 128, m), ACT.Relu,
                                             bias=mlp_b1[:, h:h + 1]).then_inc(sem("hidden_made"), 1)
                norm_help(2)
                norm_help(3)
            if last_layer >= 3:
                gcn_pass(4)
                copy_channels(D)
                act.wait_ge(sem("l2_variance"), 1)
                nc.scalar.activation(small[:, 5, 0:1], small[:, 4, 0:1], ACT.Sqrt).then_inc(sem("l2_root"), 1)
                norm_help(4)
            if last_layer >= 4:
                copy_channels(D)
                gcn_pass(5)
                norm_help(5)

        @block.vector
        def _(dve):
            V = nc.vector
            count = {"steps": 0, "groups": 0, "norms": 0}

            def done(ins):
                count["steps"] += 1
                ins.then_inc(sem("vector_steps"), 1)
                dve.wait_ge(sem("vector_steps"), count["steps"])
                return ins

            own_f = own[:, :, :].rearrange("p i d -> p (i d)")
            own_i = own_f.bitcast(I32)

            dve.wait_ge(sem("edge_lists_landed"), 64)
            lists_i = tmp2[0:LB, :].bitcast(I32)
            for n in range(2):
                V.tensor_copy(list_f(tmp, tmp2, n)[0:LB, :], lists_i[:, n * GE:(n + 1) * GE]).then_inc(sem("lists_float"), 1)
            dve.wait_ge(sem("lists_float"), 1)
            V.scalar_tensor_tensor(list_f(tmp, tmp2, 2)[0:LB, :], lists_i[:, 2 * GE:3 * GE], float(N), list_f(tmp, tmp2, 0)[0:LB, :],
                                   ALU.mult, ALU.add).then_inc(sem("lists_float"), 1)
            V.tensor_copy(list_f(tmp, tmp2, 3)[0:LB, :], tmp2[0:LB, 3 * GE:4 * GE]).then_inc(sem("lists_float"), 1)
            dve.wait_ge(sem("blocks_landed"), 96)
            dve.wait_ge(sem("node_numbers"), 1)
            done(V.tensor_copy(node_id[:, :], block_row[:, :]))
            keep_f = own_f[:, 4 * BL:5 * BL]
            V.tensor_tensor(keep_f[:, 1:BL], own_i[:, 1:BL], own_i[:, 0:BL - 1], ALU.is_equal)
            V.tensor_tensor(keep_f[:, 0:1], own_i[:, 0:1], own_i[:, BL:BL + 1], ALU.is_equal)
            done(V.memset(small[:, 7, :], 0.0))
            done(V.tensor_copy(keep_f[0:1, 0:1], small[0:1, 7, 0:1]))
            done(V.tensor_copy(keep_blocks(own), keep_f))
            done(V.tensor_scalar(reset_blocks(own), keep_f, -NEG, NEG, ALU.mult, ALU.add))
            dve.sem_inc(sem("keep_ready"), 1)
            rr = own_i[0:1, 3 * BL:3 * BL + 3 * P].rearrange("a (c p) -> a c p", c=3)
            done(V.tensor_copy(small_row(x6), rr[:, 0, :]))
            dve.sem_inc(sem("block_rows_float"), 1)
            sumw = run_w(own)
            done(V.memset(own_f[:, 5 * BL:5 * BL + 1], 0.0))
            done(V.tensor_tensor_scan(sumw, keep_f, own_f[:, 2 * BL:3 * BL], 0.0, ALU.mult, ALU.add))
            dve.sem_inc(sem("block_sums_ready"), 1)
            for n, target in enumerate((srcT, dstT, relT, weightT)):
                dve.wait_ge(sem("lists_turned"), n + 1)
                if n in (0, 2):
                    V.tensor_copy(target[:, ET:ET + GRP], bank(n, P, GRP))
                V.tensor_copy(target[:, 0:ET], bank(n, P, ET)).then_inc(sem("lists_copied"), 1)
            dve.wait_ge(sem("block_first_spread"), 1)
            cmp = x6[:, :, 0:P]
            xfirst = small_bc(x6)
            bc_first = bank(4, P, P)
            done(V.tensor_tensor(cmp_buf(arena), bc_first[:, None, :].to_broadcast([P, NT, P]),
                                 node_id[:, :, None].to_broadcast([P, NT, P]), ALU.is_le))
            done(V.tensor_reduce(small[0:P, 4, :], cmp_buf(arena), AX.X, ALU.add))
            done(V.tensor_scalar(small[0:P, 4, :], small[0:P, 4, :], -1.0, 0.0, ALU.add, ALU.max))
            done(V.tensor_copy(block_row[:, :], small[0:P, 4, :]))
            dve.sem_inc(sem("block_row_ready"), 1)
            row = x6[0:1, 1:NT, :].rearrange("a i d -> a (i d)")
            firsts, lasts, link, whole, aa, bb, cc = (row[:, c * 128:c * 128 + P] for c in range(7))
            dve.wait_ge(sem("block_ends_landed"), 16)
            done(V.tensor_copy(firsts, rr[:, 0, :]))
            done(V.tensor_copy(lasts, rr[:, 1, :]))
            done(V.memset(row[:, 2 * 128:7 * 128], 0.0))
            done(V.tensor_tensor(link[:, 1:P], firsts[:, 1:P], lasts[:, 0:P - 1], ALU.is_equal))
            done(V.tensor_tensor(whole, firsts, lasts, ALU.is_equal))
            done(V.tensor_tensor(aa[:, 1:P], link[:, 1:P], whole[:, 0:P - 1], ALU.mult))
            done(V.tensor_tensor(bb[:, 1:P], link[:, 1:P], own_f[0:1, 3 * BL + 2 * P:3 * BL + 3 * P - 1], ALU.mult))
            done(V.tensor_tensor_scan(carry_row(own), aa, bb, 0.0, ALU.mult, ALU.add))
            dve.sem_inc(sem("carry_row_ready"), 1)
            dve.wait_ge(sem("carry_landed"), 16)
            done(V.tensor_copy(small[0:P, 5, 0:1], own_i[:, 0:1]))
            prefix = own_f[:, 2 * BL:3 * BL]
            done(V.tensor_scalar(prefix, own_i[:, 0:BL], small[0:P, 5, 0:1], small[0:P, 1, 0:1], ALU.is_equal, ALU.mult))
            done(V.tensor_tensor(sumw, sumw, prefix, ALU.add))
            dve.sem_inc(sem("degree_ready"), 1)
            dve.wait_ge(sem("block_landed"), 16 * NT)
            arena_i = arena[:, :].bitcast(I32)
            junk = tmp2[0:P, 0:BL]
            for i in range(NT):
                done(V.tensor_scalar(junk, arena_i[:, i * BL:(i + 1) * BL], node_id[:, i:i + 1], 0.0, ALU.is_le, ALU.add,
                                     accum_out=small[0:P, 5, i:i + 1]))
                done(V.tensor_scalar(junk, arena_i[:, i * BL:(i + 1) * BL], node_id[:, i:i + 1], 0.0, ALU.is_equal, ALU.add,
                                     accum_out=small[0:P, 6, i:i + 1]))
            done(V.tensor_scalar(occupied[:, :], small[0:P, 6, :], 1.0, None, ALU.min))
            done(V.scalar_tensor_tensor(small[0:P, 5, :], small[0:P, 4, :], float(BL), small[0:P, 5, :], ALU.mult, ALU.add))
            done(V.tensor_copy(small[0:P, 7, :], small[0:P, 5, :]))
            done(V.tensor_scalar(small[0:P, 5, :], small[0:P, 5, :], -1.0, 0.0, ALU.add, ALU.max))
            done(V.tensor_copy(last_edge[:, :], small[0:P, 5, :]))
            dve.sem_inc(sem("last_edge_ready"), 1)
            dve.wait_ge(sem("deg_landed"), 16 * NT)
            done(V.tensor_tensor(small[0:P, 0, :], small[0:P, 0, :], occupied[:, :], ALU.mult))
            done(V.tensor_scalar(small[0:P, 0, :], small[0:P, 0, :], 1.0, None, ALU.add))
            done(V.tensor_scalar(small[0:P, 2, :], small[0:P, 0, :], 1e-30, None, ALU.max))
            dve.sem_inc(sem("deg_clamped"), 1)
            dve.wait_ge(sem("deg_roots"), 1)
            done(V.reciprocal(small[0:P, 3, :], small[0:P, 3, :]))
            done(V.tensor_scalar(small[0:P, 0, :], small[0:P, 0, :], 0.0, None, ALU.is_gt))
            done(V.tensor_tensor(dinv[:, :], small[0:P, 0, :], small[0:P, 3, :], ALU.mult))

            def each(v, w):
                return v[:, :, None].to_broadcast([P, NT, w])

            def chan(r, n, w):
                return r[:, None, :].to_broadcast([P, n, w])

            def products(width, per_bank, take):
                for a in range(0, NT, per_bank):
                    n = count["groups"]
                    m = min(per_bank, NT - a)
                    dve.wait_ge(sem("products_ready"), n + 1)
                    ps = bank(2 + n % 6, P, m * width).rearrange("p (i d) -> p i d", d=width)
                    take(a, m, ps).then_inc(sem("products_taken"), 1)
                    count["groups"] += 1
                dve.wait_ge(sem("products_taken"), count["groups"])

            def gcn_pass(k):
                d = WIDTH[k]
                base = ORDER[k] * GR
                kbase = k * GR

                def stage(g, b):
                    V.tensor_copy(idx[:, b:b + 1], GCN[k][2][:, bass.ds(g * GRP + b, 1)]).then_inc(sem("idx_staged"), 1)

                def scan(g, part):
                    a, b = PARTS[part]
                    for i in range(a, b):
                        dve.wait_ge(sem(f"rows_landed{i}"), (g + (base + 1)) * 16)
                        stage(g + 1, i)
                    dve.wait_ge(sem(f"keep_landed{part}"), (g + (kbase + 1)) * 16)
                    dve.wait_ge(sem("rows_turned"), (g + base) * GRP + b)
                    before = run_s[0:d, a * P - 1:a * P] if part else run_s[0:d, GE - 1:GE]
                    V.tensor_tensor_scan(run_s[0:d, a * P:b * P], keep[0:d, a * P:b * P], bank(part, d, (b - a) * P),
                                         before, ALU.mult, ALU.add).then_inc(sem("scanned"), 1)

                for b in range(GRP):
                    stage(0, b)
                scan(0, 0)
                dve.wait_ge(sem("scanned"), base * 2 + 1)
                scan(0, 1)
                with V.Fori(1, GR, 1) as g:
                    for part in range(2):
                        dve.wait_ge(sem("scanned"), (g + base) * 2 + part)
                        dve.wait_ge(sem("sums_turned"), (g + (base - 1)) * 2 + (part + 1))
                        scan(g, part)

            def take_ends(k, w):
                dve.wait_ge(sem(f"ends_landed{k}"), 16 * NT)
                done(V.tensor_tensor(ends(w), ends(w), each(occupied, w), ALU.mult))

            def elu(dst_ap, src_ap, w, n):
                done(V.tensor_scalar(tmp2n[:, :, 0:w], src_ap, 0.0, None, ALU.min))
                dve.sem_inc(sem("elu_input"), 1)
                dve.wait_ge(sem("elu_exp"), n)
                done(V.tensor_scalar(src_ap, src_ap, 0.0, -1.0, ALU.max, ALU.add))
                done(V.tensor_tensor(dst_ap, src_ap, tmp2n[:, :, 0:w], ALU.add))

            def layer_norm(dst_ap, src_ap):
                n = count["norms"]
                done(V.tensor_reduce(small[0:P, 1, :], src_ap, AX.X, ALU.add))
                done(V.tensor_scalar(small[0:P, 1, :], small[0:P, 1, :], 1.0 / D, None, ALU.mult))
                done(V.tensor_tensor(tmp[:, :, :], src_ap, each(small[0:P, 1, :], D), ALU.subtract))
                dve.sem_inc(sem("norm_centred"), 1)
                dve.wait_ge(sem("norm_squares"), n + 1)
                done(V.tensor_reduce(small[0:P, 2, :], tmp2n, AX.X, ALU.add))
                done(V.tensor_scalar(small[0:P, 2, :], small[0:P, 2, :], 1.0 / D, EPS, ALU.mult, ALU.add))
                dve.sem_inc(sem("norm_variance"), 1)
                dve.wait_ge(sem("norm_roots"), n + 1)
                done(V.reciprocal(small[0:P, 3, :], small[0:P, 3, :]))
                done(V.tensor_tensor(dst_ap, tmp[:, :, :], each(small[0:P, 3, :], D), ALU.mult))
                count["norms"] += 1

            def find_first_edges():
                first = small[0:P, 6, :]
                dve.wait_ge(sem("before_landed"), 16)
                done(V.tensor_scalar(small[0:P, 5, :], node_id[:, :], float(E), None, ALU.add))
                done(V.tensor_tensor(first, first, small[0:P, 5, :], ALU.subtract))
                done(V.tensor_tensor(first, first, occupied[:, :], ALU.mult))
                done(V.tensor_tensor(first_edge[:, :], first, small[0:P, 5, :], ALU.add))
                dve.sem_inc(sem("first_edge_ready"), 1)

            dve.wait_ge(sem("deg_stored"), 16)
            products(D1, BANK // D1, lambda a, m, ps: V.tensor_tensor(
                own[:, a:a + m, 0:D1], ps, dinv[:, a:a + m, None].to_broadcast([P, m, D1]), ALU.mult))
            dve.sem_inc(sem("table_ready0"), 1)
            for k, w in ((0, D1), (1, D1), (2, D2)):
                gcn_pass(k)
                if k == 1:
                    find_first_edges()
                take_ends(k, w)
                done(V.tensor_tensor(tmp[:, :, 0:w], ends(w), own[:, :, 0:w], ALU.add))
                done(V.tensor_tensor(tmp[:, :, 0:w], tmp[:, :, 0:w], each(dinv, w), ALU.mult))
                if k == 0:
                    done(V.tensor_tensor(tmp[:, :, 0:w], tmp[:, :, 0:w], chan(row_of["L0_gnn_b1"], NT, w), ALU.add))
                    elu(tmp[:, :, 0:w], tmp[:, :, 0:w], w, 1)
                    done(V.tensor_tensor(own[:, :, 0:w], tmp[:, :, 0:w], each(dinv, w), ALU.mult))
                    dve.sem_inc(sem("table_ready1"), 1)
                elif k == 1:
                    dve.sem_inc(sem("conv2_input"), 1)
                    b2 = row_of["L0_gnn_b2"]
                    products(D2, BANK // D2, lambda a, m, ps: V.tensor_tensor(
                        own[:, a:a + m, 0:D2], ps, chan(b2, m, D2), ALU.add))
                    elu(own[:, :, 0:D2], own[:, :, 0:D2], D2, 2)
                    done(V.tensor_tensor(own[:, :, 0:D2], own[:, :, 0:D2], each(dinv, D2), ALU.mult))
                    dve.sem_inc(sem("table_ready2"), 1)
                else:
                    dve.sem_inc(sem("conv3_input"), 1)
                    done(V.tensor_tensor(x[:, :, :], x[:, :, :], chan(row_of["L0_gnn_b3"], NT, D), ALU.add))
                    products(D, BANK // D, lambda a, m, ps: V.tensor_tensor(
                        x[:, a:a + m, :], ps, x[:, a:a + m, :], ALU.add))
                    layer_norm(x[:, :, :], x[:, :, :])
                    dve.sem_inc(sem("x_new"), 1)

            def attention_pass():
                def first_half(g, part, first):
                    a, b = PARTS[part]
                    n = (b - a) * P
                    cols = slice(a * P, b * P)
                    c = g * 2 + part
                    dve.wait_ge(sem("att_edges_mixed"), c + 1)
                    dve.wait_ge(sem("att_u_copied"), c + 1)
                    V.tensor_tensor(logit[:, cols], bank(2 + part, D, n), uT[:, cols], ALU.mult
                                    ).then_inc(sem("att_logits_made"), 1)
                    if part == 0 and not first:
                        V.tensor_copy(run_m[:, 0:1], run_m[:, GE:GE + 1]).then_inc(sem("att_max_carried"), 1)
                        dve.wait_ge(sem("att_max_carried"), g)
                    dve.wait_ge(sem(f"keep_landed{part}"), (g + (3 * GR + 1)) * 16)
                    dve.wait_ge(sem("att_logits_made"), c + 1)
                    V.tensor_tensor_scan(run_m[:, 1 + a * P:1 + b * P], logit[:, cols], keep[:, cols],
                                         run_m[:, a * P:a * P + 1], ALU.max, ALU.add).then_inc(sem("att_max_scanned"), 1)
                    dve.wait_ge(sem("att_max_scanned"), c + 1)
                    if not first:
                        dve.wait_ge(sem("att_clipped"), c - 1)
                    V.tensor_tensor(fall[:, cols], run_m[:, a * P:b * P], logit[:, cols], ALU.subtract
                                    ).then_inc(sem("att_falls_made"), 1)

                def second_half(g, part, first):
                    a, b = PARTS[part]
                    n = (b - a) * P
                    cols = slice(a * P, b * P)
                    c = g * 2 + part
                    dve.wait_ge(sem("att_exps_made"), c + 1)
                    dve.wait_ge(sem("att_x5_ready"), c + 1)
                    if not first:
                        dve.wait_ge(sem("att_sums_turned"), (g - 1) * 2 + (part + 1))
                    V.tensor_tensor(betax[:, cols], beta[:, cols], bank(4 + part, D, n), ALU.mult
                                    ).then_inc(sem("att_betax_made"), 1)
                    at = a * P - 1 if part else GE - 1
                    V.tensor_tensor_scan(run_s[:, cols], alpha[:, cols], beta[:, cols], run_s[:, at:at + 1],
                                         ALU.mult, ALU.add)
                    dve.wait_ge(sem("att_betax_made"), c * 2 + 1)
                    V.scalar_tensor_tensor(betax[:, cols], betax[:, cols], SLOPE, betax[:, cols], ALU.mult, ALU.max
                                           ).then_inc(sem("att_betax_made"), 1)
                    dve.wait_ge(sem("att_betax_made"), c * 2 + 2)
                    V.tensor_tensor_scan(run_n[:, cols], alpha[:, cols], betax[:, cols], run_n[:, at:at + 1],
                                         ALU.mult, ALU.add).then_inc(sem("att_scanned"), 1)

                def compare(g, part):
                    a, b = PARTS[part]
                    dve.wait_ge(sem(f"dst_row_landed{part}"), (g + 1) * 16)
                    for i in range(a, b):
                        ins = V.tensor_scalar(same[:, i * P:(i + 1) * P], dst_row[:, i * P:(i + 1) * P],
                                              dstT[:, bass.ds(g * GRP + i, 1)], None, ALU.is_equal)
                    ins.then_inc(sem("att_same_made"), 1)

                compare(0, 0)
                compare(0, 1)
                first_half(0, 0, True)
                compare(1, 0)
                first_half(0, 1, True)
                second_half(0, 0, True)
                compare(1, 1)
                first_half(1, 0, False)
                second_half(0, 1, True)
                with V.Fori(1, GR - 1, 1) as g:
                    compare(g + 1, 0)
                    first_half(g, 1, False)
                    second_half(g, 0, False)
                    compare(g + 1, 1)
                    first_half(g + 1, 0, False)
                    second_half(g, 1, False)
                first_half(GR - 1, 1, False)
                second_half(GR - 1, 0, False)
                second_half(GR - 1, 1, False)

            def affine(v):
                done(V.tensor_tensor(v, v, chan(row_of["L1_gnn_gamma"], NT, D), ALU.mult))
                done(V.tensor_tensor(v, v, chan(row_of["L1_gnn_beta"], NT, D), ALU.add))

            if last_layer >= 2:
                count["groups"] += NT
                dve.wait_ge(sem("products_taken"), count["groups"])
                for v in (tmp[:, :, :], tmp2n, k_node):
                    done(V.scalar_tensor_tensor(v, v, SLOPE, v, ALU.mult, ALU.max))
                done(V.tensor_scalar(tmp[:, :, :], tmp[:, :, :], float(HEAD) ** -0.5, None, ALU.mult))
                dve.sem_inc(sem("uv_ready"), 1)
                dve.wait_ge(sem("uv_stored"), 32)
                attention_pass()
                dve.wait_ge(sem("ends_landed3"), 16 * NT)
                both = ends(2 * D)
                num, den = both[:, :, 0:D], both[:, :, D:2 * D]
                done(V.tensor_tensor(tmp[:, :, :], k_node, den, ALU.mult))
                done(V.tensor_tensor(tmp[:, :, :], tmp[:, :, :], num, ALU.add))
                done(V.tensor_scalar(den, den, 1e-20, None, ALU.add))
                done(V.reciprocal(den, den))
                done(V.tensor_tensor(tmp[:, :, :], tmp[:, :, :], den, ALU.mult))
                done(V.tensor_tensor(tmp[:, :, :], tmp[:, :, :], each(occupied, D), ALU.mult))
                done(V.tensor_tensor(x6[:, :, :], x6[:, :, :], tmp[:, :, :], ALU.add))
                layer_norm(tmp[:, :, :], x6[:, :, :])
                affine(tmp[:, :, :])
                dve.sem_inc(sem("mlp_input"), 1)
                done(V.tensor_tensor(x6[:, :, :], tmp[:, :, :], chan(row_of["L1_gnn_mlp_b2"], NT, D), ALU.add))
                products(D, 4, lambda a, m, ps: V.tensor_tensor(x6[:, a:a + m, :], ps, x6[:, a:a + m, :], ALU.add))
                layer_norm(x6[:, :, :], x6[:, :, :])
                affine(x6[:, :, :])
                done(V.tensor_tensor(x[:, :, :], x[:, :, :], x6[:, :, :], ALU.add))
                layer_norm(x[:, :, :], x[:, :, :])
                dve.sem_inc(sem("x_new"), 1)
            if last_layer >= 3:
                dve.sem_inc(sem("table_ready4"), 1)
                gcn_pass(4)
                dve.wait_ge(sem("ends_landed4"), 16 * NT)
                done(V.tensor_tensor(tmp[:, :, :], ends(D), each(occupied, D), ALU.mult))
                dve.sem_inc(sem("l2_input"), 1)
                h = tmp2[:, 0:N]
                col = lambda c: l2_cols[:, c:c + 1]
                for a in range(0, NT, 4):
                    n = count["groups"]
                    m = min(4, NT - a) * P
                    dve.wait_ge(sem("products_ready"), n + 1)
                    V.tensor_scalar(h[:, a * P:a * P + m], bank(2 + n % 6, D, m), col(0), None, ALU.add
                                    ).then_inc(sem("products_taken"), 1)
                    count["groups"] += 1
                dve.wait_ge(sem("products_taken"), count["groups"])

                def prelu(c):
                    done(V.tensor_scalar(arena_h(xT), h, 0.0, col(c), ALU.min, ALU.mult))
                    done(V.scalar_tensor_tensor(h, h, 0.0, arena_h(xT), ALU.max, ALU.add))
                prelu(3)
                s = small[:, 4, :]
                done(V.tensor_reduce(s[:, 1:2], h, AX.X, ALU.add))
                done(V.tensor_scalar(s[:, 1:2], s[:, 1:2], 1.0 / N, None, ALU.mult))
                done(V.tensor_scalar(h, h, s[:, 1:2], None, ALU.subtract))
                done(V.tensor_tensor(arena_h(xT), h, h, ALU.mult))
                done(V.tensor_reduce(s[:, 0:1], arena_h(xT), AX.X, ALU.add))
                done(V.tensor_scalar(s[:, 0:1], s[:, 0:1], 1.0 / N, EPS, ALU.mult, ALU.add))
                dve.sem_inc(sem("l2_variance"), 1)
                dve.wait_ge(sem("l2_root"), 1)
                done(V.reciprocal(s[:, 2:3], small[:, 5, 0:1]))
                done(V.tensor_tensor(s[:, 2:3], s[:, 2:3], col(1), ALU.mult))
                done(V.tensor_scalar(h, h, s[:, 2:3], col(2), ALU.mult, ALU.add))
                prelu(4)
                dve.sem_inc(sem("l2_normed"), 1)
                products(D, 4, lambda a, m, ps: V.tensor_tensor(x[:, a:a + m, :], ps, x[:, a:a + m, :], ALU.add))
                layer_norm(x[:, :, :], x[:, :, :])
                dve.sem_inc(sem("x_new"), 1)
            if last_layer >= 4:
                for i in range(NT):
                    n = count["groups"]
                    dve.wait_ge(sem("products_ready"), n + 1)
                    if i >= SLOTS:
                        dve.wait_ge(sem(f"rel_written{i % SLOTS}"), 16 * (i // SLOTS))
                    V.tensor_copy(rel_buf(arena)[:, i % SLOTS, :], bank(2 + n % 6, P, NREL * D)).then_inc(sem("products_taken"), 1)
                    count["groups"] += 1
                    dve.wait_ge(sem("products_taken"), count["groups"])
                    dve.sem_inc(sem("rel_rows_ready"), 1)
                gcn_pass(5)
                dve.wait_ge(sem("ends_landed5"), 16 * NT)
                done(V.tensor_tensor(ends(D), ends(D), each(occupied, D), ALU.mult))
                done(V.scalar_tensor_tensor(x[:, :, :], ends(D), 0.0, x[:, :, :], ALU.max, ALU.add))
                layer_norm(x[:, :, :], x[:, :, :])
            dve.sem_inc(sem("out_ready"), 1)


WEIGHT_LOADS = 25
SLOTS = 6
FREE = 2
GROUPS_BEFORE_UV = 2 + 4 + 7
BLK = 425


def flat(a):
    return a[:, :, :].rearrange("p i d -> p (i d)")


def keep_blocks(own):
    return flat(own)[:, 5 * BLK + 8:6 * BLK + 8].bitcast(BF16)[:, 0:BLK]


def reset_blocks(own):
    return flat(own)[:, 5 * BLK + 8:6 * BLK + 8].bitcast(BF16)[:, BLK:2 * BLK]


def run_w(own):
    return flat(own)[:, 6 * BLK + 16:7 * BLK + 16]


def carry_row(own):
    return flat(own)[0:1, 7 * BLK + 16:7 * BLK + 16 + P]


def small_row(x6):
    return flat(x6)[0:1, 0:P]


def small_bc(x6):
    return flat(x6)[:, 0:P]


def cmp_buf(arena):
    return arena[:, 0:25 * P].rearrange("p (i b) -> p i b", b=P)


def list_f(tmp, tmp2, n):
    return flat(tmp)[:, n * 625:(n + 1) * 625]


def hidden(a, b, h):
    return a if h == 0 else b


def arena_h(xT):
    return xT[:, :]


def rel_buf(arena):
    return arena[:, 0:SLOTS * 384].rearrange("p (s d) -> p s d", d=384)


def channels_needed(total, tile):
    return total - 7 + tile // 4 + 1


_INS = ['x', 'src', 'dst', 'edge_attr_128', 'edge_type_3', 'edge_weight', 'L0_gnn_W1', 'L0_gnn_b1', 'L0_gnn_W2',
        'L0_gnn_b2', 'L0_gnn_W3', 'L0_gnn_b3', 'L1_gnn_w1', 'L1_gnn_w2', 'L1_gnn_w3', 'L1_gnn_w4', 'L1_gnn_w5',
        'L1_gnn_w6', 'L1_gnn_mlp_w1', 'L1_gnn_mlp_b1', 'L1_gnn_mlp_w2', 'L1_gnn_mlp_b2', 'L1_gnn_gamma',
        'L1_gnn_beta', 'L2_gnn_W', 'L2_gnn_b', 'L2_gnn_a1', 'L2_gnn_gamma', 'L2_gnn_beta', 'L2_gnn_a2',
        'L3_gnn_weight']


def kernel(**inputs):
    import numpy as _np
    import concourse.bacc as _bacc
    from concourse import mybir as _mybir
    from concourse.bass_utils import run_bass_kernel_spmd as _run

    nc = _bacc.Bacc("TRN2", target_bir_lowering=False, num_devices=1)
    arrays, t = {}, {}
    for name in _INS:
        a = _np.ascontiguousarray(inputs[name])
        arrays["in_" + name] = a
        t[name] = nc.dram_tensor("in_" + name, a.shape, _mybir.dt.from_np(a.dtype), kind="ExternalInput").ap()
    out = nc.dram_tensor("out_0", t["x"].shape, _mybir.dt.float32, kind="ExternalOutput").ap()
    build(nc, t, out)
    r = _run(nc, [arrays], core_ids=[0])
    return r.results[0]["out_0"]
```

```python
import concourse.bass as bass
from concourse import mybir
from contextlib import ExitStack

FP32 = mybir.dt.float32
BF16 = mybir.dt.bfloat16
I32 = mybir.dt.int32
ALU = mybir.AluOpType
ACT = mybir.ActivationFunctionType
AX = mybir.AxisListType

P = 125
NCH = 5
LOT = 4
GRP = 5
CUT = 3
PARTS = ((0, CUT), (CUT, GRP))
BANK = 512
NEG = -1.0e38
EPS = 1e-5
SLOPE = 0.01
WEIGHT_LOADS = 25
FREE = 2


def build(nc, t, out):
    N, D = t["x"].shape
    E = t["src"].shape[0]
    NT = N // P
    ET = E // P
    GR = ET // GRP
    GE = GRP * P
    BL = E // P
    LB = ET // GRP
    assert N == NT * P and E == ET * P and ET == GR * GRP and D == 128
    D1 = t["L0_gnn_W1"].shape[1]
    D2 = t["L0_gnn_W2"].shape[1]
    HD = t["L1_gnn_mlp_w1"].shape[1]
    HL = HD // 128
    NREL = t["L3_gnn_weight"].shape[0]
    HEAD = 32
    LOTS = [(a, min(a + LOT, NT)) for a in range(0, NT, LOT)]
    NL = len(LOTS)
    ctx = ExitStack()
    with ctx:
        def sb(name, shape, dt=FP32):
            return ctx.enter_context(nc.sbuf_tensor(name, shape, dt))

        def dram(name, shape, dt=FP32):
            return nc.dram_tensor(name, shape, dt, kind="Internal").ap()

        sems = {}

        def sem(name):
            if name not in sems:
                sems[name] = ctx.enter_context(nc.semaphore(name))
            return sems[name]

        keep_d = dram("keep_d", (E,), BF16)
        reset_d = dram("reset_d", (E + 1,), BF16)
        deg_d = dram("deg_d", (E, 1))
        table = [dram("table1", (N, D1)), dram("table2", (N, D1)), dram("table3", (N, D2)), None,
                 dram("table5", (N, D)), dram("table6", (NREL * N, D))]
        u_table = dram("u_table", (N, D))
        v_table = dram("v_table", (N, D))
        spread_v = dram("spread_v", (E + N, D))
        before_d = dram("before_d", (N + 1,))
        WIDTH = [D1, D1, D2, 2 * D, D, D]
        sums_d = [dram(f"sums{k}", (E, w)) for k, w in enumerate(WIDTH)]

        ident = sb("ident", [128, 128])
        ones = sb("ones", [1, 128])
        srcT = sb("srcT", [P, ET + 2 * GRP], I32)
        dstT = sb("dstT", [P, ET])
        relT = sb("relT", [P, ET + 2 * GRP], I32)
        weightT = sb("weightT", [P, ET])
        node_id = sb("node_id", [P, NT])
        last_edge = sb("last_edge", [P, NT], I32)
        block_row = sb("block_row", [P, NT], I32)
        occupied = sb("occupied", [P, NT])
        dinv = sb("dinv", [P, NT])
        row_of = {n: sb(n + "_row", [P, t[n].shape[0]]) for n in
                  ("L0_gnn_b1", "L0_gnn_b2", "L0_gnn_b3", "L1_gnn_mlp_b2", "L1_gnn_gamma", "L1_gnn_beta")}
        w1 = sb("w1", [D, D1])
        w2 = sb("w2", [D1, D2])
        w3 = sb("w3", [D2, D])
        att_w = sb("att_w", [D, 4, D])
        w_e3 = sb("w_e3", [D, D])
        w_e5 = sb("w_e5", [D, D])
        mlp1 = sb("mlp1", [D, HD])
        mlp2 = sb("mlp2", [128, HL, D])
        mlp_b1 = sb("mlp_b1", [128, HL])
        w_l2 = sb("w_l2", [D, D])
        l2_cols = sb("l2_cols", [D, 5])
        l2_neg = sb("l2_neg", [D, 5])
        l2_fit = sb("l2_fit", [D, 4])
        rel_w = sb("rel_w", [D, NREL, D])

        x = sb("x", [P, NT, D])
        xT = sb("xT", [D, N])
        tmp = sb("tmp", [P, NT, D])
        tmp2 = sb("tmp2", [128, NT * D])
        own = sb("own", [P, NT, D])
        x6 = sb("x6", [P, NT, D])
        arena = sb("arena", [P, max(NT * BL, NT * 3 * D)])
        k_node = arena[:, 2 * NT * D:3 * NT * D].rearrange("p (i d) -> p i d", d=D)
        small = sb("small", [128, 8, NT])
        stats = sb("stats", [P, NT, 6])
        mean_var = sb("mean_var", [P, NT, 2])
        tmp2n = tmp2[0:P, :].rearrange("p (i d) -> p i d", d=D)

        def ends(d):
            return arena[:, 0:NT * d].rearrange("p (i d) -> p i d", d=d)

        rows = sb("rows", [P, 2 * GRP, D])
        v_rows = rows[:, GRP:2 * GRP, :]
        e_rows = sb("e_rows", [P, GRP, D])
        idx = sb("idx", [P, 2 * GRP], I32)
        dst_row = sb("dst_row", [P, GE], I32)
        same = sb("same", [P, GE])
        zeros = sb("zeros", [P, D])
        start_dst = sb("start_dst", [LB, GRP], I32)
        start_v = sb("start_v", [LB, GRP, D])
        first_edge = sb("first_edge", [P, NT], I32)
        keep = sb("keep", [128, GE], BF16)
        run_s = sb("run_s", [D, GE])
        run_n = sb("run_n", [D, GE])
        run_m = sb("run_m", [D, 1 + GE])
        logit = sb("logit", [D, GE])
        fall = sb("fall", [D, GE])
        alpha = sb("alpha", [D, GE])
        beta = sb("beta", [D, GE])
        betax = sb("betax", [D, GE])
        eT = sb("eT", [D, GE])
        uT = sb("uT", [D, GE])
        bent = sb("bent", [D, GE])
        rows_out = sb("rows_out", [P, GRP * 2 * D])
        PS = ctx.enter_context(nc.psum_tensor("PS", [128, 8 * BANK], FP32))

        above = (uT, eT)
        below = (bent, alpha)

        assert HL == 2
        hidden = (eT, uT)
        rel_rows = arena[:, 0:NT * NREL * D].rearrange("p (i d) -> p i d", d=NREL * D)
        own_words = own[:, :, :].rearrange("p i d -> p (i d)")
        flags = own_words[:, 5 * BL + 8:6 * BL + 8].bitcast(BF16)
        keep_blocks = flags[:, 0:BL]
        reset_blocks = flags[:, BL:2 * BL]
        run_w = own_words[:, 6 * BL + 16:7 * BL + 16]
        carry_row = own_words[0:1, 7 * BL + 16:7 * BL + 16 + P]
        first_row = x6[:, :, :].rearrange("p i d -> p (i d)")[0:1, 0:P]
        is_below = arena[:, 0:NT * P].rearrange("p (i b) -> p i b", b=P)

        def list_f(n):
            return tmp[:, :, :].rearrange("p i d -> p (i d)")[:, n * GE:(n + 1) * GE]

        def bank(b, p, n, at=0):
            return PS[0:p, b * BANK + at:b * BANK + at + n]

        def tiles(dr, p=P):
            return dr.rearrange("(i p) d -> p i d", p=p)

        ctx.enter_context(nc.allow_non_contiguous_dma(reason="index lists and columns of weights, once"))
        block = ctx.enter_context(nc.Block())

        GCN = {0: (D1, table[0], srcT), 1: (D1, table[1], srcT), 2: (D2, table[2], srcT),
               4: (D, table[4], srcT), 5: (D, table[5], relT)}
        ORDER = {0: 0, 1: 1, 2: 2, 4: 3, 5: 4}

        def in_pairs(eng, first, end, step):
            assert (end - first) % 2 == 0
            with eng.Fori(0, (end - first) // 2, 1) as h:
                for q in range(2):
                    step(h * 2 + (first + q), (first + q) % 2, h + (first + q) // 2)

        def half_base(k, parity):
            return ORDER[k] * ((GR + 1 - parity) // 2)

        @block.gpsimd
        def _(eng):
            nc.gpsimd.memset(ident[:, :], 0.0).then_inc(sem("ident_cleared"), 1)
            nc.gpsimd.memset(ones[:, :], 1.0)
            nc.gpsimd.memset(zeros[:, :], 0.0)
            nc.gpsimd.memset(run_s[:, :], 0.0)
            nc.gpsimd.memset(run_n[:, :], 0.0)
            nc.gpsimd.memset(run_m[:, :], NEG)
            nc.gpsimd.iota(block_row[:, :], [[P, NT]], base=0, channel_multiplier=1).then_inc(sem("node_numbers"), 1)
            eng.wait_ge(sem("ident_cleared"), 1)
            nc.gpsimd.affine_select(out=ident[:, :], in_=ident[:, :], compare_op=ALU.not_equal, fill=1.0,
                                    base=0, pattern=[[-1, 128]], channel_multiplier=1).then_inc(sem("const_ready"), 1)

            eng.wait_ge(sem("block_row_ready"), 1)
            dst_blocks = t["dst"].rearrange("(b l) -> b l", l=BL)
            arena_i = arena[:, :].bitcast(I32)
            for i in range(NT):
                eng.indirect_dma_start(out=arena_i[:, i * BL:(i + 1) * BL], out_offset=None, in_=dst_blocks,
                                       in_offset=bass.IndirectOffsetOnAxis(ap=block_row[:, i:i + 1], axis=0)
                                       ).then_inc(sem(f"block_landed{i // NCH}"), 16)
            eng.wait_ge(sem("deg_stored"), 16)
            for i in range(NT):
                if i % NCH == 0:
                    eng.wait_ge(sem("last_edge_ready"), i // NCH + 1)
                eng.indirect_dma_start(out=small[0:P, 0, i:i + 1], out_offset=None, in_=deg_d,
                                       in_offset=bass.IndirectOffsetOnAxis(ap=last_edge[:, i:i + 1], axis=0)
                                       ).then_inc(sem("deg_landed"), 16)

            def gather(dst_ap, tab, index):
                return eng.indirect_dma_start(out=dst_ap, out_offset=None, in_=tab,
                                              in_offset=bass.IndirectOffsetOnAxis(ap=index, axis=0))

            def gather_pass(k):
                d, tab, index = GCN[k]
                base = ORDER[k] * GR
                staged = ORDER[k] * (GR + 2) * GRP
                eng.wait_ge(sem(f"table_stored{k}"), 16 * (1 if k < 3 else NL))

                def fetch(par, b):
                    at = par * GRP + b
                    gather(rows[:, at, 0:d], tab, idx[:, at:at + 1]).then_inc(sem(f"rows_landed{at}"), 16)

                def group(g, par, _):
                    for b in range(GRP):
                        eng.wait_ge(sem("idx_staged"), g * GRP + (staged + b + 1))
                        nc.gpsimd.nop(nofuse=True)
                        eng.wait_ge(sem("rows_turned"), (g + (base - 2)) * GRP + (b + 1))
                        nc.gpsimd.nop(nofuse=True)
                        fetch(par, b)

                for g in range(2):
                    for b in range(GRP):
                        eng.wait_ge(sem("idx_staged"), staged + g * GRP + b + 1)
                        if base:
                            eng.wait_ge(sem("rows_turned"), base * GRP)
                        fetch(g, b)
                in_pairs(nc.gpsimd, 2, GR - 1, group)
                group(GR - 1, (GR - 1) % 2, None)

            def fetch_ends(k):
                w = WIDTH[k]
                eng.wait_ge(sem(f"sums_stored{k}"), 1)
                for i in range(NT):
                    gather(arena[:, i * w:(i + 1) * w], sums_d[k], last_edge[:, i:i + 1]).then_inc(sem(f"ends_landed{i // LOT}"), 16)

            def attention_pass():
                eng.wait_ge(sem("first_edge_ready"), 1)
                eng.wait_ge(sem("spread_zeroed"), 16 * GR)
                for i in range(NT):
                    if i % LOT == 0:
                        eng.wait_ge(sem("uv_ready"), i // LOT + 1)
                    eng.indirect_dma_start(out=spread_v, out_offset=bass.IndirectOffsetOnAxis(ap=first_edge[:, i:i + 1], axis=0),
                                           in_=tmp2n[:, i, :], in_offset=None).then_inc(sem("v_spread"), 16)
                eng.wait_ge(sem("start_dst_landed"), 16)
                eng.wait_ge(sem("uv_stored"), 32 * NL)
                for j in range(GRP):
                    gather(start_v[:, j, :], v_table, start_dst[:, j:j + 1]).then_inc(sem("start_v_landed"), 16)

                def part_gathers(g, part, first):
                    a, b = PARTS[part]
                    if not first:
                        eng.wait_ge(sem("att_u_turned"), (g - 1) * 2 + (part + 1))
                    nc.gpsimd.tensor_copy(idx[:, a:b], srcT[:, bass.ds(g * GRP + a, b - a)]).then_inc(sem("att_idx_staged"), 1)
                    eng.wait_ge(sem("att_idx_staged"), g * 2 + (part + 1))
                    nc.gpsimd.nop(nofuse=True)
                    for i in range(a, b):
                        gather(rows[:, i, :], u_table, idx[:, i:i + 1]).then_inc(sem(f"att_rows_landed{i}"), 16)
                for part in range(2):
                    part_gathers(0, part, True)
                with nc.gpsimd.Fori(1, GR, 1) as g:
                    for part in range(2):
                        part_gathers(g, part, False)

            for k in range(3):
                gather_pass(k)
                fetch_ends(k)
            attention_pass()
            fetch_ends(3)
            for k in (4, 5):
                gather_pass(k)
                fetch_ends(k)

        @block.sync
        def _(eng):
            arrive = sem("edge_lists_landed")
            for n, name in enumerate(("src", "dst", "edge_type_3", "edge_weight")):
                view = (tmp2[0:LB, n * GE:(n + 1) * GE])
                if name != "edge_weight":
                    view = view.bitcast(I32)
                eng.dma_start(view.rearrange("r (j p) -> r j p", j=GRP),
                              t[name].rearrange("(j r p) -> r j p", j=GRP, p=P)).then_inc(arrive, 16)
            blk = sem("blocks_landed")
            own_i = own[:, :, :].rearrange("p i d -> p (i d)").bitcast(I32)
            eng.dma_start(own_i[:, 0:BL], t["dst"].rearrange("(p l) -> p l", l=BL)).then_inc(blk, 16)
            eng.dma_start(own_i[1:P, BL:BL + 1], t["dst"].rearrange("(p l) -> p l", l=BL)[0:P - 1, BL - 1:BL]).then_inc(blk, 16)
            eng.dma_start(own_i[0:1, BL:BL + 1], t["dst"].rearrange("(a n) -> a n", a=1)[:, 0:1]).then_inc(blk, 16)
            eng.dma_start(own[:, :, :].rearrange("p i d -> p (i d)")[:, 2 * BL:3 * BL],
                          t["edge_weight"].rearrange("(p l) -> p l", l=BL)).then_inc(blk, 16)
            own_r = own_i[0:1, 3 * BL:3 * BL + 3 * P].rearrange("a (c p) -> a c p", c=3)
            for c, at in ((0, 0), (1, BL - 1)):
                eng.dma_start(own_r[:, c, :], t["dst"].rearrange("(a p l) -> a p l", a=1, l=BL)[:, :, at]).then_inc(blk, 16)
            eng.dma_start(x[:, :, :], tiles(t["x"])).then_inc(sem("x_landed"), 16)
            eng.dma_start(start_dst[:, :], t["dst"].rearrange("(j r p) -> r j p", j=GRP, p=P)[:, :, 0]).then_inc(sem("start_dst_landed"), 16)
            wl = sem("weights_landed")
            loads = [(w1[:, :], t["L0_gnn_W1"]), (w2[:, :], t["L0_gnn_W2"]), (w3[:, :], t["L0_gnn_W3"])]
            for c, n in enumerate(("w1", "w2", "w4", "w6")):
                loads.append((att_w[:, c, :], t["L1_gnn_" + n]))
            loads += [(w_e3[:, :], t["L1_gnn_w3"]), (w_e5[:, :], t["L1_gnn_w5"]), (mlp1[:, :], t["L1_gnn_mlp_w1"]),
                      (mlp2[:, :, :], t["L1_gnn_mlp_w2"].rearrange("(c p) d -> p c d", p=128)),
                      (mlp_b1[:, :], t["L1_gnn_mlp_b1"].rearrange("(c p) -> p c", p=128)),
                      (w_l2[:, :], t["L2_gnn_W"]),
                      (rel_w[:, :, :], t["L3_gnn_weight"].rearrange("r i o -> i r o"))]
            for c, n in enumerate(("b", "gamma", "beta")):
                loads.append((l2_cols[:, c:c + 1], t["L2_gnn_" + n].rearrange("(p a) -> p a", a=1)))
            for c, n in enumerate(("a1", "a2")):
                loads.append((l2_cols[:, 3 + c:4 + c], t["L2_gnn_" + n].rearrange("(a n) -> a n", a=1).to_broadcast([D, 1])))
            for n, r in row_of.items():
                loads.append((r[:, :], t[n].rearrange("(a n) -> a n", a=1).to_broadcast([P, t[n].shape[0]])))
            assert len(loads) == WEIGHT_LOADS
            for dst_ap, src_ap in loads:
                eng.dma_start(dst_ap, src_ap).then_inc(wl, 16)

            eng.wait_ge(sem("keep_ready"), 1)
            eng.dma_start(keep_d.rearrange("(p l) -> p l", l=BL), keep_blocks).then_inc(sem("keep_stored"), 16)
            reset_v = reset_d.rearrange("(a n) -> a n", a=1)
            eng.dma_start(reset_v[:, 0:E].rearrange("a (p l) -> (a p) l", l=BL), reset_blocks).then_inc(sem("keep_stored"), 16)
            eng.dma_start(reset_v[:, E:E + 1], reset_blocks[0:1, 0:1]).then_inc(sem("keep_stored"), 16)
            eng.wait_ge(sem("block_sums_ready"), 1)
            own_rf = own[0:1, :, :].rearrange("a i d -> a (i d)")
            eng.dma_start(own_rf[:, 3 * BL + 2 * P:3 * BL + 3 * P], run_w[:, BL - 1:BL]).then_inc(sem("block_ends_landed"), 16)
            eng.wait_ge(sem("carry_row_ready"), 1)
            eng.dma_start(small[0:P, 1, 0:1], carry_row).then_inc(sem("carry_landed"), 16)
            eng.wait_ge(sem("degree_ready"), 1)
            eng.dma_start(deg_d.rearrange("(p l) a -> p (l a)", l=BL), run_w).then_inc(sem("deg_stored"), 16)
            eng.wait_ge(sem("keep_stored"), 48)

            def load_keep(k, g, part):
                a, b = PARTS[part]
                if k == 3:
                    src_ap = reset_v[:, bass.ds(g * GE + (a * P + 1), (b - a) * P)]
                else:
                    src_ap = keep_d.rearrange("(a n) -> a n", a=1)[:, bass.ds(g * GE + a * P, (b - a) * P)]
                eng.dma_start(keep[:, a * P:b * P], src_ap.to_broadcast([128, (b - a) * P])).then_inc(sem(f"keep_landed{part}"), 16)

            def stream(k):
                d = WIDTH[k]
                out_v = sums_d[k].rearrange("(i p) d -> p i d", p=P)
                base = ORDER[k] * GR

                def store(g, par):
                    eng.wait_ge(sem("rows_out_filled"), (g + base) * 2 + (2 + FREE))
                    eng.dma_start(out_v[:, bass.ds(g * GRP, GRP), :],
                                  rows_out[:, par * GRP * D:par * GRP * D + GRP * d].rearrange("p (b d) -> p b d", d=d)
                                  ).then_inc(sem(f"sums_written{par}"), 16)

                for part in range(2):
                    load_keep(k, 0, part)
                def clear(g):
                    eng.dma_start(tiles(spread_v[0:E, :])[:, bass.ds(g * GRP, GRP), :],
                                  zeros[:, None, :].to_broadcast([P, GRP, D])).then_inc(sem("spread_zeroed"), 16)

                def step(g, par, _):
                    if k == 0:
                        clear(g)
                    for part in range(2):
                        eng.wait_ge(sem("scanned"), (g + base) * 2 + (part + 1))
                        load_keep(k, g + 1, part)
                    store(g, par)
                in_pairs(nc.sync, 0, GR - 1, step)
                if k == 0:
                    clear(GR - 1)
                store(GR - 1, (GR - 1) % 2)
                for par in range(2):
                    eng.wait_ge(sem(f"sums_written{par}"), (half_base(k, par) + 1 + (GR + 1 - par) // 2) * 16)
                eng.sem_inc(sem(f"sums_stored{k}"), 1)

            def attention_loads():
                def edge_rows(g, part):
                    a, b = PARTS[part]
                    eng.dma_start(e_rows[:, a:b, :], tiles(t["edge_attr_128"])[:, bass.ds(g * GRP + a, b - a), :]
                                  ).then_inc(sem(f"e_rows_landed{part}"), 16)

                def dst_rows(g, part, first=False):
                    a, b = PARTS[part]
                    if not first:
                        eng.wait_ge(sem("att_same_made"), (g - 1) * 2 + (part + 1))
                    src_ap = t["dst"].rearrange("(a n) -> a n", a=1)[:, bass.ds(g * GE + a * P, (b - a) * P)]
                    eng.dma_start(dst_row[:, a * P:b * P], src_ap.to_broadcast([P, (b - a) * P])
                                  ).then_inc(sem(f"dst_row_landed{part}"), 16)

                def spread_rows(g, part):
                    a, b = PARTS[part]
                    eng.dma_start(v_rows[:, a:b, :], tiles(spread_v[0:E, :])[:, bass.ds(g * GRP + a, b - a), :]
                                  ).then_inc(sem(f"v_rows_landed{part}"), 16)

                for part in range(2):
                    edge_rows(0, part)
                    dst_rows(0, part, True)
                    load_keep(3, 0, part)
                eng.wait_ge(sem("v_spread"), 16 * NT)
                eng.wait_ge(sem("start_v_landed"), 16 * GRP)
                eng.dma_start(spread_v[0:E, :].rearrange("(j r p) d -> r j p d", j=GRP, p=P)[:, :, 0, :], start_v[:, :, :]
                              ).then_inc(sem("start_v_stored"), 16)
                eng.wait_ge(sem("start_v_stored"), 16)
                for part in range(2):
                    spread_rows(0, part)
                dst_rows(1, 0)

                def sums_out(g, part):
                    a, b = PARTS[part]
                    eng.wait_ge(sem("att_rows_out_filled"), g * 2 + (part + 2))
                    eng.dma_start(tiles(sums_d[3])[:, bass.ds(g * GRP + a, b - a), :],
                                  rows_out[:, a * 2 * D:b * 2 * D].rearrange("p (b d) -> p b d", d=2 * D)
                                  ).then_inc(sem(f"att_sums_written{part}"), 16)

                def step(g, first, last):
                    for part in range(2):
                        c = g * 2 + (part + 1)
                        eng.wait_ge(sem("e_turned"), c)
                        edge_rows(g + 1, part)
                        eng.wait_ge(sem("att_edges_mixed"), c)
                        spread_rows(g + 1, part)
                        if part == 0:
                            dst_rows(g + 1, 1)
                        elif not last:
                            dst_rows(g + 2, 0)
                        eng.wait_ge(sem("att_max_scanned"), c)
                        load_keep(3, g + 1, part)
                        if not first:
                            sums_out(g - 1, part)
                step(0, True, False)
                with nc.sync.Fori(1, GR - 2, 1) as g:
                    step(g, False, False)
                step(GR - 2, False, True)
                for g in (GR - 2, GR - 1):
                    for part in range(2):
                        sums_out(g, part)
                for part in range(2):
                    eng.wait_ge(sem(f"att_sums_written{part}"), GR * 16)
                eng.sem_inc(sem("sums_stored3"), 1)

            def shift_counts():
                eng.wait_ge(sem("last_edge_ready"), NT // NCH)
                before_v = before_d.rearrange("(a n) -> a n", a=1)
                eng.dma_start(before_v[:, 0:1], zeros[0:1, 0:1]).then_inc(sem("before_stored"), 16)
                eng.dma_start(before_v[:, 1:N + 1].rearrange("a (i p) -> (a p) i", p=P), small[0:P, 7, :]).then_inc(sem("before_stored"), 16)
                eng.wait_ge(sem("before_stored"), 32)
                eng.dma_start(small[0:P, 6, :], before_v[:, 0:N].rearrange("a (i p) -> (a p) i", p=P)).then_inc(sem("before_landed"), 16)

            def store_table(k, ap_src):
                eng.wait_ge(sem(f"table_ready{k}"), 1)
                eng.dma_start(tiles(table[k]), ap_src).then_inc(sem(f"table_stored{k}"), 16)

            for k, w in ((0, D1), (1, D1), (2, D2)):
                store_table(k, own[:, :, 0:w])
                stream(k)
                if k == 0:
                    shift_counts()
            for c, (a, b) in enumerate(LOTS):
                eng.wait_ge(sem("uv_ready"), c + 1)
                eng.dma_start(tiles(u_table)[:, a:b, :], tmp[:, a:b, :]).then_inc(sem("uv_stored"), 16)
                eng.dma_start(tiles(v_table)[:, a:b, :], tmp2n[:, a:b, :]).then_inc(sem("uv_stored"), 16)
            attention_loads()
            for c, (a, b) in enumerate(LOTS):
                eng.wait_ge(sem("x_new"), NL + c + 1)
                eng.dma_start(tiles(table[4])[:, a:b, :], x[:, a:b, :]).then_inc(sem("table_stored4"), 16)
            stream(4)
            rel_tiles = table[5].rearrange("(r i p) d -> p i r d", p=P, r=NREL)
            for a, b in LOTS:
                eng.wait_ge(sem("rel_rows_ready"), b)
                for i in range(a, b):
                    eng.dma_start(rel_tiles[:, i, :, :], rel_rows[:, i, :].rearrange("p (r d) -> p r d", r=NREL)
                                  ).then_inc(sem("rel_written"), 16)
            eng.wait_ge(sem("rel_written"), 16 * NT)
            eng.sem_inc(sem("table_stored5"), 16 * NL)
            stream(5)
            for c, (a, b) in enumerate(LOTS):
                eng.wait_ge(sem("out_ready"), c + 1)
                eng.dma_start(tiles(out)[:, a:b, :], x[:, a:b, :]).then_inc(sem("out_stored"), 16)
            eng.wait_ge(sem("out_stored"), 16 * NL)

        @block.tensor
        def _(pe):
            count = {"groups": 0, "turned": 0}
            takers = []

            def product_bank(taker="products_taken"):
                n = count["groups"]
                if n >= 6:
                    pe.wait_ge(sem(takers[n - 6][0]), takers[n - 6][1])
                takers.append((taker, 1 + sum(name == taker for name, _ in takers)))
                count["groups"] += 1
                return 2 + n % 6

            pe.wait_ge(sem("const_ready"), 1)
            for n in range(4):
                pe.wait_ge(sem("lists_float"), n + 1)
                for j in range(GRP):
                    ins = nc.tensor.transpose(bank(n, P, LB, j * LB), list_f(n)[0:LB, j * P:(j + 1) * P], ident[0:LB, 0:LB])
                ins.then_inc(sem("lists_turned"), 1)
            pe.wait_ge(sem("block_rows_float"), 1)
            nc.tensor.matmul(bank(4, P, P), ones[0:1, 0:P], first_row, start=True, stop=True).then_inc(sem("block_first_spread"), 1)

            def turn(lot, src, d):
                n = count["turned"]
                if n >= 2:
                    pe.wait_ge(sem("channels_copied"), n - 1)
                for i in range(*lot):
                    ins = nc.tensor.transpose(bank(n % 2, d, P, (i - lot[0]) * P), src[:, i, 0:d], ident[0:P, 0:P])
                ins.then_inc(sem("channels_turned"), 1)
                count["turned"] += 1

            def product(lot, w, width, k, per_bank, turned, taker):
                pe.wait_ge(sem("channels_copied"), turned)
                for a in range(lot[0], lot[1], per_bank):
                    at = product_bank(taker)
                    for i in range(a, min(a + per_bank, lot[1])):
                        ins = nc.tensor.matmul(bank(at, P, width, (i - a) * width), xT[0:k, i * P:(i + 1) * P],
                                               w, start=True, stop=True)
                    ins.then_inc(sem("products_ready"), 1)

            def node_stage(src, d, ready, before, w, width, per_bank, taker="products_taken"):
                for c, lot in enumerate(LOTS):
                    if ready == "x_landed":
                        pe.wait_ge(sem("x_landed"), 16)
                    else:
                        pe.wait_ge(sem(ready), before + c + 1)
                    turn(lot, src, d)
                    if c:
                        product(LOTS[c - 1], w, width, d, per_bank, count["turned"] - 1, taker)
                product(LOTS[-1], w, width, d, per_bank, count["turned"], taker)

            def gcn_pass(k):
                d = WIDTH[k]
                base = ORDER[k] * GR

                def forward(g, par, part, first):
                    a, b = PARTS[part]
                    if not first:
                        pe.wait_ge(sem("scanned"), (g + (base - 1)) * 2 + (part + 1))
                    for i in range(a, b):
                        pe.wait_ge(sem("rows_weighted"), (g + base) * GRP + (i + 1))
                        if d < 128:
                            nc.tensor.nop(nofuse=True)
                        nc.tensor.transpose(bank(part, d, P, (i - a) * P), rows[:, par * GRP + i, 0:d], ident[0:P, 0:P]
                                            ).then_inc(sem("rows_turned"), 1)

                def back(g, part):
                    a, b = PARTS[part]
                    pe.wait_ge(sem("rows_out_filled"), (g + base) * 2 + (part + 1))
                    pe.wait_ge(sem("scanned"), (g + base) * 2 + (part + 1))
                    if d < 128:
                        nc.tensor.nop(nofuse=True)
                    for i in range(a, b):
                        ins = nc.tensor.transpose(bank(2 + part, P, d, (i - a) * d), run_s[0:d, i * P:(i + 1) * P], ident[0:d, 0:d])
                    ins.then_inc(sem("sums_turned"), 1)

                def step(g, par, _):
                    for part in range(2):
                        back(g, part)
                        forward(g + 1, 1 - par, part, False)

                forward(0, 0, 0, base == 0)
                forward(0, 0, 1, base == 0)
                in_pairs(nc.tensor, 0, GR - 1, step)
                back(GR - 1, 0)
                back(GR - 1, 1)

            def attention_pass():
                def turn_edges(g, part, first=False):
                    a, b = PARTS[part]
                    pe.wait_ge(sem(f"e_rows_landed{part}"), (g + 1) * 16)
                    if not first:
                        pe.wait_ge(sem("att_e_copied"), g * 2 + part)
                    for i in range(a, b):
                        ins = nc.tensor.transpose(bank(0, D, P, (i - a) * P), e_rows[:, i, :], ident[0:P, 0:P])
                    ins.then_inc(sem("e_turned"), 1)

                def mix(g, part, first=False):
                    a, b = PARTS[part]
                    n = (b - a) * P
                    if not (first and part == 0):
                        pe.wait_ge(sem("att_u_copied"), g * 2 + part)
                    for i in range(a, b):
                        pe.wait_ge(sem(f"att_rows_landed{i}"), (g + 1) * 16)
                        ins = nc.tensor.transpose(bank(1, D, P, (i - a) * P), rows[:, i, :], ident[0:P, 0:P])
                    ins.then_inc(sem("att_u_turned"), 1)
                    if not first:
                        pe.wait_ge(sem("att_logits_made"), (g - 1) * 2 + (part + 1))
                    pe.wait_ge(sem(f"v_rows_landed{part}"), (g + 1) * 16)
                    pe.wait_ge(sem("att_same_made"), g * 2 + (part + 1))
                    for i in range(a, b):
                        nc.tensor.matmul(bank(2 + part, D, P, (i - a) * P), v_rows[:, i, :], same[:, i * P:(i + 1) * P],
                                         start=(i == a), stop=False)
                    pe.wait_ge(sem("att_e_copied"), g * 2 + (part + 1))
                    nc.tensor.matmul(bank(2 + part, D, n), w_e3[:, :], eT[:, a * P:b * P], start=False, stop=True
                                     ).then_inc(sem("att_edges_mixed"), 1)

                def branch(g, part, first=False):
                    a, b = PARTS[part]
                    if not first:
                        pe.wait_ge(sem("att_betax_made"), (g - 1) * 2 + (part + 1))
                    nc.tensor.matmul(bank(4 + part, D, (b - a) * P), w_e5[:, :], eT[:, a * P:b * P], start=True, stop=True
                                     ).then_inc(sem("att_x5_ready"), 1)

                def bend(g, part):
                    a, b = PARTS[part]
                    pe.wait_ge(sem("att_bent"), g * 2 + (part + 1))
                    nc.tensor.matmul(bank(4 + part, D, (b - a) * P), ident[:, :], bent[:, a * P:b * P], start=False, stop=True,
                                     skip_group_check=True).then_inc(sem("att_x2_ready"), 1)

                def back(g, part):
                    a, b = PARTS[part]
                    pe.wait_ge(sem("att_scanned"), g * 2 + (part + 1))
                    pe.wait_ge(sem("att_rows_out_filled"), g * 2 + (part + 1))
                    for i in range(a, b):
                        nc.tensor.transpose(bank(6, P, D, (i - a) * 2 * D), run_n[:, i * P:(i + 1) * P], ident[:, :])
                        ins = nc.tensor.transpose(bank(6, P, D, (i - a) * 2 * D + D), run_s[:, i * P:(i + 1) * P], ident[:, :])
                    ins.then_inc(sem("att_sums_turned"), 1)

                def step(g, first, last):
                    branch(g, 1, first)
                    mix(g + 1, 0)
                    bend(g, 1)
                    turn_edges(g + 1, 1)
                    branch(g + 1, 0)
                    back(g, 0)
                    mix(g + 1, 1)
                    bend(g + 1, 0)
                    if not last:
                        turn_edges(g + 2, 0)
                    back(g, 1)

                turn_edges(0, 0, True)
                mix(0, 0, True)
                turn_edges(0, 1)
                branch(0, 0, True)
                mix(0, 1, True)
                bend(0, 0)
                turn_edges(1, 0)
                step(0, True, False)
                with nc.tensor.Fori(1, GR - 2, 1) as g:
                    step(g, False, False)
                step(GR - 2, False, True)
                branch(GR - 1, 1)
                bend(GR - 1, 1)
                for part in range(2):
                    back(GR - 1, part)

            pe.wait_ge(sem("x_landed"), 16)
            pe.wait_ge(sem("lists_copied"), 4)
            pe.wait_ge(sem("block_row_ready"), 1)
            pe.wait_ge(sem("weights_landed"), 16 * WEIGHT_LOADS)
            node_stage(x, D, "x_landed", 0, w1[:, :], D1, LOT)
            gcn_pass(0)
            gcn_pass(1)
            node_stage(tmp, D1, "conv2_input", 0, w2[:, :], D2, LOT)
            pe.wait_ge(sem("table_ready2"), 1)
            gcn_pass(2)
            node_stage(tmp, D2, "conv3_input", 0, w3[:, :], D, LOT)
            node_stage(x, D, "x_new", 0, att_w[:, :, :].rearrange("p c d -> p (c d)"), 4 * D, 1, "products_copied")
            pe.wait_ge(sem("uv_ready"), NL)
            attention_pass()

            def mlp_output(c):
                pe.wait_ge(sem("hidden_made"), (c + 1) * HL)
                at = product_bank()
                for i in range(*LOTS[c]):
                    j = i - LOTS[c][0]
                    for h in range(HL):
                        nc.tensor.matmul(bank(at, P, D, j * D), hidden[h][:, j * P:(j + 1) * P],
                                         mlp2[:, h, :], start=(h == 0), stop=False)
                    nc.tensor.matmul(bank(at, P, D, j * D), ident[0:P, 0:P], tmp[:, i, :], start=False, stop=False)
                    ins = nc.tensor.matmul(bank(at, P, D, j * D), ones[0:1, 0:P], row_of["L1_gnn_mlp_b2"][0:1, :],
                                           start=False, stop=True)
                ins.then_inc(sem("products_ready"), 1)

            for c, lot in enumerate(LOTS):
                pe.wait_ge(sem("mlp_input"), c + 1)
                if c:
                    pe.wait_ge(sem("hidden_made"), c * HL)
                turn(lot, tmp, D)
                if c:
                    mlp_output(c - 1)
                pe.wait_ge(sem("channels_copied"), count["turned"])
                for h in range(HL):
                    nc.tensor.matmul(bank(h, 128, (lot[1] - lot[0]) * P), mlp1[:, h * 128:(h + 1) * 128],
                                     xT[:, lot[0] * P:lot[1] * P], start=True, stop=True).then_inc(sem("hidden_ready"), 1)
            mlp_output(NL - 1)
            pe.wait_ge(sem("x_new"), 2 * NL)
            gcn_pass(4)

            def mix_channels(c):
                a, b = LOTS[c]
                pe.wait_ge(sem("channels_copied"), count["turned"] - (0 if c == NL - 1 else 1))
                nc.tensor.matmul(bank(product_bank("l2_split"), D, (b - a) * P), w_l2[:, :], xT[:, a * P:b * P],
                                 start=True, stop=True).then_inc(sem("products_ready"), 1)
            for c, lot in enumerate(LOTS):
                pe.wait_ge(sem("l2_input"), c + 1)
                turn(lot, tmp, D)
                if c:
                    mix_channels(c - 1)
            mix_channels(NL - 1)
            for c, (a, b) in enumerate(LOTS):
                pe.wait_ge(sem("l2_joined"), NL + c + 1)
                at = product_bank()
                for i in range(a, b):
                    ins = nc.tensor.transpose(bank(at, P, D, (i - a) * D), tmp2[:, i * P:(i + 1) * P], ident[:, :])
                ins.then_inc(sem("products_ready"), 1)
            node_stage(x, D, "x_new", 2 * NL, rel_w[:, :, :].rearrange("p r d -> p (r d)"), NREL * D, 1, "rel_rows_ready")
            pe.wait_ge(sem("rel_rows_ready"), NT)
            gcn_pass(5)

        @block.scalar
        def _(act):
            count = {"turned": 0, "groups": 0, "roots": 0}

            def copy_channels(lot, d):
                n = count["turned"]
                act.wait_ge(sem("channels_turned"), n + 1)
                nc.scalar.activation(xT[0:d, lot[0] * P:lot[1] * P], bank(n % 2, d, (lot[1] - lot[0]) * P), ACT.Copy
                                     ).then_inc(sem("channels_copied"), 1)
                count["turned"] += 1

            def copy_all_channels(d):
                for lot in LOTS:
                    copy_channels(lot, d)

            def gcn_pass(k):
                d = WIDTH[k]
                base = ORDER[k] * GR

                def weigh(g, par, half, part):
                    for i in range(*PARTS[part]):
                        at = par * GRP + i
                        act.wait_ge(sem(f"rows_landed{at}"), (half + (half_base(k, par) + 1)) * 16)
                        nc.scalar.activation(rows[:, at, 0:d], rows[:, at, 0:d], ACT.Copy,
                                             scale=weightT[:, bass.ds(g * GRP + i, 1)]).then_inc(sem("rows_weighted"), 1)

                def empty(g, par, half, part):
                    a, b = PARTS[part]
                    act.wait_ge(sem(f"sums_written{par}"), (half + (half_base(k, par) + 1)) * 16)
                    act.wait_ge(sem("sums_turned"), (g + base) * 2 + (part + 1))
                    nc.scalar.activation(rows_out[:, par * GRP * D + a * d:par * GRP * D + b * d], bank(2 + part, P, (b - a) * d), ACT.Copy
                                         ).then_inc(sem("rows_out_filled"), 1)

                if base == 0:
                    act.sem_inc(sem("sums_written0"), 16)
                    act.sem_inc(sem("sums_written1"), 16)
                    act.sem_inc(sem("rows_out_filled"), FREE)

                def step(g, par, half):
                    for part in range(2):
                        empty(g, par, half, part)
                        weigh(g + 1, 1 - par, half + par, part)
                weigh(0, 0, 0, 0)
                weigh(0, 0, 0, 1)
                in_pairs(nc.scalar, 0, GR - 1, step)
                for part in range(2):
                    empty(GR - 1, (GR - 1) % 2, (GR - 1) // 2, part)

            def attention_pass():
                def copy_edges(g, part, first):
                    a, b = PARTS[part]
                    if not first:
                        act.wait_ge(sem("att_x5_ready"), (g - 1) * 2 + (part + 1))
                    act.wait_ge(sem("e_turned"), g * 2 + (part + 1))
                    nc.scalar.activation(eT[:, a * P:b * P], bank(0, D, (b - a) * P), ACT.Copy).then_inc(sem("att_e_copied"), 1)

                def copy_u(g, part, first):
                    a, b = PARTS[part]
                    if not first:
                        act.wait_ge(sem("att_logits_made"), (g - 1) * 2 + (part + 1))
                    act.wait_ge(sem("att_u_turned"), g * 2 + (part + 1))
                    nc.scalar.activation(uT[:, a * P:b * P], bank(1, D, (b - a) * P), ACT.Copy).then_inc(sem("att_u_copied"), 1)

                def exps(g, part):
                    a, b = PARTS[part]
                    cols = slice(a * P, b * P)
                    c = g * 2 + part
                    act.wait_ge(sem("att_falls_made"), c + 1)
                    nc.scalar.activation(beta[:, cols], fall[:, cols], ACT.Relu)
                    nc.scalar.activation(alpha[:, cols], fall[:, cols], ACT.Relu, scale=-1.0).then_inc(sem("att_clipped"), 1)
                    act.wait_ge(sem("att_clipped"), c + 1)
                    nc.scalar.activation(beta[:, cols], beta[:, cols], ACT.Exp, scale=-1.0).then_inc(sem("att_beta_made"), 1)
                    nc.scalar.activation(alpha[:, cols], alpha[:, cols], ACT.Exp, scale=-1.0).then_inc(sem("att_exps_made"), 1)

                def bend(g, part):
                    a, b = PARTS[part]
                    act.wait_ge(sem("att_x5_ready"), g * 2 + (part + 1))
                    nc.scalar.activation(bent[:, a * P:b * P], bank(4 + part, D, (b - a) * P), ACT.Relu,
                                         scale=1.0 / SLOPE - 1.0).then_inc(sem("att_bent"), 1)

                def empty(g, part, first=False):
                    a, b = PARTS[part]
                    if not first:
                        act.wait_ge(sem(f"att_sums_written{part}"), g * 16)
                    act.wait_ge(sem("att_sums_turned"), g * 2 + (part + 1))
                    nc.scalar.activation(rows_out[:, a * 2 * D:b * 2 * D], bank(6, P, (b - a) * 2 * D), ACT.Copy
                                         ).then_inc(sem("att_rows_out_filled"), 1)

                act.sem_inc(sem("att_rows_out_filled"), 1)
                copy_edges(0, 0, True)
                copy_u(0, 0, True)
                copy_edges(0, 1, True)
                bend(0, 0)
                copy_u(0, 1, True)
                exps(0, 0)
                copy_edges(1, 0, False)

                def step(g, first, last):
                    bend(g, 1)
                    copy_u(g + 1, 0, False)
                    exps(g, 1)
                    copy_edges(g + 1, 1, False)
                    bend(g + 1, 0)
                    empty(g, 0, first)
                    copy_u(g + 1, 1, False)
                    exps(g + 1, 0)
                    if not last:
                        copy_edges(g + 2, 0, False)
                    empty(g, 1, first)
                step(0, True, False)
                with nc.scalar.Fori(1, GR - 2, 1) as g:
                    step(g, False, False)
                step(GR - 2, False, True)
                bend(GR - 1, 1)
                exps(GR - 1, 1)
                empty(GR - 1, 0)
                empty(GR - 1, 1)

            def root(lot):
                count["roots"] += 1
                act.wait_ge(sem("norm_variance"), count["roots"])
                nc.scalar.activation(small[0:P, 3, lot[0]:lot[1]], small[0:P, 2, lot[0]:lot[1]], ACT.Sqrt
                                     ).then_inc(sem("norm_roots"), 1)

            def norm_turn_take(take):
                for c in range(NL + 2):
                    if c < NL:
                        root(LOTS[c])
                    if 1 <= c <= NL:
                        copy_channels(LOTS[c - 1], D)
                    if c >= 2:
                        for i in range(*LOTS[c - 2]):
                            n = count["groups"]
                            act.wait_ge(sem("products_ready"), n + 1)
                            take(i, 2 + n % 6)
                            count["groups"] += 1

            copy_all_channels(D)
            count["groups"] += NL
            act.wait_ge(sem("deg_clamped"), 1)
            nc.scalar.activation(small[0:P, 3, :], small[0:P, 2, :], ACT.Sqrt).then_inc(sem("deg_roots"), 1)
            gcn_pass(0)
            act.wait_ge(sem("elu_input"), 1)
            nc.scalar.activation(tmp2n[:, :, 0:D1], tmp2n[:, :, 0:D1], ACT.Exp).then_inc(sem("elu_exp"), 1)
            gcn_pass(1)
            copy_all_channels(D1)
            count["groups"] += NL
            act.wait_ge(sem("elu_input"), 2)
            nc.scalar.activation(tmp2n[:, :, 0:D2], tmp2n[:, :, 0:D2], ACT.Exp).then_inc(sem("elu_exp"), 1)
            gcn_pass(2)
            copy_all_channels(D2)
            count["groups"] += NL

            def take_uv(i, b):
                nc.scalar.activation(tmp[:, i, :], bank(b, P, D), ACT.Copy, scale=float(HEAD) ** -0.5)
                nc.scalar.activation(tmp2n[:, i, :], bank(b, P, D, D), ACT.Copy)
                nc.scalar.activation(k_node[:, i, :], bank(b, P, D, 2 * D), ACT.Copy)
                nc.scalar.activation(x6[:, i, :], bank(b, P, D, 3 * D), ACT.Copy).then_inc(sem("products_copied"), 1)
            norm_turn_take(take_uv)
            attention_pass()
            hid = 0
            later = [LOTS[i] for c in range(NL + 1) for i in (c, c - 1) if 0 <= i < NL]
            root(LOTS[0])
            for c, lot in enumerate(LOTS):
                if c + 1 < NL:
                    root(LOTS[c + 1])
                else:
                    root(later[0])
                copy_channels(lot, D)
                if c + 1 == NL:
                    root(later[1])
                    root(later[2])
                count["groups"] += 1
                if lot[0]:
                    act.wait_ge(sem("products_ready"), count["groups"] - 1)
                m = (lot[1] - lot[0]) * P
                for h in range(HL):
                    hid += 1
                    act.wait_ge(sem("hidden_ready"), hid)
                    nc.scalar.activation(hidden[h][:, 0:m], bank(h, 128, m), ACT.Relu,
                                         bias=mlp_b1[:, h:h + 1]).then_inc(sem("hidden_made"), 1)
            for lot in later[3:]:
                root(lot)
            gcn_pass(4)

            def split(c, nth, src_ap, scale, shift, neg_scale, neg_shift):
                m = (LOTS[c][1] - LOTS[c][0]) * P
                if nth * NL + c >= 2:
                    act.wait_ge(sem("l2_joined"), nth * NL + c - 1)
                nc.scalar.activation(above[c % 2][:, 0:m], src_ap, ACT.Relu, scale=scale, bias=shift)
                nc.scalar.activation(below[c % 2][:, 0:m], src_ap, ACT.Relu, scale=neg_scale, bias=neg_shift
                                     ).then_inc(sem("l2_split"), 1)

            for c in range(NL + 1):
                if c < NL:
                    copy_channels(LOTS[c], D)
                if c >= 1:
                    a, b = LOTS[c - 1]
                    n = count["groups"]
                    act.wait_ge(sem("products_ready"), n + 1)
                    split(c - 1, 0, bank(2 + n % 6, D, (b - a) * P), 1.0, l2_cols[:, 0:1], -1.0, l2_neg[:, 0:1])
                    count["groups"] += 1
            act.wait_ge(sem("l2_variance"), 1)
            nc.scalar.activation(small[:, 5, 0:1], small[:, 4, 0:1], ACT.Sqrt).then_inc(sem("l2_root"), 1)
            act.wait_ge(sem("l2_fitted"), 1)
            for c, (a, b) in enumerate(LOTS):
                split(c, 1, tmp2[:, a * P:b * P], *(l2_fit[:, q:q + 1] for q in range(4)))
            count["groups"] += NL

            def take_rel(i, b):
                nc.scalar.activation(rel_rows[:, i, :], bank(b, P, NREL * D), ACT.Copy).then_inc(sem("rel_rows_ready"), 1)
            norm_turn_take(take_rel)
            gcn_pass(5)
            for lot in LOTS:
                root(lot)

        @block.vector
        def _(dve):
            V = nc.vector
            count = {"steps": 0, "groups": 0, "taken": 0, "opened": 0, "closed": 0, "passes": 0, "half0": 0, "half1": 0}

            def done(ins):
                count["steps"] += 1
                ins.then_inc(sem("vector_steps"), 1)
                dve.wait_ge(sem("vector_steps"), count["steps"])
                return ins

            own_f = own[:, :, :].rearrange("p i d -> p (i d)")
            own_i = own_f.bitcast(I32)

            dve.wait_ge(sem("edge_lists_landed"), 64)
            lists_i = tmp2[0:LB, :].bitcast(I32)
            for n in range(2):
                V.tensor_copy(list_f(n)[0:LB, :], lists_i[:, n * GE:(n + 1) * GE]).then_inc(sem("lists_float"), 1)
            dve.wait_ge(sem("lists_float"), 1)
            V.scalar_tensor_tensor(list_f(2)[0:LB, :], lists_i[:, 2 * GE:3 * GE], float(N), list_f(0)[0:LB, :],
                                   ALU.mult, ALU.add).then_inc(sem("lists_float"), 1)
            V.tensor_copy(list_f(3)[0:LB, :], tmp2[0:LB, 3 * GE:4 * GE]).then_inc(sem("lists_float"), 1)
            dve.wait_ge(sem("blocks_landed"), 96)
            dve.wait_ge(sem("node_numbers"), 1)
            done(V.tensor_copy(node_id[:, :], block_row[:, :]))
            keep_f = own_f[:, 4 * BL:5 * BL]
            V.tensor_tensor(keep_f[:, 1:BL], own_i[:, 1:BL], own_i[:, 0:BL - 1], ALU.is_equal)
            V.tensor_tensor(keep_f[:, 0:1], own_i[:, 0:1], own_i[:, BL:BL + 1], ALU.is_equal)
            done(V.memset(small[:, 7, :], 0.0))
            done(V.tensor_copy(keep_f[0:1, 0:1], small[0:1, 7, 0:1]))
            done(V.tensor_copy(keep_blocks, keep_f))
            done(V.tensor_scalar(reset_blocks, keep_f, -NEG, NEG, ALU.mult, ALU.add))
            dve.sem_inc(sem("keep_ready"), 1)
            rr = own_i[0:1, 3 * BL:3 * BL + 3 * P].rearrange("a (c p) -> a c p", c=3)
            done(V.tensor_copy(first_row, rr[:, 0, :]))
            dve.sem_inc(sem("block_rows_float"), 1)
            sumw = run_w
            done(V.memset(own_f[:, 5 * BL:5 * BL + 1], 0.0))
            done(V.tensor_tensor_scan(sumw, keep_f, own_f[:, 2 * BL:3 * BL], 0.0, ALU.mult, ALU.add))
            dve.sem_inc(sem("block_sums_ready"), 1)
            for n, target in enumerate((srcT, dstT, relT, weightT)):
                dve.wait_ge(sem("lists_turned"), n + 1)
                if n in (0, 2):
                    V.tensor_copy(target[:, ET:ET + 2 * GRP], bank(n, P, 2 * GRP))
                V.tensor_copy(target[:, 0:ET], bank(n, P, ET)).then_inc(sem("lists_copied"), 1)
            dve.wait_ge(sem("block_first_spread"), 1)
            bc_first = bank(4, P, P)
            done(V.tensor_tensor(is_below, bc_first[:, None, :].to_broadcast([P, NT, P]),
                                 node_id[:, :, None].to_broadcast([P, NT, P]), ALU.is_le))
            done(V.tensor_reduce(small[0:P, 4, :], is_below, AX.X, ALU.add))
            done(V.tensor_scalar(small[0:P, 4, :], small[0:P, 4, :], -1.0, 0.0, ALU.add, ALU.max))
            done(V.tensor_copy(block_row[:, :], small[0:P, 4, :]))
            dve.sem_inc(sem("block_row_ready"), 1)
            row = x6[0:1, 1:NT, :].rearrange("a i d -> a (i d)")
            firsts, lasts, link, whole, aa, bb, cc = (row[:, c * 128:c * 128 + P] for c in range(7))
            dve.wait_ge(sem("block_ends_landed"), 16)
            done(V.tensor_copy(firsts, rr[:, 0, :]))
            done(V.tensor_copy(lasts, rr[:, 1, :]))
            done(V.memset(row[:, 2 * 128:7 * 128], 0.0))
            done(V.tensor_tensor(link[:, 1:P], firsts[:, 1:P], lasts[:, 0:P - 1], ALU.is_equal))
            done(V.tensor_tensor(whole, firsts, lasts, ALU.is_equal))
            done(V.tensor_tensor(aa[:, 1:P], link[:, 1:P], whole[:, 0:P - 1], ALU.mult))
            done(V.tensor_tensor(bb[:, 1:P], link[:, 1:P], own_f[0:1, 3 * BL + 2 * P:3 * BL + 3 * P - 1], ALU.mult))
            done(V.tensor_tensor_scan(carry_row, aa, bb, 0.0, ALU.mult, ALU.add))
            dve.sem_inc(sem("carry_row_ready"), 1)
            dve.wait_ge(sem("carry_landed"), 16)
            done(V.tensor_copy(small[0:P, 5, 0:1], own_i[:, 0:1]))
            prefix = own_f[:, 2 * BL:3 * BL]
            done(V.tensor_scalar(prefix, own_i[:, 0:BL], small[0:P, 5, 0:1], small[0:P, 1, 0:1], ALU.is_equal, ALU.mult))
            done(V.tensor_tensor(sumw, sumw, prefix, ALU.add))
            dve.sem_inc(sem("degree_ready"), 1)
            arena_i = arena[:, :].bitcast(I32)
            junk = tmp2[0:P, 0:BL]
            for c in range(NT // NCH):
                dve.wait_ge(sem(f"block_landed{c}"), 16 * NCH)
                lot = slice(c * NCH, (c + 1) * NCH)
                for i in range(c * NCH, (c + 1) * NCH):
                    done(V.tensor_scalar(junk, arena_i[:, i * BL:(i + 1) * BL], node_id[:, i:i + 1], 0.0, ALU.is_le, ALU.add,
                                         accum_out=small[0:P, 5, i:i + 1]))
                    done(V.tensor_scalar(junk, arena_i[:, i * BL:(i + 1) * BL], node_id[:, i:i + 1], 0.0, ALU.is_equal, ALU.add,
                                         accum_out=small[0:P, 6, i:i + 1]))
                done(V.scalar_tensor_tensor(small[0:P, 7, lot], small[0:P, 4, lot], float(BL), small[0:P, 5, lot], ALU.mult, ALU.add))
                done(V.tensor_scalar(small[0:P, 5, lot], small[0:P, 7, lot], -1.0, 0.0, ALU.add, ALU.max))
                V.tensor_copy(last_edge[:, lot], small[0:P, 5, lot]).then_inc(sem("last_edge_ready"), 1)
            done(V.tensor_scalar(occupied[:, :], small[0:P, 6, :], 1.0, None, ALU.min))
            dve.wait_ge(sem("deg_landed"), 16 * NT)
            done(V.tensor_tensor(small[0:P, 0, :], small[0:P, 0, :], occupied[:, :], ALU.mult))
            done(V.tensor_scalar(small[0:P, 0, :], small[0:P, 0, :], 1.0, None, ALU.add))
            done(V.tensor_scalar(small[0:P, 2, :], small[0:P, 0, :], 1e-30, None, ALU.max))
            dve.sem_inc(sem("deg_clamped"), 1)
            dve.wait_ge(sem("deg_roots"), 1)
            done(V.reciprocal(small[0:P, 3, :], small[0:P, 3, :]))
            done(V.tensor_scalar(small[0:P, 0, :], small[0:P, 0, :], 0.0, None, ALU.is_gt))
            done(V.tensor_tensor(dinv[:, :], small[0:P, 0, :], small[0:P, 3, :], ALU.mult))

            def each(v, w):
                return v[:, :, None].to_broadcast([P, v.shape[1], w])

            def chan(r, n, w):
                return r[:, None, :].to_broadcast([P, n, w])

            def on_halves(lot, op):
                a, b = lot
                mid = a + (b - a + 1) // 2
                for h, (c, d) in enumerate(((a, mid), (mid, b))):
                    if d > c:
                        if count[f"half{h}"]:
                            dve.wait_ge(sem(f"half_done{h}"), count[f"half{h}"])
                        count[f"half{h}"] += 1
                        op(slice(c, d)).then_inc(sem(f"half_done{h}"), 1)

            def signal(name):
                for h in range(2):
                    dve.wait_ge(sem(f"half_done{h}"), count[f"half{h}"])
                dve.sem_inc(sem(name), 1)

            def product_of(lot, width, take):
                a, b = lot
                n = count["groups"]
                dve.wait_ge(sem("products_ready"), n + 1)
                for h in range(2):
                    if count[f"half{h}"]:
                        dve.wait_ge(sem(f"half_done{h}"), count[f"half{h}"])
                ps = bank(2 + n % 6, P, (b - a) * width).rearrange("p (i d) -> p i d", d=width)
                take(a, b - a, ps).then_inc(sem("products_taken"), 1)
                count["groups"] += 1
                count["taken"] += 1
                dve.wait_ge(sem("products_taken"), count["taken"])

            def products(width, take):
                for lot in LOTS:
                    product_of(lot, width, take)

            def gcn_pass(k):
                d = WIDTH[k]
                base = ORDER[k] * GR
                kbase = k * GR

                def stage(g, par, b):
                    at = par * GRP + b
                    V.tensor_copy(idx[:, at:at + 1], GCN[k][2][:, bass.ds(g * GRP + b, 1)]).then_inc(sem("idx_staged"), 1)

                def scan(g, par, half, part):
                    a, b = PARTS[part]
                    for i in range(a, b):
                        dve.wait_ge(sem(f"rows_landed{par * GRP + i}"), (half + (half_base(k, par) + 1)) * 16)
                        stage(g + 2, par, i)
                    dve.wait_ge(sem(f"keep_landed{part}"), (g + (kbase + 1)) * 16)
                    dve.wait_ge(sem("rows_turned"), (g + base) * GRP + b)
                    before = run_s[0:d, a * P - 1:a * P] if part else run_s[0:d, GE - 1:GE]
                    V.tensor_tensor_scan(run_s[0:d, a * P:b * P], keep[0:d, a * P:b * P], bank(part, d, (b - a) * P),
                                         before, ALU.mult, ALU.add).then_inc(sem("scanned"), 1)

                def step(g, par, half):
                    for part in range(2):
                        dve.wait_ge(sem("scanned"), (g + base) * 2 + part)
                        dve.wait_ge(sem("sums_turned"), (g + (base - 1)) * 2 + (part + 1))
                        scan(g, par, half, part)

                for g in range(2):
                    for b in range(GRP):
                        stage(g, g, b)
                scan(0, 0, 0, 0)
                dve.wait_ge(sem("scanned"), base * 2 + 1)
                scan(0, 0, 0, 1)
                in_pairs(V, 1, GR, step)

            def as_ends_land(take, signals=None):
                count["passes"] += 1
                for c, lot in enumerate(LOTS):
                    ends_here(c)
                    take(lot)
                    if signals:
                        signal(signals)

            def ends_here(c):
                dve.wait_ge(sem(f"ends_landed{c}"), 16 * (LOTS[c][1] - LOTS[c][0]) * count["passes"])

            def elu(dst_ap, src_ap, w, n):
                done(V.tensor_scalar(tmp2n[:, :, 0:w], src_ap, 0.0, None, ALU.min))
                dve.sem_inc(sem("elu_input"), 1)
                dve.wait_ge(sem("elu_exp"), n)
                done(V.tensor_scalar(src_ap, src_ap, 0.0, -1.0, ALU.max, ALU.add))
                done(V.tensor_tensor(dst_ap, src_ap, tmp2n[:, :, 0:w], ALU.add))

            stats_f = stats[:, :, :].rearrange("p i s -> p (i s)")
            mv_f = mean_var[:, :, :].rearrange("p i s -> p (i s)")

            def tile_of(v):
                return lambda i: v[:, i, :]

            def bend_down(h, v):
                return V.scalar_tensor_tensor(v[:, h, :], v[:, h, :], SLOPE, v[:, h, :], ALU.mult, ALU.max)

            def norm_open(lot, src):
                def statistics(half):
                    for i in range(half.start, half.stop):
                        ins = V.bn_stats(stats_f[:, i * 6:i * 6 + 6], src(i))
                    return ins

                def aggregate(half):
                    for i in range(half.start, half.stop):
                        ins = V.bn_aggr(mv_f[:, i * 2:i * 2 + 2], stats_f[:, i * 6:i * 6 + 6])
                    return ins
                on_halves(lot, statistics)
                on_halves(lot, aggregate)
                on_halves(lot, lambda h: V.tensor_scalar(small[0:P, 2, h], mean_var[:, h, 1], EPS, None, ALU.add))
                signal("norm_variance")

            def norm_close(lot, dst_ap, src_ap):
                dst_f, src_f = (v.rearrange("p i d -> p (i d)") for v in (dst_ap, src_ap))
                count["closed"] += 1
                dve.wait_ge(sem("norm_roots"), count["closed"])

                def normalise(half):
                    for i in range(half.start, half.stop):
                        ins = V.tensor_scalar(dst_f[:, i * D:(i + 1) * D], src_f[:, i * D:(i + 1) * D], mv_f[:, i * 2:i * 2 + 1],
                                              small[0:P, 3, i:i + 1], ALU.subtract, ALU.mult)
                    return ins
                on_halves(lot, lambda h: V.reciprocal(small[0:P, 3, h], small[0:P, 3, h]))
                on_halves(lot, normalise)

            def find_first_edges():
                first = small[0:P, 6, :]
                dve.wait_ge(sem("before_landed"), 16)
                done(V.tensor_scalar(small[0:P, 5, :], node_id[:, :], float(E), None, ALU.add))
                done(V.tensor_tensor(first, first, small[0:P, 5, :], ALU.subtract))
                done(V.tensor_tensor(first, first, occupied[:, :], ALU.mult))
                done(V.tensor_tensor(first_edge[:, :], first, small[0:P, 5, :], ALU.add))
                dve.sem_inc(sem("first_edge_ready"), 1)

            dve.wait_ge(sem("weights_landed"), 16 * WEIGHT_LOADS)
            done(V.tensor_scalar(l2_neg[:, :], l2_cols[:, :], -1.0, None, ALU.mult))
            dve.wait_ge(sem("deg_stored"), 16)
            products(D1, lambda a, m, ps: V.tensor_tensor(
                own[:, a:a + m, 0:D1], ps, dinv[:, a:a + m, None].to_broadcast([P, m, D1]), ALU.mult))
            dve.sem_inc(sem("table_ready0"), 1)
            for k, w in ((0, D1), (1, D1), (2, D2)):
                gcn_pass(k)
                if k == 1:
                    find_first_edges()

                def sum_up(lot):
                    on_halves(lot, lambda h: V.tensor_tensor(tmp[:, h, 0:w], ends(w)[:, h, :], each(occupied[:, h], w), ALU.mult))
                    on_halves(lot, lambda h: V.tensor_tensor(tmp[:, h, 0:w], tmp[:, h, 0:w], own[:, h, 0:w], ALU.add))
                    on_halves(lot, lambda h: V.tensor_tensor(tmp[:, h, 0:w], tmp[:, h, 0:w], each(dinv[:, h], w), ALU.mult))
                if k == 2:
                    done(V.tensor_tensor(x[:, :, :], x[:, :, :], chan(row_of["L0_gnn_b3"], NT, D), ALU.add))
                as_ends_land(sum_up, ("conv1_summed", "conv2_input", "conv3_input")[k])
                if k == 0:
                    done(V.tensor_tensor(tmp[:, :, 0:w], tmp[:, :, 0:w], chan(row_of["L0_gnn_b1"], NT, w), ALU.add))
                    elu(tmp[:, :, 0:w], tmp[:, :, 0:w], w, 1)
                    done(V.tensor_tensor(own[:, :, 0:w], tmp[:, :, 0:w], each(dinv, w), ALU.mult))
                    dve.sem_inc(sem("table_ready1"), 1)
                elif k == 1:
                    b2 = row_of["L0_gnn_b2"]
                    products(D2, lambda a, m, ps: V.tensor_tensor(
                        own[:, a:a + m, 0:D2], ps, chan(b2, m, D2), ALU.add))
                    elu(own[:, :, 0:D2], own[:, :, 0:D2], D2, 2)
                    done(V.tensor_tensor(own[:, :, 0:D2], own[:, :, 0:D2], each(dinv, D2), ALU.mult))
                    dve.sem_inc(sem("table_ready2"), 1)
                else:
                    products(D, lambda a, m, ps: V.tensor_tensor(x[:, a:a + m, :], ps, x[:, a:a + m, :], ALU.add))
                    for c in range(NL + 4):
                        if c < NL:
                            norm_open(LOTS[c], tile_of(x))
                        if 1 <= c <= NL:
                            norm_close(LOTS[c - 1], x[:, :, :], x[:, :, :])
                            signal("x_new")
                        if c >= 4:
                            lot = LOTS[c - 4]
                            dve.wait_ge(sem("products_copied"), lot[1])
                            for v in (tmp2n, tmp, k_node):
                                on_halves(lot, lambda h: bend_down(h, v))
                            signal("uv_ready")
                    count["groups"] += NT

            def attention_pass():
                def logits(g, part):
                    a, b = PARTS[part]
                    c = g * 2 + part
                    dve.wait_ge(sem("att_edges_mixed"), c + 1)
                    dve.wait_ge(sem("att_u_copied"), c + 1)
                    V.tensor_tensor(logit[:, a * P:b * P], bank(2 + part, D, (b - a) * P), uT[:, a * P:b * P], ALU.mult
                                    ).then_inc(sem("att_logits_made"), 1)

                def carry_maximum(g):
                    V.tensor_copy(run_m[:, 0:1], run_m[:, GE:GE + 1]).then_inc(sem("att_max_carried"), 1)

                def maxima(g, part):
                    a, b = PARTS[part]
                    c = g * 2 + part
                    dve.wait_ge(sem(f"keep_landed{part}"), (g + (3 * GR + 1)) * 16)
                    dve.wait_ge(sem("att_logits_made"), c + 1)
                    V.tensor_tensor_scan(run_m[:, 1 + a * P:1 + b * P], logit[:, a * P:b * P], keep[:, a * P:b * P],
                                         run_m[:, a * P:a * P + 1], ALU.max, ALU.add).then_inc(sem("att_max_scanned"), 1)

                def falls(g, part, first):
                    a, b = PARTS[part]
                    c = g * 2 + part
                    dve.wait_ge(sem("att_max_scanned"), c + 1)
                    if not first:
                        dve.wait_ge(sem("att_clipped"), c - 1)
                    V.tensor_tensor(fall[:, a * P:b * P], run_m[:, a * P:b * P], logit[:, a * P:b * P], ALU.subtract
                                    ).then_inc(sem("att_falls_made"), 1)

                def branches(g, part):
                    a, b = PARTS[part]
                    c = g * 2 + part
                    dve.wait_ge(sem("att_beta_made"), c + 1)
                    dve.wait_ge(sem("att_x2_ready"), c + 1)
                    V.tensor_tensor(betax[:, a * P:b * P], beta[:, a * P:b * P], bank(4 + part, D, (b - a) * P), ALU.mult
                                    ).then_inc(sem("att_betax_made"), 1)

                def sums(g, part, first):
                    a, b = PARTS[part]
                    cols = slice(a * P, b * P)
                    if not first:
                        dve.wait_ge(sem("att_sums_turned"), (g - 1) * 2 + (part + 1))
                    at = a * P - 1 if part else GE - 1
                    dve.wait_ge(sem("att_exps_made"), g * 2 + (part + 1))
                    if not (first and part == 0):
                        dve.wait_ge(sem("att_scanned"), g * 2 + part)
                    V.tensor_tensor_scan(run_s[:, cols], alpha[:, cols], beta[:, cols], run_s[:, at:at + 1],
                                         ALU.mult, ALU.add)
                    dve.wait_ge(sem("att_betax_made"), g * 2 + (part + 1))
                    V.tensor_tensor_scan(run_n[:, cols], alpha[:, cols], betax[:, cols], run_n[:, at:at + 1],
                                         ALU.mult, ALU.add).then_inc(sem("att_scanned"), 1)

                def compare_tile(g, i):
                    return V.tensor_scalar(same[:, i * P:(i + 1) * P], dst_row[:, i * P:(i + 1) * P],
                                           dstT[:, bass.ds(g * GRP + i, 1)], None, ALU.is_equal)

                def compare_first(g, part):
                    dve.wait_ge(sem(f"dst_row_landed{part}"), (g + 1) * 16)
                    compare_tile(g, PARTS[part][0])

                def compare_rest(g, part):
                    for i in range(PARTS[part][0] + 1, PARTS[part][1]):
                        ins = compare_tile(g, i)
                    ins.then_inc(sem("att_same_made"), 1)

                def compare(g, part):
                    compare_first(g, part)
                    compare_rest(g, part)

                def open_part(g, part, first):
                    logits(g, part)
                    maxima(g, part)
                    falls(g, part, first)

                def close_part(g, part, first):
                    branches(g, part)
                    sums(g, part, first)

                def both_parts(new, old, compared, first):
                    (g, p), (h, q) = new, old
                    logits(g, p)
                    if p == 0:
                        carry_maximum(g)
                    branches(h, q)
                    if p == 0:
                        dve.wait_ge(sem("att_max_carried"), g)
                    maxima(g, p)
                    if compared:
                        compare_first(*compared)
                    falls(g, p, False)
                    if compared:
                        compare_rest(*compared)
                    sums(h, q, first)

                compare(0, 0)
                compare(0, 1)
                open_part(0, 0, True)
                compare(1, 0)
                open_part(0, 1, True)
                close_part(0, 0, True)
                both_parts((1, 0), (0, 1), (1, 1), True)
                compare(2, 0)
                with V.Fori(1, GR - 2, 1) as g:
                    both_parts((g, 1), (g, 0), (g + 1, 1), False)
                    both_parts((g + 1, 0), (g, 1), (g + 2, 0), False)
                both_parts((GR - 2, 1), (GR - 2, 0), (GR - 1, 1), False)
                both_parts((GR - 1, 0), (GR - 2, 1), None, False)
                open_part(GR - 1, 1, False)
                close_part(GR - 1, 0, False)
                close_part(GR - 1, 1, False)

            dve.wait_ge(sem("uv_stored"), 32 * NL)
            attention_pass()
            both = ends(2 * D)

            def aggregate(lot):
                num, den = both[:, :, 0:D], both[:, :, D:2 * D]
                on_halves(lot, lambda h: V.tensor_tensor(tmp[:, h, :], k_node[:, h, :], den[:, h, :], ALU.mult))
                on_halves(lot, lambda h: V.tensor_scalar(den[:, h, :], den[:, h, :], 1e-20, None, ALU.add))
                on_halves(lot, lambda h: V.reciprocal(den[:, h, :], den[:, h, :]))
                on_halves(lot, lambda h: V.scalar_tensor_tensor(tmp[:, h, :], num[:, h, :], SLOPE, tmp[:, h, :], ALU.mult, ALU.add))
                on_halves(lot, lambda h: V.tensor_tensor(tmp[:, h, :], tmp[:, h, :], den[:, h, :], ALU.mult))
                add_occupied(lot, x6, tmp, None)

            def add_occupied(lot, to, v, clip):
                def step(half):
                    for i in range(half.start, half.stop):
                        ins = V.scalar_tensor_tensor(to[:, i, :], v[:, i, :], occupied[:, i:i + 1], to[:, i, :], ALU.mult, ALU.add)
                    return ins
                if clip:
                    on_halves(lot, lambda h: V.tensor_scalar(v[:, h, :], v[:, h, :], 0.0, None, ALU.max))
                on_halves(lot, step)

            def norm_close_affine(lot, dst, src, added, bank_used=False):
                count["closed"] += 1
                dve.wait_ge(sem("norm_roots"), count["closed"])

                def centre(half):
                    for i in range(half.start, half.stop):
                        ins = V.scalar_tensor_tensor(x6[:, i, :], src(i), mean_var[:, i, 0:1], row_of["L1_gnn_gamma"][:, :],
                                                     ALU.subtract, ALU.mult)
                    return ins

                def scale(half):
                    for i in range(half.start, half.stop):
                        ins = V.scalar_tensor_tensor(dst[:, i, :], x6[:, i, :], small[0:P, 3, i:i + 1], added(i), ALU.mult, ALU.add)
                    return ins
                on_halves(lot, centre)
                on_halves(lot, lambda h: V.reciprocal(small[0:P, 3, h], small[0:P, 3, h]))
                if bank_used:
                    signal("products_taken")
                    count["taken"] += 1
                on_halves(lot, scale)

            def mlp_input(lot):
                norm_close_affine(lot, tmp, tile_of(x6), lambda i: row_of["L1_gnn_beta"][:, :])
                signal("mlp_input")

            done(V.tensor_tensor(x[:, :, :], x[:, :, :], chan(row_of["L1_gnn_beta"], NT, D), ALU.add))
            count["passes"] += 1
            for c in range(NL + 1):
                if c < NL:
                    ends_here(c)
                    aggregate(LOTS[c])
                if c >= 1:
                    mlp_input(LOTS[c - 1])
                if c < NL:
                    norm_open(LOTS[c], tile_of(x6))
            first_group = count["groups"]

            def mixed(c):
                return lambda i: bank(2 + (first_group + c) % 6, P, D, (i - LOTS[c][0]) * D)
            for c in range(NL + 2):
                if c < NL:
                    dve.wait_ge(sem("products_ready"), first_group + c + 1)
                    norm_open(LOTS[c], mixed(c))
                if 1 <= c <= NL:
                    lot = LOTS[c - 1]
                    norm_close_affine(lot, x, mixed(c - 1), tile_of(x), True)
                    norm_open(lot, tile_of(x))
                if c >= 2:
                    norm_close(LOTS[c - 2], x[:, :, :], x[:, :, :])
                    signal("x_new")
            count["groups"] += NL
            gcn_pass(4)
            h_all = tmp2[:, 0:N]
            col = lambda c: l2_cols[:, c:c + 1]

            def join(c, nth, slope):
                a, b = LOTS[c]
                dve.wait_ge(sem("l2_split"), nth * NL + c + 1)
                V.scalar_tensor_tensor(h_all[:, a * P:b * P], below[c % 2][:, 0:(b - a) * P], l2_neg[:, slope:slope + 1],
                                       above[c % 2][:, 0:(b - a) * P], ALU.mult, ALU.add).then_inc(sem("l2_joined"), 1)
            batch = logit
            count["passes"] += 1
            for c in range(NL + 3):
                if c < NL:
                    ends_here(c)
                    on_halves(LOTS[c], lambda h: V.tensor_tensor(
                        tmp[:, h, :], ends(D)[:, h, :], each(occupied[:, h], D), ALU.mult))
                    signal("l2_input")
                if 2 <= c < NL + 2:
                    join(c - 2, 0, 3)
                if c >= 3:
                    a, b = LOTS[c - 3]
                    dve.wait_ge(sem("l2_joined"), c - 2)
                    ins = V.bn_stats(batch[:, (c - 3) * 6:(c - 2) * 6], h_all[:, a * P:b * P])
            done(ins)
            count["groups"] += NL
            s = small[:, 4, :]
            mean = batch[:, NL * 6:NL * 6 + 1]
            done(V.bn_aggr(batch[:, NL * 6:NL * 6 + 2], batch[:, 0:NL * 6]))
            done(V.tensor_scalar(s[:, 0:1], batch[:, NL * 6 + 1:NL * 6 + 2], EPS, None, ALU.add))
            dve.sem_inc(sem("l2_variance"), 1)
            dve.wait_ge(sem("l2_root"), 1)
            done(V.reciprocal(s[:, 2:3], small[:, 5, 0:1]))
            done(V.tensor_tensor(l2_fit[:, 0:1], s[:, 2:3], col(1), ALU.mult))
            done(V.tensor_tensor(l2_fit[:, 3:4], l2_fit[:, 0:1], mean, ALU.mult))
            done(V.tensor_tensor(l2_fit[:, 3:4], l2_fit[:, 3:4], col(2), ALU.subtract))
            V.tensor_scalar(l2_fit[:, 2:3], l2_fit[:, 0:1], -1.0, None, ALU.mult)
            done(V.tensor_scalar(l2_fit[:, 1:2], l2_fit[:, 3:4], -1.0, None, ALU.mult))
            dve.sem_inc(sem("l2_fitted"), 1)
            for c in range(NL):
                join(c, 1, 4)
            products(D, lambda a, m, ps: V.tensor_tensor(x[:, a:a + m, :], ps, x[:, a:a + m, :], ALU.add))
            for c in range(NL + 1):
                if c < NL:
                    norm_open(LOTS[c], tile_of(x))
                if c >= 1:
                    norm_close(LOTS[c - 1], x[:, :, :], x[:, :, :])
                    signal("x_new")
            gcn_pass(5)
            count["passes"] += 1
            for c in range(NL + 1):
                if c < NL:
                    ends_here(c)
                    add_occupied(LOTS[c], x, ends(D), True)
                    norm_open(LOTS[c], tile_of(x))
                if c >= 1:
                    norm_close(LOTS[c - 1], x[:, :, :], x[:, :, :])
                    signal("out_ready")


_INS = ['x', 'src', 'dst', 'edge_attr_128', 'edge_type_3', 'edge_weight', 'L0_gnn_W1', 'L0_gnn_b1', 'L0_gnn_W2',
        'L0_gnn_b2', 'L0_gnn_W3', 'L0_gnn_b3', 'L1_gnn_w1', 'L1_gnn_w2', 'L1_gnn_w3', 'L1_gnn_w4', 'L1_gnn_w5',
        'L1_gnn_w6', 'L1_gnn_mlp_w1', 'L1_gnn_mlp_b1', 'L1_gnn_mlp_w2', 'L1_gnn_mlp_b2', 'L1_gnn_gamma',
        'L1_gnn_beta', 'L2_gnn_W', 'L2_gnn_b', 'L2_gnn_a1', 'L2_gnn_gamma', 'L2_gnn_beta', 'L2_gnn_a2',
        'L3_gnn_weight']


def kernel(**inputs):
    import numpy as _np
    import concourse.bacc as _bacc
    from concourse import mybir as _mybir
    from concourse.bass_utils import run_bass_kernel_spmd as _run

    nc = _bacc.Bacc("TRN2", target_bir_lowering=False, num_devices=1)
    arrays, t = {}, {}
    for name in _INS:
        a = _np.ascontiguousarray(inputs[name])
        arrays["in_" + name] = a
        t[name] = nc.dram_tensor("in_" + name, a.shape, _mybir.dt.from_np(a.dtype), kind="ExternalInput").ap()
    out = nc.dram_tensor("out_0", t["x"].shape, _mybir.dt.float32, kind="ExternalOutput").ap()
    build(nc, t, out)
    r = _run(nc, [arrays], core_ids=[0])
    return r.results[0]["out_0"]
```
